# Optimizing a Trainium2 kernel written in Bass

```python
import numpy as np
import jax
import jax.numpy as jnp

def _softmax(x, axis=-1):
    return jax.nn.softmax(x, axis=axis)

def _gelu(x):
    return jax.nn.gelu(x, approximate=True)

def _silu(x):
    return jax.nn.silu(x)

def _sigmoid(x):
    return jax.nn.sigmoid(x)

def _layernorm(x, axis=-1, eps=1e-05):
    m = jnp.mean(x, axis=axis, keepdims=True)
    v = jnp.var(x, axis=axis, keepdims=True)
    return (x - m) / jnp.sqrt(v + eps)

def _scatter_add(tgt, idx, src, axis=0):
    return tgt.at[idx].add(src)

def _segment_sum(src, seg, n):
    return jax.ops.segment_sum(src, seg, n)
kernel_name = 'mk_adaln_d2_jaxref_r8_c6edbf'

def setup_inputs(seed: int=0):
    np.random.seed(seed)
    _w = jnp.asarray

    def _L0_attn_setup():
        import jax, jax.numpy as jnp
        import numpy as np
        D_MODEL, D_STATE, D_CONV, EXPAND = (128, 16, 4, 2)
        D_INNER = EXPAND * D_MODEL
        BATCH, LENGTH = (2, 128)

        def _mamba_fwd(x, in_proj_w, in_proj_b, conv_w, conv_b, x_proj_w, x_proj_b, dt_proj_w, dt_proj_b, D, out_proj_w, out_proj_b):
            batch, length, _ = x.shape
            d_inner = D.shape[0]
            d_state = dt_proj_w.shape[0]
            d_conv = conv_w.shape[-1]
            xz = x @ in_proj_w + in_proj_b
            xc, z = jnp.split(xz, 2, axis=-1)
            xc_bdl = jnp.transpose(xc, (0, 2, 1))
            xc_bdl = jax.lax.conv_general_dilated(xc_bdl, conv_w, window_strides=(1,), padding=[(d_conv - 1, 0)], dimension_numbers=('NCH', 'OIH', 'NCH'), feature_group_count=d_inner)
            xc_bdl = xc_bdl + conv_b[None, :, None]
            xc = jnp.transpose(xc_bdl, (0, 2, 1))
            xc = jax.nn.silu(xc)
            dBu = xc @ x_proj_w + x_proj_b
            delta_s, B, u = jnp.split(dBu, [d_state, 2 * d_state], axis=-1)
            delta = jax.nn.softplus(delta_s @ dt_proj_w + dt_proj_b)
            A = -jnp.arange(1, d_state + 1, dtype=x.dtype)
            deltaA = jnp.exp(delta[..., None] * A)
            deltaB_u = delta[..., None] * B[:, :, None, :] * u[..., None]
            dA_t = jnp.moveaxis(deltaA, 1, 0)
            dBu_t = jnp.moveaxis(deltaB_u, 1, 0)

            def step(h, inp):
                dA, dBu_ = inp
                h = dA * h + dBu_
                return (h, h.sum(-1))
            h0 = jnp.zeros((batch, d_inner, d_state), x.dtype)
            _, y_t = jax.lax.scan(step, h0, (dA_t, dBu_t))
            y = jnp.moveaxis(y_t, 0, 1)
            y = y + u * D
            y = y * jax.nn.silu(z)
            return y @ out_proj_w + out_proj_b
        key = jax.random.key(seed)
        ks = jax.random.split(key, 12)
        s = lambda fan_in: 1.0 / np.sqrt(fan_in)
        return {'x': jax.random.normal(ks[0], (BATCH, LENGTH, D_MODEL), jnp.float32), 'in_proj_w': jax.random.normal(ks[1], (D_MODEL, 2 * D_INNER), jnp.float32) * s(D_MODEL), 'in_proj_b': jax.random.normal(ks[2], (2 * D_INNER,), jnp.float32) * s(D_MODEL), 'conv_w': jax.random.normal(ks[3], (D_INNER, 1, D_CONV), jnp.float32) * s(D_CONV), 'conv_b': jax.random.normal(ks[4], (D_INNER,), jnp.float32) * s(D_CONV), 'x_proj_w': jax.random.normal(ks[5], (D_INNER, 2 * D_STATE + D_INNER), jnp.float32) * s(D_INNER), 'x_proj_b': jax.random.normal(ks[6], (2 * D_STATE + D_INNER,), jnp.float32) * s(D_INNER), 'dt_proj_w': jax.random.normal(ks[7], (D_STATE, D_INNER), jnp.float32) * s(D_STATE), 'dt_proj_b': jax.random.normal(ks[8], (D_INNER,), jnp.float32) * s(D_STATE), 'D': jnp.ones((D_INNER,), jnp.float32), 'out_proj_w': jax.random.normal(ks[9], (D_INNER, D_MODEL), jnp.float32) * s(D_INNER), 'out_proj_b': jax.random.normal(ks[10], (D_MODEL,), jnp.float32) * s(D_INNER)}
    _L0_attn_in = _L0_attn_setup()

    def _L0_ffn_setup():
        import jax, jax.numpy as jnp
        import numpy as np
        MAX_THRESHOLD = 0.125
        key = jax.random.key(seed)
        ks = jax.random.split(key, 5)
        B, S, D, FF, E = (2, 256, 128, 512, 8)
        sd = 1.0 / np.sqrt(D)
        sf = 1.0 / np.sqrt(FF)
        return {'inputs': jax.random.normal(ks[0], (B, S, D), dtype=jnp.float32), 'Wg': jax.random.normal(ks[1], (D, E), dtype=jnp.float32) * sd, 'bg': jnp.zeros((E,), dtype=jnp.float32), 'Wt': jax.random.normal(ks[2], (D, 1), dtype=jnp.float32) * sd, 'bt': jnp.zeros((1,), dtype=jnp.float32), 'W1': jax.random.normal(ks[3], (E, D, FF), dtype=jnp.float32) * sd, 'b1': jnp.zeros((E, FF), dtype=jnp.float32), 'W2': jax.random.normal(ks[4], (E, FF, D), dtype=jnp.float32) * sf, 'b2': jnp.zeros((E, D), dtype=jnp.float32)}
    _L0_ffn_in = _L0_ffn_setup()
    _L0_c = _w((lambda *s: np.random.randn(*s).astype(np.float32) * 0.05)(4, 128))
    _L0_wmod = _w((lambda *s: np.random.randn(*s).astype(np.float32) * 0.05)(128, 6 * 128) * 128 ** (-0.5))

    def _L1_attn_setup():
        import jax, jax.numpy as jnp
        import numpy as np
        EMB = 128
        HEADS = 16
        HEAD_DIM = EMB // HEADS
        BLOCK = 32
        N_GLOBAL = 4
        WINDOW = 128
        ROPE_BASE = 10000.0

        def rotate_half(x):
            x1 = x[..., ::2]
            x2 = x[..., 1::2]
            return jnp.stack((-x2, x1), axis=-1).reshape(x.shape)

        def rope_cos_sin(seq_len, dtype=jnp.float32):
            inv_freq = 1.0 / ROPE_BASE ** (jnp.arange(0, HEAD_DIM, 2, dtype=jnp.float32) / HEAD_DIM)
            pos = jnp.arange(seq_len, dtype=jnp.float32)
            freqs = jnp.outer(pos, inv_freq)
            emb = jnp.concatenate([freqs, freqs], -1)
            return (jnp.cos(emb)[None, None].astype(dtype), jnp.sin(emb)[None, None].astype(dtype))

        def block_mask(seq_len):
            i = jnp.arange(seq_len)[:, None]
            j = jnp.arange(seq_len)[None, :]
            blk = i // BLOCK == j // BLOCK
            glob = (i < N_GLOBAL) | (j < N_GLOBAL)
            slide = jnp.abs(i - j) <= WINDOW
            return (blk | glob | slide) & (j <= i)
        key = jax.random.key(seed)
        kx, kq, ko = jax.random.split(key, 3)
        B, S = (2, 256)
        x = jax.random.normal(kx, (B, S, EMB), jnp.float32)
        qkv_w = jax.random.normal(kq, (3 * EMB, EMB), jnp.float32) * EMB ** (-0.5)
        out_w = jax.random.normal(ko, (EMB, EMB), jnp.float32) * EMB ** (-0.5)
        return {'x': x, 'qkv_w': qkv_w, 'out_w': out_w}
    _L1_attn_in = _L1_attn_setup()

    def _L1_ffn_setup():
        import jax, jax.numpy as jnp
        import numpy as np
        DIM = 128
        DEPTH = 2
        HEADS = 8
        DIM_HEAD = 64
        WINDOW = 64
        INNER = HEADS * DIM_HEAD
        HID = int(DIM * 4 * 2 / 3)
        B, N = (2, 1024)
        QK_SCALE = 8.0

        def shift_token(t):
            t1, t2 = jnp.split(t, 2, axis=-1)
            t2 = jnp.pad(t2, ((0, 0), (1, 0), (0, 0)))[:, :-1]
            return jnp.concatenate([t1, t2], axis=-1)

        def l2norm(t):
            return t / jnp.clip(jnp.linalg.norm(t, axis=-1, keepdims=True), 1e-12)

        def rotate_half(x):
            x1, x2 = jnp.split(x, 2, axis=-1)
            return jnp.concatenate([-x2, x1], axis=-1)

        def rotary_xpos(q, k):
            n = q.shape[-2]
            half_idx = jnp.arange(0, DIM_HEAD, 2, dtype=jnp.float32)
            inv_freq = 1.0 / 10000.0 ** (half_idx / DIM_HEAD)
            t = jnp.arange(n, dtype=jnp.float32)
            freqs = t[:, None] * inv_freq[None, :]
            freqs = jnp.concatenate([freqs, freqs], axis=-1)
            base = (half_idx + 0.4 * DIM_HEAD) / (1.4 * DIM_HEAD)
            power = (t - n // 2) / float(WINDOW // 2)
            scale = base[None, :] ** power[:, None]
            scale = jnp.concatenate([scale, scale], axis=-1)
            cos, sin = (jnp.cos(freqs), jnp.sin(freqs))
            q = q * cos * scale + rotate_half(q) * sin * scale
            k = k * cos / scale + rotate_half(k) * sin / scale
            return (q, k)

        def local_attention(q, k, v):
            b, h, n, d = q.shape
            w = n // WINDOW
            bq = q.reshape(b, h, w, WINDOW, d) * QK_SCALE
            bk = k.reshape(b, h, w, WINDOW, d)
            bv = v.reshape(b, h, w, WINDOW, d)

            def look_around(t):
                p = jnp.pad(t, ((0, 0), (0, 0), (1, 0), (0, 0), (0, 0)))
                return jnp.concatenate([p[:, :, :w], p[:, :, 1:]], axis=3)
            bk, bv = (look_around(bk), look_around(bv))
            bt = jnp.arange(n).reshape(w, WINDOW)
            btp = jnp.pad(bt, ((1, 0), (0, 0)), constant_values=-1)
            btk = jnp.concatenate([btp[:w], btp[1:]], axis=1)
            sim = jnp.einsum('bhwid,bhwjd->bhwij', bq, bk)
            i = bt[:, :, None]
            j = btk[:, None, :]
            mask = (i < j) | (i > j + WINDOW) | (j == -1)
            sim = jnp.where(mask, -jnp.finfo(sim.dtype).max, sim)
            attn = jax.nn.softmax(sim, axis=-1)
            out = jnp.einsum('bhwij,bhwjd->bhwid', attn, bv)
            return out.reshape(b, h, n, d)

        def _layer(x, wqkv, qs, ksc, wo, lg, lb, w1, b1, w2, b2):
            b, n, _ = x.shape
            h = shift_token(x)
            qkv = h @ wqkv
            q, k, v = jnp.split(qkv, 3, axis=-1)
            to_heads = lambda t: t.reshape(b, n, HEADS, DIM_HEAD).transpose(0, 2, 1, 3)
            q, k, v = (to_heads(q), to_heads(k), to_heads(v))
            q = l2norm(q) * qs
            k = l2norm(k) * ksc
            q, k = rotary_xpos(q, k)
            o = local_attention(q, k, v)
            o = o.transpose(0, 2, 1, 3).reshape(b, n, INNER)
            x = x + o @ wo
            h = shift_token(x)
            mu = h.mean(-1, keepdims=True)
            var = h.var(-1, keepdims=True)
            h = (h - mu) / jnp.sqrt(var + 1e-05) * lg + lb
            h = h @ w1 + b1
            a, g = jnp.split(h, 2, axis=-1)
            h = a * jax.nn.gelu(g, approximate=False)
            x = x + h @ w2 + b2
            return x
        key = jax.random.key(seed)
        ks = jax.random.split(key, 6)
        return {'x': jax.random.normal(ks[0], (B, N, DIM), jnp.float32), 'wqkv': jax.random.normal(ks[1], (DEPTH, DIM, 3 * INNER), jnp.float32) * 0.02, 'q_scale': jnp.ones((DEPTH, DIM_HEAD), jnp.float32), 'k_scale': jnp.ones((DEPTH, DIM_HEAD), jnp.float32), 'wo': jax.random.normal(ks[2], (DEPTH, INNER, DIM), jnp.float32) * 0.02, 'ln_g': jnp.ones((DEPTH, DIM), jnp.float32), 'ln_b': jnp.zeros((DEPTH, DIM), jnp.float32), 'w1': jax.random.normal(ks[3], (DEPTH, DIM, 2 * HID), jnp.float32) * 0.02, 'b1': jnp.zeros((DEPTH, 2 * HID), jnp.float32), 'w2': jax.random.normal(ks[4], (DEPTH, HID, DIM), jnp.float32) * 0.02, 'b2': jnp.zeros((DEPTH, DIM), jnp.float32)}
    _L1_ffn_in = _L1_ffn_setup()
    _L1_c = _w((lambda *s: np.random.randn(*s).astype(np.float32) * 0.05)(4, 128))
    _L1_wmod = _w((lambda *s: np.random.randn(*s).astype(np.float32) * 0.05)(128, 6 * 128) * 128 ** (-0.5))
    _d = {'L0_attn_x': _L0_attn_in['x'], 'L0_attn_in_proj_w': _L0_attn_in['in_proj_w'], 'L0_attn_in_proj_b': _L0_attn_in['in_proj_b'], 'L0_attn_conv_w': _L0_attn_in['conv_w'], 'L0_attn_conv_b': _L0_attn_in['conv_b'], 'L0_attn_x_proj_w': _L0_attn_in['x_proj_w'], 'L0_attn_x_proj_b': _L0_attn_in['x_proj_b'], 'L0_attn_dt_proj_w': _L0_attn_in['dt_proj_w'], 'L0_attn_dt_proj_b': _L0_attn_in['dt_proj_b'], 'L0_attn_D': _L0_attn_in['D'], 'L0_attn_out_proj_w': _L0_attn_in['out_proj_w'], 'L0_attn_out_proj_b': _L0_attn_in['out_proj_b'], 'L0_ffn_Wg': _L0_ffn_in['Wg'], 'L0_ffn_bg': _L0_ffn_in['bg'], 'L0_ffn_Wt': _L0_ffn_in['Wt'], 'L0_ffn_bt': _L0_ffn_in['bt'], 'L0_ffn_W1': _L0_ffn_in['W1'], 'L0_ffn_b1': _L0_ffn_in['b1'], 'L0_ffn_W2': _L0_ffn_in['W2'], 'L0_ffn_b2': _L0_ffn_in['b2'], 'L0_c': _L0_c, 'L0_wmod': _L0_wmod, 'L1_attn_qkv_w': _L1_attn_in['qkv_w'], 'L1_attn_out_w': _L1_attn_in['out_w'], 'L1_ffn_wqkv': _L1_ffn_in['wqkv'], 'L1_ffn_q_scale': _L1_ffn_in['q_scale'], 'L1_ffn_k_scale': _L1_ffn_in['k_scale'], 'L1_ffn_wo': _L1_ffn_in['wo'], 'L1_ffn_ln_g': _L1_ffn_in['ln_g'], 'L1_ffn_ln_b': _L1_ffn_in['ln_b'], 'L1_ffn_w1': _L1_ffn_in['w1'], 'L1_ffn_b1': _L1_ffn_in['b1'], 'L1_ffn_w2': _L1_ffn_in['w2'], 'L1_ffn_b2': _L1_ffn_in['b2'], 'L1_c': _L1_c, 'L1_wmod': _L1_wmod}
    _x0 = _d['L0_attn_x']
    _d['L0_attn_x'] = jax.random.normal(jax.random.fold_in(jax.random.key(seed), 1), (4, 1024, 128), dtype=_x0.dtype)
    del _x0
    return _d

def reference(L0_attn_x, L0_attn_in_proj_w, L0_attn_in_proj_b, L0_attn_conv_w, L0_attn_conv_b, L0_attn_x_proj_w, L0_attn_x_proj_b, L0_attn_dt_proj_w, L0_attn_dt_proj_b, L0_attn_D, L0_attn_out_proj_w, L0_attn_out_proj_b, L0_ffn_Wg, L0_ffn_bg, L0_ffn_Wt, L0_ffn_bt, L0_ffn_W1, L0_ffn_b1, L0_ffn_W2, L0_ffn_b2, L0_c, L0_wmod, L1_attn_qkv_w, L1_attn_out_w, L1_ffn_wqkv, L1_ffn_q_scale, L1_ffn_k_scale, L1_ffn_wo, L1_ffn_ln_g, L1_ffn_ln_b, L1_ffn_w1, L1_ffn_b1, L1_ffn_w2, L1_ffn_b2, L1_c, L1_wmod):

    def _L0_attn_ref(x, in_proj_w, in_proj_b, conv_w, conv_b, x_proj_w, x_proj_b, dt_proj_w, dt_proj_b, D, out_proj_w, out_proj_b):
        import jax, jax.numpy as jnp
        import numpy as np
        D_MODEL, D_STATE, D_CONV, EXPAND = (128, 16, 4, 2)
        D_INNER = EXPAND * D_MODEL
        BATCH, LENGTH = (2, 128)

        def _mamba_fwd(x, in_proj_w, in_proj_b, conv_w, conv_b, x_proj_w, x_proj_b, dt_proj_w, dt_proj_b, D, out_proj_w, out_proj_b):
            batch, length, _ = x.shape
            d_inner = D.shape[0]
            d_state = dt_proj_w.shape[0]
            d_conv = conv_w.shape[-1]
            xz = x @ in_proj_w + in_proj_b
            xc, z = jnp.split(xz, 2, axis=-1)
            xc_bdl = jnp.transpose(xc, (0, 2, 1))
            xc_bdl = jax.lax.conv_general_dilated(xc_bdl, conv_w, window_strides=(1,), padding=[(d_conv - 1, 0)], dimension_numbers=('NCH', 'OIH', 'NCH'), feature_group_count=d_inner)
            xc_bdl = xc_bdl + conv_b[None, :, None]
            xc = jnp.transpose(xc_bdl, (0, 2, 1))
            xc = jax.nn.silu(xc)
            dBu = xc @ x_proj_w + x_proj_b
            delta_s, B, u = jnp.split(dBu, [d_state, 2 * d_state], axis=-1)
            delta = jax.nn.softplus(delta_s @ dt_proj_w + dt_proj_b)
            A = -jnp.arange(1, d_state + 1, dtype=x.dtype)
            deltaA = jnp.exp(delta[..., None] * A)
            deltaB_u = delta[..., None] * B[:, :, None, :] * u[..., None]
            dA_t = jnp.moveaxis(deltaA, 1, 0)
            dBu_t = jnp.moveaxis(deltaB_u, 1, 0)

            def step(h, inp):
                dA, dBu_ = inp
                h = dA * h + dBu_
                return (h, h.sum(-1))
            h0 = jnp.zeros((batch, d_inner, d_state), x.dtype)
            _, y_t = jax.lax.scan(step, h0, (dA_t, dBu_t))
            y = jnp.moveaxis(y_t, 0, 1)
            y = y + u * D
            y = y * jax.nn.silu(z)
            return y @ out_proj_w + out_proj_b
        return _mamba_fwd(x, in_proj_w, in_proj_b, conv_w, conv_b, x_proj_w, x_proj_b, dt_proj_w, dt_proj_b, D, out_proj_w, out_proj_b)

    def _L0_ffn_ref(inputs, Wg, bg, Wt, bt, W1, b1, W2, b2):
        import jax, jax.numpy as jnp
        import numpy as np
        MAX_THRESHOLD = 0.125
        x = inputs.reshape(-1, inputs.shape[-1])
        gate = jax.nn.softmax(x @ Wg + bg, axis=-1)
        thr = jax.nn.sigmoid(x @ Wt + bt) * MAX_THRESHOLD
        adapted = gate - thr
        mask = (adapted >= 0).astype(x.dtype)
        w = adapted * mask
        s = jnp.sum(w, axis=-1, keepdims=True)
        s = jnp.where(s == 0, jnp.ones_like(s), s)
        w = w / s
        h = jax.nn.gelu(jnp.einsum('td,edf->etf', x, W1) + b1[:, None, :])
        eo = jnp.einsum('etf,efd->etd', h, W2) + b2[:, None, :]
        out = jnp.einsum('te,etd->td', w, eo)
        return out.reshape(inputs.shape)

    def _L1_attn_ref(x, qkv_w, out_w):
        import jax, jax.numpy as jnp
        import numpy as np
        EMB = 128
        HEADS = 16
        HEAD_DIM = EMB // HEADS
        BLOCK = 32
        N_GLOBAL = 4
        WINDOW = 128
        ROPE_BASE = 10000.0

        def rotate_half(x):
            x1 = x[..., ::2]
            x2 = x[..., 1::2]
            return jnp.stack((-x2, x1), axis=-1).reshape(x.shape)

        def rope_cos_sin(seq_len, dtype=jnp.float32):
            inv_freq = 1.0 / ROPE_BASE ** (jnp.arange(0, HEAD_DIM, 2, dtype=jnp.float32) / HEAD_DIM)
            pos = jnp.arange(seq_len, dtype=jnp.float32)
            freqs = jnp.outer(pos, inv_freq)
            emb = jnp.concatenate([freqs, freqs], -1)
            return (jnp.cos(emb)[None, None].astype(dtype), jnp.sin(emb)[None, None].astype(dtype))

        def block_mask(seq_len):
            i = jnp.arange(seq_len)[:, None]
            j = jnp.arange(seq_len)[None, :]
            blk = i // BLOCK == j // BLOCK
            glob = (i < N_GLOBAL) | (j < N_GLOBAL)
            slide = jnp.abs(i - j) <= WINDOW
            return (blk | glob | slide) & (j <= i)
        B, S, E = x.shape
        scale = HEAD_DIM ** (-0.5)
        qkv = x @ qkv_w.T
        qkv = qkv.reshape(B, S, 3, HEADS, HEAD_DIM)
        qkv = jnp.transpose(qkv, (2, 0, 3, 1, 4))
        q, k, v = (qkv[0], qkv[1], qkv[2])
        cos, sin = rope_cos_sin(S, x.dtype)
        q = q * cos + rotate_half(q) * sin
        k = k * cos + rotate_half(k) * sin
        mask = block_mask(S)
        scores = jnp.einsum('bhqd,bhkd->bhqk', q, k) * scale
        scores = jnp.where(mask[None, None], scores, jnp.finfo(scores.dtype).min)
        attn = jax.nn.softmax(scores, axis=-1)
        out = jnp.einsum('bhqk,bhkd->bhqd', attn, v)
        out = jnp.transpose(out, (0, 2, 1, 3)).reshape(B, S, E)
        return out @ out_w.T

    def _L1_ffn_ref(x, wqkv, q_scale, k_scale, wo, ln_g, ln_b, w1, b1, w2, b2):
        import jax, jax.numpy as jnp
        import numpy as np
        DIM = 128
        DEPTH = 2
        HEADS = 8
        DIM_HEAD = 64
        WINDOW = 64
        INNER = HEADS * DIM_HEAD
        HID = int(DIM * 4 * 2 / 3)
        B, N = (2, 1024)
        QK_SCALE = 8.0

        def shift_token(t):
            t1, t2 = jnp.split(t, 2, axis=-1)
            t2 = jnp.pad(t2, ((0, 0), (1, 0), (0, 0)))[:, :-1]
            return jnp.concatenate([t1, t2], axis=-1)

        def l2norm(t):
            return t / jnp.clip(jnp.linalg.norm(t, axis=-1, keepdims=True), 1e-12)

        def rotate_half(x):
            x1, x2 = jnp.split(x, 2, axis=-1)
            return jnp.concatenate([-x2, x1], axis=-1)

        def rotary_xpos(q, k):
            n = q.shape[-2]
            half_idx = jnp.arange(0, DIM_HEAD, 2, dtype=jnp.float32)
            inv_freq = 1.0 / 10000.0 ** (half_idx / DIM_HEAD)
            t = jnp.arange(n, dtype=jnp.float32)
            freqs = t[:, None] * inv_freq[None, :]
            freqs = jnp.concatenate([freqs, freqs], axis=-1)
            base = (half_idx + 0.4 * DIM_HEAD) / (1.4 * DIM_HEAD)
            power = (t - n // 2) / float(WINDOW // 2)
            scale = base[None, :] ** power[:, None]
            scale = jnp.concatenate([scale, scale], axis=-1)
            cos, sin = (jnp.cos(freqs), jnp.sin(freqs))
            q = q * cos * scale + rotate_half(q) * sin * scale
            k = k * cos / scale + rotate_half(k) * sin / scale
            return (q, k)

        def local_attention(q, k, v):
            b, h, n, d = q.shape
            w = n // WINDOW
            bq = q.reshape(b, h, w, WINDOW, d) * QK_SCALE
            bk = k.reshape(b, h, w, WINDOW, d)
            bv = v.reshape(b, h, w, WINDOW, d)

            def look_around(t):
                p = jnp.pad(t, ((0, 0), (0, 0), (1, 0), (0, 0), (0, 0)))
                return jnp.concatenate([p[:, :, :w], p[:, :, 1:]], axis=3)
            bk, bv = (look_around(bk), look_around(bv))
            bt = jnp.arange(n).reshape(w, WINDOW)
            btp = jnp.pad(bt, ((1, 0), (0, 0)), constant_values=-1)
            btk = jnp.concatenate([btp[:w], btp[1:]], axis=1)
            sim = jnp.einsum('bhwid,bhwjd->bhwij', bq, bk)
            i = bt[:, :, None]
            j = btk[:, None, :]
            mask = (i < j) | (i > j + WINDOW) | (j == -1)
            sim = jnp.where(mask, -jnp.finfo(sim.dtype).max, sim)
            attn = jax.nn.softmax(sim, axis=-1)
            out = jnp.einsum('bhwij,bhwjd->bhwid', attn, bv)
            return out.reshape(b, h, n, d)

        def _layer(x, wqkv, qs, ksc, wo, lg, lb, w1, b1, w2, b2):
            b, n, _ = x.shape
            h = shift_token(x)
            qkv = h @ wqkv
            q, k, v = jnp.split(qkv, 3, axis=-1)
            to_heads = lambda t: t.reshape(b, n, HEADS, DIM_HEAD).transpose(0, 2, 1, 3)
            q, k, v = (to_heads(q), to_heads(k), to_heads(v))
            q = l2norm(q) * qs
            k = l2norm(k) * ksc
            q, k = rotary_xpos(q, k)
            o = local_attention(q, k, v)
            o = o.transpose(0, 2, 1, 3).reshape(b, n, INNER)
            x = x + o @ wo
            h = shift_token(x)
            mu = h.mean(-1, keepdims=True)
            var = h.var(-1, keepdims=True)
            h = (h - mu) / jnp.sqrt(var + 1e-05) * lg + lb
            h = h @ w1 + b1
            a, g = jnp.split(h, 2, axis=-1)
            h = a * jax.nn.gelu(g, approximate=False)
            x = x + h @ w2 + b2
            return x
        for l in range(DEPTH):
            x = _layer(x, wqkv[l], q_scale[l], k_scale[l], wo[l], ln_g[l], ln_b[l], w1[l], b1[l], w2[l], b2[l])
        return x
    x = L0_attn_x
    mod = (_silu(L0_c) @ L0_wmod).reshape(L0_c.shape[0], 6, 1, -1)
    sa, ca, ga, sb, cb, gb = (mod[:, 0], mod[:, 1], mod[:, 2], mod[:, 3], mod[:, 4], mod[:, 5])
    ga = (2 * (ga >= 0) - 1) * jnp.maximum(jnp.abs(ga), 0.25)
    gb = (2 * (gb >= 0) - 1) * jnp.maximum(jnp.abs(gb), 0.25)
    h = _layernorm(x, axis=-1) * (1 + ca) + sa
    x = x + ga * _L0_attn_ref(h, L0_attn_in_proj_w, L0_attn_in_proj_b, L0_attn_conv_w, L0_attn_conv_b, L0_attn_x_proj_w, L0_attn_x_proj_b, L0_attn_dt_proj_w, L0_attn_dt_proj_b, L0_attn_D, L0_attn_out_proj_w, L0_attn_out_proj_b)
    h = _layernorm(x, axis=-1) * (1 + cb) + sb
    x = x + gb * _L0_ffn_ref(h, L0_ffn_Wg, L0_ffn_bg, L0_ffn_Wt, L0_ffn_bt, L0_ffn_W1, L0_ffn_b1, L0_ffn_W2, L0_ffn_b2)
    mod = (_silu(L1_c) @ L1_wmod).reshape(L1_c.shape[0], 6, 1, -1)
    sa, ca, ga, sb, cb, gb = (mod[:, 0], mod[:, 1], mod[:, 2], mod[:, 3], mod[:, 4], mod[:, 5])
    ga = (2 * (ga >= 0) - 1) * jnp.maximum(jnp.abs(ga), 0.25)
    gb = (2 * (gb >= 0) - 1) * jnp.maximum(jnp.abs(gb), 0.25)
    h = _layernorm(x, axis=-1) * (1 + ca) + sa
    x = x + ga * _L1_attn_ref(h, L1_attn_qkv_w, L1_attn_out_w)
    h = _layernorm(x, axis=-1) * (1 + cb) + sb
    x = x + gb * _L1_ffn_ref(h, L1_ffn_wqkv, L1_ffn_q_scale, L1_ffn_k_scale, L1_ffn_wo, L1_ffn_ln_g, L1_ffn_ln_b, L1_ffn_w1, L1_ffn_b1, L1_ffn_w2, L1_ffn_b2)
    return x

_drawn_inputs = setup_inputs


def setup_inputs(seed=0):
    import zlib

    import numpy as np

    out = dict(_drawn_inputs(seed))
    spreads = {'L0_attn_D': (1.0, 0.6),
     'L0_ffn_bg': (0.0, 0.8),
     'L0_ffn_b1': (0.0, 0.748),
     'L0_ffn_b2': (0.0, 0.539),
     'L1_ffn_q_scale': (1.0, 0.6),
     'L1_ffn_k_scale': (1.0, 0.6),
     'L1_ffn_ln_g': (1.0, 0.6),
     'L1_ffn_ln_b': (0.0, 0.8),
     'L1_ffn_b1': (0.0, 0.8),
     'L1_ffn_b2': (0.0, 0.8)}
    factors = {'L0_attn_out_proj_b': 3.148,
     'L0_ffn_Wt': 4.223,
     'L1_ffn_wqkv': 7.965,
     'L1_ffn_wo': 8.0,
     'L1_ffn_w1': 8.0,
     'L1_ffn_w2': 8.0}
    for name, (base, spread) in spreads.items():
        noise = np.random.default_rng([zlib.crc32(name.encode()), seed]).standard_normal(out[name].shape)
        drawn = base * np.exp(spread * noise) if base else spread * noise
        out[name] = jnp.asarray(drawn.astype(out[name].dtype))
    for name, factor in factors.items():
        out[name] = (out[name] * factor).astype(out[name].dtype)
    return out
```

```python
from contextlib import ExitStack

import numpy as np

import concourse.bass as bass
from concourse import mybir

ALU = mybir.AluOpType
ACT = mybir.ActivationFunctionType
F32 = mybir.dt.float32
BF16 = mybir.dt.bfloat16
AX_X = mybir.AxisListType.X

P = 128
NB = 4
L = 1024
T = NB * L
TILE = 512
PAIRS = T // (2 * TILE)
XCW = L + 4
NS = 16
EPS = 1e-5
LN_EXP = "natural_log_exp_and_others"


class Pool_:

    def __init__(self, nc, prefix):
        self.nc, self.prefix, self.stack, self.sems = nc, prefix, ExitStack(), []

    def __enter__(self):
        return self

    def __exit__(self, *a):
        if self.sems:
            self.nc.clear_and_free_semaphores(self.sems)
            self.nc.all_engine_barrier()
        return self.stack.__exit__(*a)

    def sb(self, name, shape, dt=F32):
        return self.stack.enter_context(self.nc.sbuf_tensor(self.prefix + name, shape, dt))

    def ps(self, name, shape, dt=F32):
        return self.stack.enter_context(self.nc.psum_tensor(self.prefix + name, shape, dt))

    def sem(self, name):
        self.sems.append(self.nc.alloc_semaphore(name=self.prefix + name))
        return self.sems[-1]


def cols(t, n=TILE):
    return bass.ds(t * n, n)


def modulation(nc, mem, cT_d, wmod_d, tag, mod):
    with Pool_(nc, tag) as m:
        cT = m.sb("cT", [P, NB])
        silu_c = m.sb("silu_c", [P, NB])
        wmod = m.sb("wmod", [P, 6 * P])
        raw = m.sb("raw", [P, 6, NB])
        sign = m.sb("sign", [P, 2, NB])
        size = m.sb("size", [P, 2, NB])
        size2 = m.sb("size2", [P, 2, NB])
        acc = m.ps("acc", [P, 6, NB])
        loaded = m.sem("loaded")
        silu_done = m.sem("silu_done")
        mm_done = m.sem("mm_done")
        step = m.sem("step")
        with nc.Block() as block:
            @block.sync
            def _(sp):
                sp.dma_start(cT[:, :], cT_d).then_inc(loaded, 16)
                sp.dma_start(wmod[:, :], wmod_d).then_inc(loaded, 16)

            @block.scalar
            def _(act):
                act.wait_ge(loaded, 32)
                nc.scalar.activation(silu_c[:, :], cT[:, :], ACT.Silu).then_inc(silu_done, 1)

            @block.tensor
            def _(pe):
                pe.wait_ge(silu_done, 1)
                for j in range(6):
                    last = nc.tensor.matmul(acc[:, j, :], wmod[:, j * P:(j + 1) * P], silu_c[:, :], start=True, stop=True)
                last.then_inc(mm_done, 1)

            @block.vector
            def _(dve):
                dve.wait_ge(mm_done, 1)
                nc.vector.tensor_copy(raw[:, :, :], acc[:, :, :]).then_inc(step, 1)
                dve.wait_ge(step, 1)
                nc.vector.tensor_copy(mod[:, 0::3, :], raw[:, 0::3, :]).then_inc(step, 1)
                nc.vector.tensor_scalar(mod[:, 1::3, :], raw[:, 1::3, :], 1.0, None, ALU.add).then_inc(step, 1)
                nc.vector.tensor_scalar(sign[:, :, :], raw[:, 2::3, :], 0.0, 2.0, ALU.is_ge, ALU.mult).then_inc(step, 1)
                nc.vector.scalar_tensor_tensor(out=size[:, :, :], in0=raw[:, 2::3, :], scalar=-1.0, in1=raw[:, 2::3, :],
                                               op0=ALU.mult, op1=ALU.max).then_inc(step, 1)
                dve.wait_ge(step, 5)
                nc.vector.tensor_scalar(size2[:, :, :], size[:, :, :], 0.25, None, ALU.max).then_inc(step, 1)
                dve.wait_ge(step, 6)
                nc.vector.scalar_tensor_tensor(out=mod[:, 2::3, :], in0=sign[:, :, :], scalar=-1.0, in1=size2[:, :, :],
                                               op0=ALU.add, op1=ALU.mult).then_inc(step, 1)


def layernorm(nc, mem, tag, x, h, center, mean, eps_col, scale_of, shift_of, modulated=True):
    with Pool_(nc, tag) as m:
        sq = m.sb("sq", [P, 2, TILE])
        lnv = m.sb("lnv", [P, 2, TILE])
        rstd = m.sb("rstd", [P, 2, TILE])
        xn = m.sb("xn", [P, 2, TILE])
        cen = m.ps("cen", [P, 2, 512])
        var = m.ps("var", [P, 2, 512])
        cen_done = m.sem("cen_done")
        sq_done = m.sem("sq_done")
        var_done = m.sem("var_done")
        ln_done = m.sem("ln_done")
        rstd_done = m.sem("rstd_done")
        xn_done = m.sem("xn_done")
        h_done = m.sem("h_done")
        with nc.Block() as block:
            @block.tensor
            def _(pe):
                nc.tensor.sem_inc(var_done, 2)
                with nc.tensor.Fori(0, PAIRS) as p:
                    for j in range(2):
                        pe.wait_ge(xn_done, 2 * p + j + 1)
                        nc.tensor.matmul(cen[:, j, :], center, x[:, cols(2 * p + j)], start=True, stop=True).then_inc(cen_done, 1)
                    for j in range(2):
                        pe.wait_ge(sq_done, 2 * p + j + 1)
                        pe.wait_ge(ln_done, 2 * p + j + 1)
                        nc.tensor.matmul(var[:, j, :], mean, sq[:, j, :], start=True, stop=True).then_inc(var_done, 1)

            @block.scalar
            def _(act):
                nc.scalar.preload_act_table_set(LN_EXP)
                nc.scalar.sem_inc(ln_done, 2)
                with nc.scalar.Fori(0, PAIRS) as p:
                    for j in range(2):
                        act.wait_ge(cen_done, 2 * p + j + 1)
                        act.wait_ge(var_done, 2 * p + j + 1)
                        nc.scalar.activation(sq[:, j, :], cen[:, j, :], ACT.Square).then_inc(sq_done, 1)
                    for j in range(2):
                        act.wait_ge(var_done, 2 * p + j + 3)
                        nc.scalar.activation(lnv[:, j, :], var[:, j, :], ACT.Ln, bias=eps_col).then_inc(ln_done, 1)
                    for j in range(2):
                        act.wait_ge(ln_done, 2 * p + j + 3)
                        act.wait_ge(xn_done, 2 * p + j + 1)
                        nc.scalar.activation(rstd[:, j, :], lnv[:, j, :], ACT.Exp, scale=-0.5).then_inc(rstd_done, 1)

            @block.vector
            def _(dve):
                nc.vector.sem_inc(xn_done, 2)
                nc.vector.sem_inc(h_done, 2)
                with nc.vector.Fori(0, PAIRS) as p:
                    for j in range(2):
                        dve.wait_ge(rstd_done, 2 * p + j + 1)
                        dve.wait_ge(h_done, 2 * p + j + 1)
                        nc.vector.tensor_tensor(xn[:, j, :], cen[:, j, :], rstd[:, j, :], ALU.mult).then_inc(xn_done, 1)
                        dve.wait_ge(xn_done, 2 * p + j + 3)
                        nc.vector.tensor_scalar(h[:, cols(2 * p + j)], xn[:, j, :], scale_of(p), shift_of(p),
                                                ALU.mult, ALU.add).then_inc(h_done, 1)


def mamba_inputs(nc, tag, W, h, u, delta, zs, B_dram):
    with Pool_(nc, tag) as m:
        xc = m.sb("xc", [P, 2, NB * XCW])
        cv = m.sb("cv", [P, 2, TILE])
        cv2 = m.sb("cv2", [P, 2, TILE])
        xcs = m.sb("xcs", [P, 2, 2, TILE])
        dsB = m.sb("dsB", [32, 2, TILE])
        p_in = m.ps("p_in", [P, 4, 512])
        p_xp = m.ps("p_xp", [P, 3, 512])
        p_dt = m.ps("p_dt", [P, 512])
        pads = m.sem("pads")
        in_done = m.sem("in_done")
        xc_done = m.sem("xc_done")
        conv_step = m.sem("conv_step")
        silu_done = m.sem("silu_done")
        xp_done = m.sem("xp_done")
        xp_out = m.sem("xp_out")
        dt_done = m.sem("dt_done")
        dt_out = m.sem("dt_out")
        B_out = [m.sem(f"B_out{j}") for j in range(2)]
        with nc.Block() as block:
            @block.tensor
            def _(pe):
                def in_proj(t):
                    for k in range(4):
                        pe.wait_ge(xc_done, 4 * t + k + 1)
                        nc.tensor.matmul(p_in[:, k, :], W["in_w"][:, k * P:(k + 1) * P], h[:, cols(t)],
                                         start=True, stop=True).then_inc(in_done, 1)

                def x_proj(t, j):
                    for k in range(3):
                        out = p_xp[0:32, 0, :] if k == 0 else p_xp[:, k, :]
                        lo, hi = (0, 32) if k == 0 else (32 + (k - 1) * P, 32 + k * P)
                        pe.wait_ge(silu_done, 2 * t + 4)
                        pe.wait_ge(xp_out, 3 * t + k + 1)
                        for c in range(2):
                            last = nc.tensor.matmul(out, W["xp_w"][:, c, lo:hi], xcs[:, j, c, :],
                                                    start=c == 0, stop=c == 1)
                        last.then_inc(xp_done, 1)
                    for c in range(2):
                        pe.wait_ge(xp_out, 3 * t + 4)
                        pe.wait_ge(dt_out, 2 * t + c + 1)
                        nc.tensor.matmul(p_dt[:, :], W["dt_w"][:, c * P:(c + 1) * P], dsB[0:16, j, :],
                                         start=True, stop=True).then_inc(dt_done, 1)

                nc.tensor.sem_inc(xp_done, 6)
                nc.tensor.sem_inc(dt_done, 4)
                in_proj(0)
                with nc.tensor.Fori(0, PAIRS - 1) as p:
                    for j in range(2):
                        in_proj(2 * p + j + 1)
                        x_proj(2 * p + j, j)
                in_proj(T // TILE - 1)
                x_proj(T // TILE - 2, 0)
                x_proj(T // TILE - 1, 1)

            @block.scalar
            def _(act):
                def leave_in(t, b, half):
                    for k in range(4):
                        act.wait_ge(in_done, 4 * t + k + 1)
                        if k < 2:
                            nc.scalar.activation(xc[:, k, bass.ds(b * XCW + 3 + half * TILE, TILE)], p_in[:, k, :],
                                                 ACT.Identity, bias=W["in_b"][:, k:k + 1]).then_inc(xc_done, 1)
                        else:
                            nc.scalar.activation(zs[:, k - 2, cols(t)], p_in[:, k, :], ACT.Silu,
                                                 bias=W["in_b"][:, k:k + 1]).then_inc(xc_done, 1)

                def silu_conv(t, j):
                    for c in range(2):
                        act.wait_ge(conv_step, 8 * t + 8 + c)
                        act.wait_ge(xp_done, 3 * t + 3)
                        nc.scalar.activation(xcs[:, j, c, :], cv[:, c, :], ACT.Silu,
                                             bias=W["conv_b"][:, c:c + 1]).then_inc(silu_done, 1)

                nc.scalar.sem_inc(xc_done, 4)
                nc.scalar.sem_inc(silu_done, 2)
                nc.scalar.preload_act_table(ACT.Silu)
                leave_in(0, 0, 0)
                with nc.scalar.Fori(0, PAIRS - 1) as p:
                    for j in range(2):
                        t = 2 * p + j + 1
                        leave_in(t, p + j, 1 - j)
                        silu_conv(2 * p + j, j)
                leave_in(T // TILE - 1, NB - 1, 1)
                silu_conv(T // TILE - 2, 0)
                silu_conv(T // TILE - 1, 1)

            @block.vector
            def _(dve):
                def conv(t, p, half):
                    dve.wait_ge(xc_done, 4 * t + 4 + 2)
                    for k in range(4):
                        for c in range(2):
                            n = 8 * t + 1 + 2 * k + c
                            src = xc[:, c, bass.ds(p * XCW + half * TILE + k, TILE)]
                            w = W["conv_w"][:, c, k:k + 1]
                            dst = (cv2 if k % 2 == 0 else cv)[:, c, :]
                            if k == 0:
                                if c == 0:
                                    dve.wait_ge(conv_step, n)
                                nc.vector.tensor_scalar(dst, src, w, None, ALU.mult).then_inc(conv_step, 1)
                            else:
                                dve.wait_ge(conv_step, n - 1)
                                if k == 1:
                                    dve.wait_ge(silu_done, 2 * t + c + 1)
                                prev = (cv if k % 2 == 0 else cv2)[:, c, :]
                                nc.vector.scalar_tensor_tensor(out=dst, in0=src, scalar=w, in1=prev, op0=ALU.mult,
                                                               op1=ALU.add).then_inc(conv_step, 1)

                def leave_xp(t, j):
                    dve.wait_ge(xp_done, 3 * t + 7)
                    dve.wait_ge(dt_done, 2 * t + 2)
                    dve.wait_ge(B_out[j], 8 * t - 8 * j + 16)
                    nc.vector.tensor_scalar(dsB[:, j, :], p_xp[0:32, 0, :], W["dsB_b"], None, ALU.add).then_inc(xp_out, 1)
                    for c in range(2):
                        dve.wait_ge(xp_done, 3 * t + 8 + c)
                        nc.vector.tensor_scalar(u[:, c, cols(t)], p_xp[:, 1 + c, :], W["u_b"][:, c:c + 1], None,
                                                ALU.add).then_inc(xp_out, 1)
                    for c in range(2):
                        dve.wait_ge(dt_done, 2 * t + c + 5)
                        nc.vector.tensor_scalar(delta[:, c, cols(t)], p_dt[:, :], W["dt_b"][:, c:c + 1], None,
                                                ALU.add).then_inc(dt_out, 1)

                nc.vector.sem_inc(xp_out, 3)
                nc.vector.sem_inc(dt_out, 1)
                nc.vector.memset(xc[:, :, :].rearrange("q c (b w) -> q c b w", b=NB)[:, :, :, 0:3], 0.0).then_inc(conv_step, 1)
                with nc.vector.Fori(0, PAIRS) as p:
                    for j in range(2):
                        conv(2 * p + j, p, j)
                        leave_xp(2 * p + j, j)

            @block.sync
            def _(sp):
                for j in range(2):
                    nc.sync.sem_inc(B_out[j], 16)
                with nc.sync.Fori(0, PAIRS) as p:
                    for j in range(2):
                        sp.wait_ge(xp_out, 3 * (2 * p + j) + 4)
                        sp.dma_start(B_dram[:, cols(2 * p + j)], dsB[16:32, j, :]).then_inc(B_out[j], 16)
                for j in range(2):
                    sp.wait_ge(B_out[j], 16 * (PAIRS + 1))


def softplus(nc, tag, delta, one_col):
    with Pool_(nc, tag) as m:
        size = m.sb("size", [P, 2, L])
        e = m.sb("e", [P, 2, L])
        l = m.sb("l", [P, 2, L])
        size_done = m.sem("size_done")
        e_done = m.sem("e_done")
        l_done = m.sem("l_done")
        out_done = m.sem("out_done")
        with nc.Block() as block:
            @block.vector
            def _(dve):
                def absolute(b):
                    for c in range(2):
                        dve.wait_ge(e_done, 2 * b + c + 1)
                        v = delta[:, c, cols(b, L)]
                        nc.vector.scalar_tensor_tensor(out=size[:, c, :], in0=v, scalar=-1.0, in1=v, op0=ALU.mult,
                                                       op1=ALU.max).then_inc(size_done, 1)

                def total(b):
                    for c in range(2):
                        dve.wait_ge(l_done, 2 * b + c + 3)
                        v = delta[:, c, cols(b, L)]
                        nc.vector.scalar_tensor_tensor(out=v, in0=v, scalar=0.0, in1=l[:, c, :], op0=ALU.max,
                                                       op1=ALU.add).then_inc(out_done, 1)

                nc.vector.sem_inc(out_done, 2)
                absolute(0)
                with nc.vector.Fori(0, NB - 1) as b:
                    absolute(b + 1)
                    total(b)
                total(NB - 1)

            @block.scalar
            def _(act):
                nc.scalar.sem_inc(e_done, 2)
                nc.scalar.sem_inc(l_done, 2)
                nc.scalar.preload_act_table_set(LN_EXP)
                with nc.scalar.Fori(0, NB) as b:
                    for c in range(2):
                        act.wait_ge(size_done, 2 * b + c + 1)
                        act.wait_ge(l_done, 2 * b + c + 1)
                        nc.scalar.activation(e[:, c, :], size[:, c, :], ACT.Exp, scale=-1.0).then_inc(e_done, 1)
                    for c in range(2):
                        act.wait_ge(e_done, 2 * b + c + 3)
                        act.wait_ge(out_done, 2 * b + c + 1)
                        nc.scalar.activation(l[:, c, :], e[:, c, :], ACT.Ln, bias=one_col).then_inc(l_done, 1)


def mamba_scan(nc, tag, W, x, u, delta, zs, B_dram, ident, mod):
    NG = 4
    CH = NS // NG
    ND = 2
    NI = 4
    NT = 2
    U = 2 * NS
    with Pool_(nc, tag) as m:
        w = m.sb("w", [P, 2, L])
        Bb = m.sb("Bb", [P, 2, NG, L])
        dec = m.sb("dec", [P, ND, L])
        inp = m.sb("inp", [P, NI, L])
        st = m.sb("st", [P, NT, L])
        y = m.sb("y", [P, 2, L])
        upd = m.sb("upd", [P, 2, TILE])
        p_y = m.ps("p_y", [P, 2, 2, 512])
        p_o = m.ps("p_o", [P, 2, 512])
        B_in = [m.sem(f"B_in{k}") for k in range(2)]
        w_done = m.sem("w_done")
        tick = m.sem("tick")
        dec_done = m.sem("dec_done")
        inp_v = m.sem("inp_v")
        inp_g = m.sem("inp_g")
        st_done = m.sem("st_done")
        sum_done = m.sem("sum_done")
        yu_done = m.sem("yu_done")
        y_done = m.sem("y_done")
        o_done = m.sem("o_done")
        upd_step = m.sem("upd_step")
        units = [(q, c, q * NG + i, i) for q in range(CH) for c in range(2) for i in range(NG)]
        on_pool = [k % 2 == 1 for k in range(U)]
        before_v = [sum(not o for o in on_pool[:k]) for k in range(U + 1)]
        before_g = [sum(on_pool[:k]) for k in range(U + 1)]
        with nc.Block() as block:
            @block.sync
            def _(sp):
                with nc.sync.Fori(0, NB) as b:
                    for q in range(CH):
                        sp.wait_ge(inp_v, before_v[U] * b + before_v[8 * q] + 4)
                        sp.wait_ge(inp_g, before_g[U] * b + before_g[8 * q] + 4)
                        sp.dma_start(Bb[:, q % 2, :, :], B_dram[q * NG:(q + 1) * NG, cols(b, L)].partition_broadcast(P)
                                     ).then_inc(B_in[q % 2], 16)

            @block.scalar
            def _(act):
                nc.scalar.preload_act_table_set(LN_EXP)
                with nc.scalar.Fori(0, NB) as b:
                    for k, (q, c, n, i) in enumerate(units):
                        act.wait_ge(st_done, U * b + k + NI - ND + 1)
                        nc.scalar.sem_inc(tick, 1)
                        nc.scalar.activation(dec[:, k % ND, :], delta[:, c, cols(b, L)], ACT.Exp,
                                             scale=-float(n + 1)).then_inc(dec_done, 1)

            def make_input(eng, ns, k, b, done):
                q, c, n, i = units[k]
                eng.wait_ge(B_in[q % 2], 32 * b + 16 * (q // 2) + 16)
                eng.wait_ge(w_done, 2 * b + c + 1)
                eng.wait_ge(st_done, U * b + k + 1)
                ns.tensor_tensor(inp[:, k % NI, :], w[:, c, :], Bb[:, q % 2, i, :], ALU.mult).then_inc(done, 1)

            @block.gpsimd
            def _(pool):
                nc.gpsimd.sem_inc(inp_g, 8)
                with nc.gpsimd.Fori(0, NB) as b:
                    for c in range(2):
                        pool.wait_ge(inp_v, before_v[U] * b + 8)
                        pool.wait_ge(inp_g, before_g[U] * b + 8)
                        nc.gpsimd.tensor_tensor(w[:, c, :], u[:, c, cols(b, L)], delta[:, c, cols(b, L)],
                                                ALU.mult).then_inc(w_done, 1)
                    for k in range(U):
                        if on_pool[k]:
                            make_input(pool, nc.gpsimd, k, b, inp_g)

            @block.vector
            def _(dve):
                nc.vector.sem_inc(inp_v, 8)
                nc.vector.sem_inc(st_done, NI)
                nc.vector.sem_inc(yu_done, 2)
                nc.vector.sem_inc(upd_step, 4)

                def scan(k, b):
                    dve.wait_ge(dec_done, U * b + k + 1)
                    if on_pool[k]:
                        dve.wait_ge(inp_g, before_g[U] * b + before_g[k] + 9)
                    else:
                        dve.wait_ge(inp_v, before_v[U] * b + before_v[k] + 9)
                    dve.wait_ge(sum_done, U * b + k + 1)
                    nc.vector.tensor_tensor_scan(st[:, k % NT, :], dec[:, k % ND, :], inp[:, k % NI, :], 0.0,
                                                 ALU.mult, ALU.add).then_inc(st_done, 1)

                with nc.vector.Fori(0, NB) as b:
                    for k in range(U):
                        if not on_pool[k]:
                            make_input(dve, nc.vector, k, b, inp_v)
                        if k >= 1:
                            scan(k - 1, b)
                    scan(U - 1, b)
                    dve.wait_ge(sum_done, U * b + U + NT)
                    for c in range(2):
                        dve.wait_ge(o_done, 2 * b + 2)
                        nc.vector.scalar_tensor_tensor(
                            out=y[:, c, :], in0=u[:, c, cols(b, L)], scalar=W["D"][:, c:c + 1],
                            in1=p_y[:, c, :, :].rearrange("q a n -> q (a n)"), op0=ALU.mult, op1=ALU.add).then_inc(yu_done, 1)
                    for c in range(2):
                        dve.wait_ge(yu_done, 2 * b + c + 3)
                        nc.vector.tensor_tensor(y[:, c, :], y[:, c, :], zs[:, c, cols(b, L)], ALU.mult).then_inc(y_done, 1)
                    for k in range(2):
                        dve.wait_ge(o_done, 2 * b + k + 3)
                        dve.wait_ge(upd_step, 4 * b + k + 3)
                        nc.vector.tensor_scalar(upd[:, k, :], p_o[:, k, :], W["out_b"], mod[:, 2, bass.ds(b, 1)], ALU.add,
                                                ALU.mult).then_inc(upd_step, 1)
                    for k in range(2):
                        dve.wait_ge(upd_step, 4 * b + k + 5)
                        nc.vector.tensor_tensor(x[:, cols(2 * b + k)], x[:, cols(2 * b + k)], upd[:, k, :],
                                                ALU.add).then_inc(upd_step, 1)

            @block.tensor
            def _(pe):
                nc.tensor.sem_inc(sum_done, NT)
                nc.tensor.sem_inc(o_done, 2)
                with nc.tensor.Fori(0, NB) as b:
                    for k, (q, c, n, i) in enumerate(units):
                        pe.wait_ge(st_done, U * b + k + NI + 1)
                        if n == 0:
                            pe.wait_ge(yu_done, 2 * b + 2)
                        for a in range(2):
                            last = nc.tensor.matmul(p_y[:, c, a, :], ident, st[:, k % NT, a * TILE:(a + 1) * TILE],
                                                    start=n == 0, stop=n == NS - 1)
                        last.then_inc(sum_done, 1)
                    for a in range(2):
                        pe.wait_ge(y_done, 2 * b + 2)
                        pe.wait_ge(upd_step, 4 * b + a + 1)
                        for c in range(2):
                            last = nc.tensor.matmul(p_o[:, a, :], W["out_w"][:, c, :], y[:, c, a * TILE:(a + 1) * TILE],
                                                    start=c == 0, stop=c == 1)
                        last.then_inc(o_done, 1)


def moe_gate(nc, tag, h, gate_w, gate_b, ident, w_dram):
    E, NT = 8, T // P
    with Pool_(nc, tag) as m:
        hs = m.sb("hs", [P, 2, TILE])
        lg = m.sb("lg", [P, NT, E + 1])
        top = m.sb("top", [P, NT])
        ex = m.sb("ex", [P, NT, E])
        ez = m.sb("ez", [P, NT])
        den = m.sb("den", [P, NT])
        rden = m.sb("rden", [P, NT])
        thr = m.sb("thr", [P, NT])
        gate = m.sb("gate", [P, NT, E])
        w = m.sb("w", [P, PAIRS, E, NT // PAIRS])
        wT = m.sb("wT", [64, PAIRS, P])
        p_lg = m.ps("p_lg", [P, 2, 512])
        p_wT = m.ps("p_wT", [64, PAIRS, P])
        hs_done = m.sem("hs_done")
        lg_mm = m.sem("lg_mm")
        lg_done = m.sem("lg_done")
        step = m.sem("step")
        exp_done = m.sem("exp_done")
        wT_mm = m.sem("wT_mm")
        wT_done = m.sem("wT_done")
        stored = m.sem("stored")
        with nc.Block() as block:
            @block.scalar
            def _(act):
                with nc.scalar.Fori(0, PAIRS) as p:
                    for j in range(2):
                        act.wait_ge(lg_mm, 2 * p + j + 1)
                        nc.scalar.activation(hs[:, j, :], h[:, cols(2 * p + j)], ACT.Copy).then_inc(hs_done, 1)
                act.wait_ge(step, 2)
                nc.scalar.activation(ex[:, :, :], gate[:, :, :], ACT.Exp).then_inc(exp_done, 1)
                nc.scalar.activation(ez[:, :], lg[:, :, E], ACT.Exp, scale=-1.0).then_inc(exp_done, 1)

            @block.tensor
            def _(pe):
                nc.tensor.sem_inc(lg_mm, 2)
                with nc.tensor.Fori(0, PAIRS) as p:
                    for j in range(2):
                        pe.wait_ge(hs_done, 2 * p + j + 1)
                        pe.wait_ge(lg_done, 2 * p + j + 1)
                        for q in range(4):
                            last = nc.tensor.matmul(p_lg[:, j, q * 16:q * 16 + E + 1], hs[:, j, q * P:(q + 1) * P],
                                                    gate_w, start=True, stop=True)
                        last.then_inc(lg_mm, 1)
                pe.wait_ge(step, 12)
                for p in range(PAIRS):
                    last = nc.tensor.transpose(p_wT[:, p, :], w[:, p, :, :].rearrange("q e t -> q (e t)"), ident)
                last.then_inc(wT_mm, 1)

            @block.vector
            def _(dve):
                nc.vector.sem_inc(lg_done, 2)
                with nc.vector.Fori(0, PAIRS) as p:
                    for j in range(2):
                        dve.wait_ge(lg_mm, 2 * p + j + 3)
                        nc.vector.tensor_tensor(
                            lg[:, bass.ds(8 * p + 4 * j, 4), :],
                            p_lg[:, j, 0:64].rearrange("q (a e) -> q a e", e=16)[:, :, 0:E + 1],
                            gate_b.unsqueeze(1).to_broadcast([P, 4, E + 1]), ALU.add).then_inc(lg_done, 1)
                n = [0]

                def then(ins):
                    n[0] += 1
                    ins.then_inc(step, 1)
                    dve.wait_ge(step, n[0])

                def over_e(v):
                    return v.unsqueeze(2).to_broadcast([P, NT, E])

                dve.wait_ge(lg_done, 2 * PAIRS + 2)
                then(nc.vector.tensor_reduce(top[:, :], lg[:, :, 0:E], AX_X, ALU.max))
                then(nc.vector.tensor_tensor(gate[:, :, :], lg[:, :, 0:E], over_e(top[:, :]), ALU.subtract))
                dve.wait_ge(exp_done, 2)
                then(nc.vector.tensor_reduce(den[:, :], ex[:, :, :], AX_X, ALU.add))
                then(nc.vector.reciprocal(rden[:, :], den[:, :]))
                then(nc.vector.tensor_tensor(gate[:, :, :], ex[:, :, :], over_e(rden[:, :]), ALU.mult))
                then(nc.vector.tensor_scalar(ez[:, :], ez[:, :], 1.0, None, ALU.add))
                then(nc.vector.reciprocal(thr[:, :], ez[:, :]))
                then(nc.vector.tensor_scalar(thr[:, :], thr[:, :], 0.125, None, ALU.mult))
                then(nc.vector.tensor_tensor(gate[:, :, :], gate[:, :, :], over_e(thr[:, :]), ALU.subtract))
                then(nc.vector.tensor_scalar(gate[:, :, :], gate[:, :, :], 0.0, None, ALU.max))
                then(nc.vector.tensor_reduce(den[:, :], gate[:, :, :], AX_X, ALU.add))
                then2 = nc.vector.scalar_tensor_tensor(out=top[:, :], in0=den[:, :], scalar=0.0, in1=den[:, :],
                                                       op0=ALU.is_equal, op1=ALU.add)
                then2.then_inc(wT_done, 1)
                dve.wait_ge(wT_done, 1)
                nc.vector.reciprocal(rden[:, :], top[:, :]).then_inc(wT_done, 1)
                dve.wait_ge(wT_done, 2)
                then(nc.vector.tensor_tensor(
                    w[:, :, :, :].rearrange("q p e t -> q p t e"),
                    gate[:, :, :].rearrange("q (p t) e -> q p t e", p=PAIRS),
                    rden[:, :].rearrange("q (p t) -> q p t", p=PAIRS).unsqueeze(3).to_broadcast([P, PAIRS, NT // PAIRS, E]),
                    ALU.mult))
                dve.wait_ge(wT_mm, 1)
                nc.vector.tensor_copy(wT[:, :, :], p_wT[:, :, :]).then_inc(wT_done, 1)

            @block.sync
            def _(sp):
                sp.wait_ge(wT_done, 3)
                sp.dma_start(w_dram.rearrange("p (e t) k -> (e t) p k", e=E), wT[:, :, :]).then_inc(stored, 16)
                sp.wait_ge(stored, 16)


def moe(nc, tag, x, h, w1, b1, w2, b2, weights_loaded, n_loads, w_dram, mod):
    E, K = 8, 4
    U = 2 * E
    with Pool_(nc, tag) as m:
        wb = m.sb("wb", [P, 2, E, TILE])
        wT = m.sb("wT", [E, 2, TILE])
        hid = m.sb("hid", [P, 2, K, TILE])
        part = m.sb("part", [P, 2, TILE])
        b2w = m.sb("b2w", [P, 2, TILE])
        acc = m.sb("acc", [P, 2, TILE])
        p_up = m.ps("p_up", [P, K, 512])
        p_dn = m.ps("p_dn", [P, 2, 512])
        p_b = m.ps("p_b", [P, 512])
        w_in = [m.sem(f"w_in{j}") for j in range(2)]
        up_done = m.sem("up_done")
        gelu_done = m.sem("gelu_done")
        dn_done = m.sem("dn_done")
        mul_done = m.sem("mul_done")
        add_done = m.sem("add_done")
        b_done = m.sem("b_done")
        b2w_done = m.sem("b2w_done")
        x_done = m.sem("x_done")
        with nc.Block() as block:
            @block.sync
            def _(sp):
                with nc.sync.Fori(0, PAIRS) as p:
                    for j in range(2):
                        sp.wait_ge(x_done, 2 * p + j + 1)
                        src = w_dram[bass.ds(p, 1), :, :].rearrange("p (e t) k -> (p e) (t k)", e=E)[:, j * TILE:(j + 1) * TILE]
                        sp.dma_start(wb[:, j, :, :], src.partition_broadcast(P)).then_inc(w_in[j], 16)
                        sp.dma_start(wT[:, j, :], src).then_inc(w_in[j], 16)

            @block.tensor
            def _(pe):
                nc.tensor.sem_inc(dn_done, 2)
                pe.wait_ge(weights_loaded, n_loads)

                def up(p, k):
                    j, e = divmod(k, E)
                    for i in range(K):
                        pe.wait_ge(gelu_done, 4 * U * p + 4 * k + i + 1)
                        nc.tensor.matmul(p_up[:, i, :], w1[:, e, i * P:(i + 1) * P], h[:, cols(2 * p + j)],
                                         start=True, stop=True).then_inc(up_done, 1)

                def down(p, k):
                    j, e = divmod(k, E)
                    if e == 0:
                        pe.wait_ge(w_in[j], 32 * p + 32)
                        pe.wait_ge(b2w_done, 2 * p + j + 1)
                        nc.tensor.matmul(p_b[:, :], b2, wT[:, j, :], start=True, stop=True).then_inc(b_done, 1)
                    pe.wait_ge(mul_done, U * p + k + 1)
                    for i in range(K):
                        pe.wait_ge(gelu_done, 4 * U * p + 4 * k + i + 5)
                        last = nc.tensor.matmul(p_dn[:, k % 2, :], w2[:, e, i, :], hid[:, k % 2, i, :],
                                                start=i == 0, stop=i == K - 1)
                    last.then_inc(dn_done, 1)

                with nc.tensor.Fori(0, PAIRS) as p:
                    up(p, 0)
                    for k in range(U):
                        if k + 1 < U:
                            up(p, k + 1)
                        down(p, k)

            @block.scalar
            def _(act):
                nc.scalar.preload_act_table(ACT.Gelu_apprx_tanh)
                nc.scalar.sem_inc(gelu_done, 4)
                nc.scalar.sem_inc(b2w_done, 1)
                with nc.scalar.Fori(0, PAIRS) as p:
                    for k in range(U):
                        j, e = divmod(k, E)
                        act.wait_ge(dn_done, U * p + k + 1)
                        for i in range(K):
                            act.wait_ge(up_done, 4 * U * p + 4 * k + i + 1)
                            nc.scalar.activation(hid[:, k % 2, i, :], p_up[:, i, :], ACT.Gelu_apprx_tanh,
                                                 bias=b1[:, e * K + i:e * K + i + 1]).then_inc(gelu_done, 1)
                        if e == 0:
                            act.wait_ge(b_done, 2 * p + j + 1)
                            act.wait_ge(x_done, 2 * p + j + 1)
                            nc.scalar.activation(b2w[:, j, :], p_b[:, :], ACT.Copy).then_inc(b2w_done, 1)

            @block.vector
            def _(dve):
                nc.vector.sem_inc(mul_done, 2)
                nc.vector.sem_inc(x_done, 2)
                with nc.vector.Fori(0, PAIRS) as p:
                    for k in range(U):
                        j, e = divmod(k, E)
                        dve.wait_ge(w_in[j], 32 * p + 32)
                        dve.wait_ge(dn_done, U * p + k + 3)
                        dve.wait_ge(add_done, U * p + k + 1)
                        nc.vector.tensor_tensor(part[:, k % 2, :], p_dn[:, k % 2, :], wb[:, j, e, :],
                                                ALU.mult).then_inc(mul_done, 1)
                        if e == E - 1:
                            dve.wait_ge(add_done, U * p + k + 3)
                            nc.vector.scalar_tensor_tensor(
                                out=x[:, cols(2 * p + j)], in0=acc[:, j, :], scalar=mod[:, 5, bass.ds(p, 1)],
                                in1=x[:, cols(2 * p + j)], op0=ALU.mult, op1=ALU.add).then_inc(x_done, 1)

            @block.gpsimd
            def _(pool):
                nc.gpsimd.sem_inc(add_done, 2)
                with nc.gpsimd.Fori(0, PAIRS) as p:
                    for k in range(U):
                        j, e = divmod(k, E)
                        pool.wait_ge(mul_done, U * p + k + 3)
                        pool.wait_ge(add_done, U * p + k + 2)
                        if e == 0:
                            pool.wait_ge(b2w_done, 2 * p + j + 2)
                            pool.wait_ge(x_done, 2 * p + j + 1)
                        nc.gpsimd.tensor_tensor(acc[:, j, :], b2w[:, j, :] if e == 0 else acc[:, j, :], part[:, k % 2, :],
                                                ALU.add).then_inc(add_done, 1)


HB = 16
DH = P // HB
VW = HB * (DH + 1)
QT = P
NG4 = 4
NQ = T // QT
MASKED = -1e30


def rope_qkv(nc, tag, h, qkv_w, rope, q, k, v, vg, hm):
    with Pool_(nc, tag) as m:
        hs = m.sb("hs", [P, 2, TILE])
        hg = m.sb("hg", [P, HB // 2, NG4])
        turned = m.sb("turned", [P, 4, TILE])
        p_qk = m.ps("p_qk", [P, 4, 512])
        p_v = m.ps("p_v", [P, 4, P])
        p_g = m.ps("p_g", [32, P])
        pads = m.sem("pads")
        hs_done = m.sem("hs_done")
        hg_done = m.sem("hg_done")
        qk_mm = m.sem("qk_mm")
        v_mm = m.sem("v_mm")
        g_mm = m.sem("g_mm")
        turned_done = m.sem("turned_done")
        sum_done = m.sem("sum_done")
        v_done = m.sem("v_done")
        g_done = m.sem("g_done")
        with nc.Block() as block:
            @block.tensor
            def _(pe):
                nc.tensor.sem_inc(v_mm, 2)
                nc.tensor.sem_inc(g_mm, 1)
                with nc.tensor.Fori(0, PAIRS) as p:
                    for j in range(2):
                        t = 2 * p + j
                        for r in range(4):
                            pe.wait_ge(turned_done, 4 * t + r + 1)
                            nc.tensor.matmul(p_qk[:, r, :], qkv_w[:, r * P:(r + 1) * P], h[:, cols(t)],
                                             start=True, stop=True).then_inc(qk_mm, 1)
                        pe.wait_ge(hs_done, t + 1)
                        pe.wait_ge(v_done, t + 1)
                        for a in range(4):
                            last = nc.tensor.matmul(p_v[:, a, :], hs[:, j, a * P:(a + 1) * P], qkv_w[:, 4 * P:5 * P],
                                                    start=True, stop=True)
                        last.then_inc(v_mm, 1)
                        if j == 0:
                            pe.wait_ge(hg_done, p + 1)
                            pe.wait_ge(g_done, p + 1)
                            nc.tensor.matmul(p_g[:, :], hg[:, :, :].rearrange("q h j -> q (h j)"), qkv_w[:, 4 * P:5 * P],
                                             start=True, stop=True).then_inc(g_mm, 1)

            @block.scalar
            def _(act):
                nc.scalar.sem_inc(v_done, 1)
                act.wait_ge(pads, 5)
                with nc.scalar.Fori(0, PAIRS) as p:
                    for j in range(2):
                        t = 2 * p + j
                        act.wait_ge(v_mm, t + 1)
                        nc.scalar.activation(hs[:, j, :], h[:, cols(t)], ACT.Copy).then_inc(hs_done, 1)
                        if j == 0:
                            act.wait_ge(hs_done, t + 1)
                            act.wait_ge(g_mm, p + 1)
                            nc.scalar.activation(hg[:, :, :], hs[:, 0, 0:NG4].unsqueeze(1).to_broadcast([P, HB // 2, NG4]),
                                                 ACT.Copy).then_inc(hg_done, 1)
                        act.wait_ge(v_mm, t + 3)
                        nc.scalar.activation(
                            v[:, bass.ds(4 * t + 1, 4), :].rearrange("q t (h d) -> q (t h) d", d=DH + 1)[:, :, 0:DH],
                            p_v[:, :, :].rearrange("q t (h d) -> q (t h) d", d=DH), ACT.Copy).then_inc(v_done, 1)

            @block.vector
            def _(dve):
                nc.vector.memset(k[:, 0:QT], 0.0).then_inc(pads, 1)
                nc.vector.memset(k[:, QT + T:2 * QT + T], 0.0).then_inc(pads, 1)
                nc.vector.memset(q[:, T:T + QT], 0.0).then_inc(pads, 1)
                nc.vector.memset(v[:, :, :], 1.0).then_inc(pads, 1)
                nc.vector.memset(turned[:, 0, 0:1], 0.0).then_inc(pads, 1)
                dve.wait_ge(pads, 5)
                nc.vector.sem_inc(turned_done, 4)
                nc.vector.sem_inc(g_done, 1)
                with nc.vector.Fori(0, PAIRS) as p:
                    for j in range(2):
                        t = 2 * p + j
                        for r in range(4):
                            dve.wait_ge(qk_mm, 4 * t + r + 1)
                            dve.wait_ge(sum_done, 2 * t + r // 2 + 1)
                            nc.vector.tensor_tensor(turned[:, r, :], p_qk[:, r, :], rope[:, r, j * TILE:(j + 1) * TILE],
                                                    ALU.mult).then_inc(turned_done, 1)
                        if j == 0:
                            dve.wait_ge(g_mm, p + 2)
                            for a in range(2):
                                last = nc.vector.tensor_tensor(
                                    vg[:, a, bass.ds(p, 1), :].rearrange("q b (h d) -> q (b h) d", d=DH + 1)[:, :, 0:DH],
                                    p_g[:, 8 * a * DH:8 * (a + 1) * DH].rearrange("q (h d) -> q h d", d=DH),
                                    hm.unsqueeze(2).to_broadcast([32, 8, DH]), ALU.mult)
                            last.then_inc(g_done, 1)

            @block.gpsimd
            def _(pool):
                nc.gpsimd.sem_inc(sum_done, 2)
                pool.wait_ge(pads, 5)
                with nc.gpsimd.Fori(0, PAIRS) as p:
                    for j in range(2):
                        t = 2 * p + j
                        for r, dst in ((0, q[:, cols(t)]), (1, k[:, bass.ds(QT + t * TILE, TILE)])):
                            pool.wait_ge(turned_done, 4 * t + 2 * r + 6)
                            nc.gpsimd.tensor_tensor(dst, turned[:, 2 * r, :], turned[:, 2 * r + 1, :],
                                                    ALU.add).then_inc(sum_done, 1)


def band_attention(nc, tag, q, k, v, vg, head_mask, masks, ident, oT):
    KW = 2 * QT + NG4
    with Pool_(nc, tag) as m:
        qm = m.sb("qm", [P, HB, QT])
        ms = m.sb("ms", [P, 4, KW])
        nmx = m.sb("nmx", [P, HB])
        pr = m.sb("pr", [P, HB, KW])
        prT = m.sb("prT", [P, 2, 2, 2 * QT])
        pgT = m.sb("pgT", [32, 2, QT])
        rs = m.sb("rs", [P, HB])
        on = m.sb("on", [P, HB, DH])
        p_s = m.ps("p_s", [P, 2, 512])
        p_t = m.ps("p_t", [P, 2, 512])
        p_g = m.ps("p_g", [32, 512])
        p_o = m.ps("p_o", [P, 512])
        p_ot = m.ps("p_ot", [P, 512])
        pg = m.sb("pg", [P, 2, HB // 2, NG4])
        qm_done = m.sem("qm_done")
        pg_done = m.sem("pg_done")
        s_done = m.sem("s_done")
        max_done = m.sem("max_done")
        exp_done = m.sem("exp_done")
        t_done = m.sem("t_done")
        ev_done = [m.sem("ev_act"), m.sem("ev_dve")]
        av_done = m.sem("av_done")
        gT_done = m.sem("gT_done")
        gc_done = m.sem("gc_done")
        ag_done = m.sem("ag_done")
        rs_done = m.sem("rs_done")
        on_done = m.sem("on_done")
        ot_done = m.sem("ot_done")
        tick = m.sem("tick")
        oc_done = m.sem("oc_done")
        H2 = HB // 2

        def tiles(eng, body):
            with eng.Fori(0, NB) as b:
                body(b, 8 * b, 0, b)
                body(b, 8 * b + 1, 1, b)
                with eng.Fori(2, 7) as i:
                    body(b, 8 * b + i, 2, b)
                body(b, 8 * b + 7, 2, b + 1)

        with nc.Block() as block:
            @block.gpsimd
            def _(pool):
                def mask_queries(g, a):
                    pool.wait_ge(s_done, HB * g + H2 * a + H2)
                    nc.gpsimd.sem_inc(tick, 1)
                    nc.gpsimd.tensor_tensor(
                        qm[:, H2 * a:H2 * (a + 1), :], q[:, bass.ds(g * QT, QT)].unsqueeze(1).to_broadcast([P, H2, QT]),
                        head_mask[:, H2 * a:H2 * (a + 1)].unsqueeze(2).to_broadcast([P, H2, QT]),
                        ALU.mult).then_inc(qm_done, 1)

                nc.gpsimd.sem_inc(pg_done, 2)
                mask_queries(0, 0)
                mask_queries(0, 1)
                with nc.gpsimd.Fori(0, NQ) as g:
                    for a in range(2):
                        mask_queries(g + 1, a)
                        pool.wait_ge(exp_done, HB * g + H2 * a + H2 + 4)
                        pool.wait_ge(gT_done, 2 * g + a + 1)
                        nc.gpsimd.sem_inc(tick, 1)
                        nc.gpsimd.tensor_copy(pg[:, a, :, :], pr[:, H2 * a:H2 * (a + 1), 2 * QT:KW]).then_inc(pg_done, 1)

            @block.tensor
            def _(pe):
                nc.tensor.sem_inc(s_done, HB)
                nc.tensor.sem_inc(t_done, HB)
                nc.tensor.sem_inc(av_done, 4)
                nc.tensor.sem_inc(gT_done, 2)
                nc.tensor.sem_inc(ag_done, 2)

                def scores(g, b, hd):
                    if hd % H2 == 0:
                        pe.wait_ge(qm_done, 2 * g + hd // H2 + 1)
                    pe.wait_ge(max_done, HB * g + hd + 1)
                    nc.tensor.matmul(p_s[:, hd % 2, 0:2 * QT], qm[:, hd, :], k[:, bass.ds(g * QT, 2 * QT)],
                                     start=True, stop=True)
                    nc.tensor.matmul(p_s[:, hd % 2, 2 * QT:KW], qm[:, hd, :], k[:, bass.ds(QT + b * L, NG4)],
                                     start=True, stop=True).then_inc(s_done, 1)

                def turn(g, hd):
                    pe.wait_ge(exp_done, HB * g + hd + 5)
                    if hd % 2 == 0:
                        pe.wait_ge(ev_done[hd // 2 % 2], 4 * g + hd // 4 + 1)
                    for a in range(2):
                        last = nc.tensor.transpose(p_t[:, hd // 2 % 2, (2 * (hd % 2) + a) * QT:(2 * (hd % 2) + a + 1) * QT],
                                                   pr[:, hd, a * QT:(a + 1) * QT], ident)
                    last.then_inc(t_done, 1)

                def values(g, hd):
                    if hd % 2 == 0:
                        pe.wait_ge(ev_done[hd // 2 % 2], 4 * g + hd // 4 + 2)
                    if hd == 0:
                        pe.wait_ge(on_done, g + 1)
                    for a in range(2):
                        last = nc.tensor.matmul(p_o[:, hd * (DH + 1):(hd + 1) * (DH + 1)],
                                                prT[:, hd // 2 % 2, hd % 2, a * QT:(a + 1) * QT],
                                                v[:, bass.ds(g + a, 1), hd * (DH + 1):(hd + 1) * (DH + 1)].rearrange(
                                                    "q t d -> q (t d)"),
                                                start=hd == 0 and a == 0, stop=False, skip_group_check=True)
                    last.then_inc(av_done, 1)

                def turn_global(g, a):
                    pe.wait_ge(pg_done, 2 * g + a + 3)
                    pe.wait_ge(gc_done, 2 * g + a + 1)
                    nc.tensor.transpose(p_g[:, 0:QT], pg[:, a, :, :].rearrange("q h j -> q (h j)"), ident
                                        ).then_inc(gT_done, 1)

                def values_global(g, b, a):
                    pe.wait_ge(gc_done, 2 * g + a + 2)
                    nc.tensor.sem_inc(tick, 1)
                    w = H2 * (DH + 1)
                    nc.tensor.matmul(p_o[:, a * w:(a + 1) * w], pgT[:, a, :],
                                     vg[:, a, bass.ds(b, 1), :].rearrange("q b d -> q (b d)"),
                                     start=False, stop=a == 1, skip_group_check=True).then_inc(ag_done, 1)

                def turn_out(g):
                    pe.wait_ge(on_done, g + 1)
                    pe.wait_ge(oc_done, g + 1)
                    nc.tensor.transpose(p_ot[:, 0:QT], on[:, :, :].rearrange("q h d -> q (h d)"), ident).then_inc(ot_done, 1)

                def body(b, g, mask, nb):
                    for s in range(HB):
                        if s + 2 < HB:
                            scores(g, b, s + 2)
                        else:
                            scores(g + 1, nb, s + 2 - HB)
                        turn(g, s)
                        if s >= 3:
                            values(g, s - 3)
                        if s == 2:
                            turn_out(g)
                        if s == 9:
                            turn_global(g, 0)
                        if s == 11:
                            values_global(g, b, 0)
                    turn_global(g, 1)
                    for s in range(HB - 3, HB):
                        values(g, s)
                    values_global(g, b, 1)

                scores(0, 0, 0)
                scores(0, 0, 1)
                tiles(nc.tensor, body)
                turn_out(NQ)

            @block.scalar
            def _(act):
                nc.scalar.preload_act_table_set(LN_EXP)
                nc.scalar.sem_inc(exp_done, 4)
                nc.scalar.sem_inc(ev_done[0], 1)
                nc.scalar.sem_inc(oc_done, 1)

                def leave_out(g):
                    act.wait_ge(ot_done, g + 1)
                    nc.scalar.sem_inc(tick, 1)
                    nc.scalar.activation(oT[:, bass.ds(g * QT, QT)], p_ot[:, 0:QT], ACT.Copy).then_inc(oc_done, 1)

                def body(b, g, mask, nb):
                    for s in range(HB):
                        act.wait_ge(max_done, HB * g + s + 3)
                        act.wait_ge(t_done, HB * g + s + 1)
                        if s % H2 == 0:
                            act.wait_ge(pg_done, 2 * g + s // H2 + 1)
                        nc.scalar.activation(pr[:, s, :], ms[:, s % 4, :], ACT.Exp, bias=nmx[:, s:s + 1],
                                             scale=-1.0).then_inc(exp_done, 1)
                        if s % 4 == 2:
                            evacuate(g, s // 2 - 1)
                        if s == 4:
                            leave_out(g)

                def evacuate(g, mm):
                    act.wait_ge(t_done, HB * g + 2 * mm + 2 + HB)
                    act.wait_ge(av_done, HB * g + 2 * mm + 2)
                    nc.scalar.activation(prT[:, 0, :, :].rearrange("q a n -> q (a n)"), p_t[:, 0, :], ACT.Copy
                                         ).then_inc(ev_done[0], 1)

                tiles(nc.scalar, body)
                leave_out(NQ)

            @block.vector
            def _(dve):
                nc.vector.memset(on[:, :, :], 0.0).then_inc(rs_done, 1)
                dve.wait_ge(rs_done, 1)
                nc.vector.sem_inc(max_done, 2)
                nc.vector.sem_inc(ev_done[1], 1)
                nc.vector.sem_inc(gc_done, 1)
                nc.vector.sem_inc(on_done, 1)

                def evacuate(g, mm):
                    dve.wait_ge(t_done, HB * g + 2 * mm + 2 + HB)
                    dve.wait_ge(av_done, HB * g + 2 * mm + 2)
                    nc.vector.tensor_copy(prT[:, 1, :, :].rearrange("q a n -> q (a n)"), p_t[:, 1, :]).then_inc(ev_done[1], 1)

                def leave_global(g, a):
                    dve.wait_ge(gT_done, 2 * g + a + 3)
                    dve.wait_ge(ag_done, 2 * g + a + 1)
                    nc.vector.tensor_copy(pgT[:, a, :], p_g[:, 0:QT]).then_inc(gc_done, 1)

                def body(b, g, mask, nb):
                    for s in range(HB):
                        dve.wait_ge(s_done, HB * g + s + HB + 1)
                        dve.wait_ge(exp_done, HB * g + s + 1)
                        nc.vector.sem_inc(tick, 1)
                        nc.vector.tensor_tensor_reduce(ms[:, s % 4, :], p_s[:, s % 2, 0:KW], masks[:, mask, :], -1.0, 3e38,
                                                       ALU.add, ALU.min, nmx[:, s:s + 1]).then_inc(max_done, 1)
                        if s % 4 == 1 and s > 1:
                            evacuate(g, (s - 3) // 2)
                        if s == 10:
                            leave_global(g, 0)
                    evacuate(g, 7)
                    leave_global(g, 1)
                    dve.wait_ge(av_done, HB * g + HB + 4)
                    dve.wait_ge(ag_done, 2 * g + 4)
                    o = p_o[:, 0:VW].rearrange("q (h d) -> q h d", d=DH + 1)
                    nc.vector.reciprocal(rs[:, :], o[:, :, DH]).then_inc(rs_done, 1)
                    dve.wait_ge(rs_done, g + 2)
                    dve.wait_ge(ot_done, g + 1)
                    nc.vector.tensor_tensor(on[:, :, :], o[:, :, 0:DH], rs[:, :].unsqueeze(2).to_broadcast([P, HB, DH]),
                                            ALU.mult).then_inc(on_done, 1)

                tiles(nc.vector, body)


def out_project(nc, tag, x, oT, off, w, mod_gate):
    with Pool_(nc, tag) as m:
        p_o = m.ps("p_o", [P, 2, 512])
        mm_done = m.sem("mm_done")
        x_done = m.sem("x_done")
        with nc.Block() as block:
            @block.tensor
            def _(pe):
                with nc.tensor.Fori(0, PAIRS) as p:
                    for j in range(2):
                        pe.wait_ge(x_done, 2 * p + j + 1)
                        nc.tensor.matmul(p_o[:, j, :], w, oT[:, bass.ds(off + (2 * p + j) * TILE, TILE)],
                                         start=True, stop=True).then_inc(mm_done, 1)

            @block.vector
            def _(dve):
                nc.vector.sem_inc(x_done, 2)
                with nc.vector.Fori(0, PAIRS) as p:
                    for j in range(2):
                        dve.wait_ge(mm_done, 2 * p + j + 1)
                        xt = x[:, cols(2 * p + j)]
                        nc.vector.scalar_tensor_tensor(out=xt, in0=p_o[:, j, :], scalar=mod_gate(p), in1=xt, op0=ALU.mult,
                                                       op1=ALU.add).then_inc(x_done, 1)


HF = 8
DF = 64
WIN = 64
VF = HF * (DF + 1)
HID = 341
HR = HID - 2 * P
LN_SCALE = 65536.0
TINY = 1e-24


def shifted_copy(nc, tag, y, sh):
    with Pool_(nc, tag) as m:
        done = m.sem("done")
        zero = m.sem("zero")
        with nc.Block() as block:
            @block.scalar
            def _(act):
                for b in range(NB):
                    lo = b * L
                    nc.scalar.activation(sh[0:64, lo:lo + L], y[0:64, lo:lo + L], ACT.Copy).then_inc(done, 1)

            @block.vector
            def _(dve):
                for b in range(NB):
                    lo = b * L
                    nc.vector.memset(sh[64:P, lo:lo + 1], 0.0).then_inc(zero, 1)
                    nc.vector.tensor_copy(sh[64:P, lo + 1:lo + L], y[64:P, lo:lo + L - 1]).then_inc(done, 1)


def local_layer(nc, tag, W, y, sh, tables, blocks, center, mean, ident, head_mask, masks, cols_):
    eps_col, norm_bias = cols_
    NU = 16
    NI = L // QT
    KW = WIN + QT
    with Pool_(nc, tag) as m:
        q = m.sb("q", [P, 4, L])
        k = m.sb("k", [P, 4, QT + L])
        v = m.sb("v", [P, NI + 1, VF])
        oT = m.sb("oT", [P, 4, L])
        hs = m.sb("hs", [P, 2, TILE])
        sq = m.sb("sq", [P, 2, TILE])
        turned = m.sb("turned", [P, 2, 2, TILE])
        ss = m.sb("ss", [P, 2, TILE])
        lns = m.sb("lns", [P, 2, TILE])
        rn = m.sb("rn", [P, 2, TILE])
        tsum = m.sb("tsum", [P, 2, TILE])
        qm = m.sb("qm", [P, HF, QT])
        ms = m.sb("ms", [P, 4, KW])
        nmx = m.sb("nmx", [P, HF])
        pr = m.sb("pr", [P, HF, 2 * QT])
        prT = m.sb("prT", [P, 2, 2, 2 * QT])
        rs = m.sb("rs", [P, 2, 4])
        on = m.sb("on", [P, HF, DF])
        in_q = q[:, :, :].rearrange("q r (j n) -> q r j n", j=2)
        y1, fsq, fln, frs = (in_q[:, n] for n in range(4))
        in_k = k[:, :, QT:QT + L].rearrange("q r (j n) -> q r j n", j=2)
        fh, gg = in_k[:, 0], in_k[:, 1]
        hm = [in_k[:, 2, 0], in_k[:, 2, 1], in_k[:, 3, 0]]
        sh1 = turned[:, :, :, :].rearrange("q a b n -> q (a b n)")
        bank = [m.ps(f"bank{n}", [P, 512]) for n in range(8)]

        init = m.sem("init")
        tick = m.sem("tick")
        pq_done = m.sem("pq_done")
        sq_done = m.sem("sq_done")
        ss_mm = m.sem("ss_mm")
        ss_done = m.sem("ss_done")
        ln_done = m.sem("ln_done")
        rn_done = m.sem("rn_done")
        turned_done = m.sem("turned_done")
        sum_done = m.sem("sum_done")
        qk_done = m.sem("qk_done")
        hs_done = m.sem("hs_done")
        v_mm = m.sem("v_mm")
        v_done = m.sem("v_done")
        qm_done = m.sem("qm_done")
        s_done = m.sem("s_done")
        max_done = m.sem("max_done")
        exp_done = m.sem("exp_done")
        t_done = m.sem("t_done")
        ev_done = [m.sem("ev_act"), m.sem("ev_dve")]
        av_done = m.sem("av_done")
        rs_done = m.sem("rs_done")
        on_done = m.sem("on_done")
        ot_done = m.sem("ot_done")
        oc_done = m.sem("oc_done")
        wo_mm = m.sem("wo_mm")
        y1_done = m.sem("y1_done")
        sh1_done = m.sem("sh1_done")
        cen_mm = m.sem("cen_mm")
        fsq_done = m.sem("fsq_done")
        zero_done = m.sem("zero_done")
        var_mm = m.sem("var_mm")
        fln_done = m.sem("fln_done")
        frs_done = m.sem("frs_done")
        xn_done = m.sem("xn_done")
        fh_done = m.sem("fh_done")
        up_mm = m.sem("up_mm")
        gg_done = m.sem("gg_done")
        hm_done = m.sem("hm_done")
        dn_mm = m.sem("dn_mm")
        y_done = m.sem("y_done")
        sh_done = m.sem("sh_done")
        HW = (P, P, HR)
        units = [(j, r, z) for j in range(2) for z in range(2) for r in range(4)]

        def tiles(eng, b, body):
            body(b, 8 * b, 0, 0)
            with eng.Fori(1, NI - 1) as i:
                body(b, 8 * b + i, i, 1)
            body(b, 8 * b + NI - 1, NI - 1, 2)

        with nc.Block() as block:
            @block.tensor
            def _(pe):
                nc.tensor.sem_inc(ss_mm, 2)
                nc.tensor.sem_inc(v_mm, 8)
                nc.tensor.sem_inc(s_done, HF)
                nc.tensor.sem_inc(t_done, HF)
                nc.tensor.sem_inc(av_done, 4)
                nc.tensor.sem_inc(dn_mm, 6)

                def project(b, n):
                    j, r, z = units[n]
                    pe.wait_ge(sq_done, NU * b + n + 1)
                    pe.wait_ge(turned_done, NU * b + n + 1)
                    if n == 0:
                        pe.wait_ge(hm_done, 6 * b + 1)
                        pe.wait_ge(sh_done, 2 * b + 2)
                    for a in range(2):
                        last = nc.tensor.matmul(bank[2 * a + n % 2][:, :], W["qk"][:, 2 * z + a, r * P:(r + 1) * P],
                                                sh[:, cols(2 * b + j)], start=True, stop=True)
                    last.then_inc(pq_done, 1)

                def squares(b, n):
                    pe.wait_ge(sq_done, NU * b + n + 3)
                    pe.wait_ge(ss_done, NU * b + n + 1)
                    nc.tensor.matmul(bank[4 + n % 2][:, :], blocks, sq[:, n % 2, :], start=True, stop=True).then_inc(ss_mm, 1)

                def scores(g, i, hd):
                    if hd % 4 == 0:
                        pe.wait_ge(qm_done, 2 * g + hd // 4 + 1)
                    pe.wait_ge(max_done, HF * g + hd + 1)
                    nc.tensor.matmul(bank[hd % 2][:, 0:KW], qm[:, hd, :], k[:, hd // 2, bass.ds(i * QT + QT - WIN, KW)],
                                     start=True, stop=True).then_inc(s_done, 1)

                def turn(g, hd):
                    pe.wait_ge(exp_done, HF * g + hd + 5)
                    if hd % 2 == 0:
                        pe.wait_ge(ev_done[hd // 2 % 2], 2 * g + hd // 4 + 1)
                    for a in range(2):
                        last = nc.tensor.transpose(bank[2 + hd // 2 % 2][:, (2 * (hd % 2) + a) * QT:(2 * (hd % 2) + a + 1) * QT],
                                                   pr[:, hd, a * QT:(a + 1) * QT], ident)
                    last.then_inc(t_done, 1)

                def values(g, i, hd):
                    if hd % 2 == 0:
                        pe.wait_ge(ev_done[hd // 2 % 2], 2 * g + hd // 4 + 2)
                    if hd == 0:
                        pe.wait_ge(on_done, g + 1)
                    for a in range(2):
                        last = nc.tensor.matmul(bank[4 + hd // 4][:, hd % 4 * (DF + 1):(hd % 4 + 1) * (DF + 1)],
                                                prT[:, hd // 2 % 2, hd % 2, a * QT:(a + 1) * QT],
                                                v[:, bass.ds(i + a, 1), hd * (DF + 1):(hd + 1) * (DF + 1)].rearrange(
                                                    "q t d -> q (t d)"),
                                                start=hd % 4 == 0 and a == 0, stop=hd % 4 == 3 and a == 1,
                                                skip_group_check=True)
                    last.then_inc(av_done, 1)

                def turn_out(g):
                    pe.wait_ge(on_done, g + 2)
                    pe.wait_ge(oc_done, g + 1)
                    for r in range(4):
                        last = nc.tensor.transpose(bank[6][:, r * QT:(r + 1) * QT],
                                                   on[:, 2 * r:2 * r + 2, :].rearrange("q h d -> q (h d)"), ident)
                    last.then_inc(ot_done, 1)

                def body(b, g, i, where):
                    for s in range(HF):
                        if s + 2 < HF:
                            scores(g, i, s + 2)
                        elif where < 2:
                            scores(g + 1, i + 1, s + 2 - HF)
                        turn(g, s)
                        if s >= 3:
                            values(g, i, s - 3)
                        if s == 2 and where > 0:
                            turn_out(g - 1)
                    for s in range(HF - 3, HF):
                        values(g, i, s)
                    if where == 2:
                        turn_out(g)

                with nc.tensor.Fori(0, NB) as b:
                    project(b, 0)
                    for n in range(NU):
                        if n + 1 < NU:
                            project(b, n + 1)
                        squares(b, n)
                    for t in range(NI):
                        if t % 4 == 0:
                            pe.wait_ge(hs_done, 2 * b + t // 4 + 1)
                        pe.wait_ge(v_done, NI * b + t + 1)
                        nc.tensor.matmul(bank[6 + t % 2][:, :], hs[:, t // 4, t % 4 * P:(t % 4 + 1) * P], W["v"][:, :],
                                         start=True, stop=True).then_inc(v_mm, 1)
                    pe.wait_ge(qk_done, NU * b + NU + 2)
                    pe.wait_ge(v_done, NI * b + NI + 2)
                    scores(8 * b, 0, 0)
                    scores(8 * b, 0, 1)
                    tiles(nc.tensor, b, body)
                    for j in range(2):
                        if j == 0:
                            pe.wait_ge(oc_done, NI * b + 4 + 1)
                        else:
                            pe.wait_ge(oc_done, NI * b + NI + 1)
                        for r in range(4):
                            last = nc.tensor.matmul(bank[7 - j][:, :], W["wo"][:, r, :],
                                                    oT[:, r, j * TILE:(j + 1) * TILE], start=r == 0, stop=r == 3)
                        last.then_inc(wo_mm, 1)
                    for j in range(2):
                        pe.wait_ge(sh1_done, 4 * b + 2 * j + 2)
                        pe.wait_ge(zero_done, b + 1)
                        nc.tensor.matmul(bank[4 + j][:, :], center, sh1[:, j * TILE:(j + 1) * TILE],
                                         start=True, stop=True).then_inc(cen_mm, 1)
                    for j in range(2):
                        pe.wait_ge(fsq_done, 2 * b + j + 1)
                        nc.tensor.matmul(bank[7 - j][:, :], mean, fsq[:, j, :], start=True, stop=True).then_inc(var_mm, 1)
                    for j in range(2):
                        pe.wait_ge(fh_done, 2 * b + j + 1)

                        def down(r):
                            pe.wait_ge(hm_done, 6 * b + 3 * j + r + 2)
                            nc.tensor.matmul(bank[4 + j][:, :], W["w2"][0:HW[r], r, :], hm[r][0:HW[r], :], start=r == 0,
                                             stop=r == 2).then_inc(dn_mm, 1)

                        for r in range(3):
                            if 3 * j + r >= 2:
                                pe.wait_ge(hm_done, 6 * b + 3 * j + r)
                            n = (3 * j + r) % 2
                            for a in range(2):
                                last = nc.tensor.matmul(bank[2 * n + a][0:HW[r], :],
                                                        W["w1"][:, a * HID + r * P:a * HID + r * P + HW[r]], fh[:, j, :],
                                                        start=True, stop=True)
                            last.then_inc(up_mm, 1)
                            if r > 0:
                                down(r - 1)
                        down(2)

            @block.scalar
            def _(act):
                nc.scalar.sem_inc(sq_done, 2)
                nc.scalar.sem_inc(ln_done, 2)
                nc.scalar.sem_inc(rn_done, 2)
                nc.scalar.sem_inc(v_done, 2)
                nc.scalar.sem_inc(exp_done, 4)
                nc.scalar.sem_inc(ev_done[0], 1)
                nc.scalar.sem_inc(oc_done, 1)
                nc.scalar.sem_inc(sh_done, 2)
                act.wait_ge(init, 4)

                def square(b, n):
                    act.wait_ge(pq_done, NU * b + n + 1)
                    act.wait_ge(ss_mm, NU * b + n + 1)
                    nc.scalar.activation(sq[:, n % 2, :], bank[n % 2][:, :], ACT.Square).then_inc(sq_done, 1)

                def inverse_norm(b, n):
                    act.wait_ge(ss_done, NU * b + n + 3)
                    act.wait_ge(rn_done, NU * b + n + 1)
                    nc.scalar.activation(lns[:, n % 2, :], ss[:, n % 2, :], ACT.Ln, scale=LN_SCALE).then_inc(ln_done, 1)
                    act.wait_ge(ln_done, NU * b + n + 3)
                    act.wait_ge(qk_done, NU * b + n + 1)
                    nc.scalar.activation(rn[:, n % 2, :], lns[:, n % 2, :], ACT.Exp, scale=-0.5,
                                         bias=norm_bias).then_inc(rn_done, 1)

                def evacuate(g, mm):
                    act.wait_ge(t_done, HF * g + 2 * mm + 2 + HF)
                    act.wait_ge(av_done, HF * g + 2 * mm + 2)
                    nc.scalar.activation(prT[:, 0, :, :].rearrange("q a n -> q (a n)"), bank[2][:, :], ACT.Copy
                                         ).then_inc(ev_done[0], 1)

                def leave_out(g, i):
                    act.wait_ge(ot_done, g + 1)
                    nc.scalar.sem_inc(tick, 1)
                    nc.scalar.activation(oT[:, :, bass.ds(i * QT, QT)],
                                         bank[6][:, :].rearrange("q (r n) -> q r n", r=4), ACT.Copy).then_inc(oc_done, 1)

                def body(b, g, i, where):
                    for s in range(HF):
                        act.wait_ge(max_done, HF * g + s + 3)
                        act.wait_ge(t_done, HF * g + s + 1)
                        nc.scalar.activation(pr[:, s, QT - WIN:2 * QT], ms[:, s % 4, :], ACT.Exp, bias=nmx[:, s:s + 1],
                                             scale=-1.0).then_inc(exp_done, 1)
                        if s % 4 == 2:
                            evacuate(g, s // 2 - 1)
                        if s == 4 and where > 0:
                            leave_out(g - 1, i - 1)
                    if where == 2:
                        leave_out(g, i)

                with nc.scalar.Fori(0, NB) as b:
                    nc.scalar.preload_act_table_set(LN_EXP)
                    for j in range(2):
                        act.wait_ge(v_mm, NI * b + 4 * j + 4)
                        act.wait_ge(sh_done, 2 * b + 2)
                        nc.scalar.sem_inc(tick, 1)
                        nc.scalar.activation(hs[:, j, :], sh[:, cols(2 * b + j)], ACT.Copy).then_inc(hs_done, 1)
                    square(b, 0)
                    for n in range(NU):
                        if n + 1 < NU:
                            square(b, n + 1)
                        inverse_norm(b, n)
                    for t in range(NI):
                        act.wait_ge(v_mm, NI * b + t + NI + 1)
                        nc.scalar.activation(v[:, t + 1, :].rearrange("q (h d) -> q h d", d=DF + 1)[:, :, 0:DF],
                                             bank[6 + t % 2][:, :].rearrange("q (h d) -> q h d", d=DF),
                                             ACT.Copy).then_inc(v_done, 1)
                    tiles(nc.scalar, b, body)
                    for j in range(2):
                        act.wait_ge(y1_done, 2 * b + j + 1)
                        act.wait_ge(sh_done, 2 * b + 2)
                        nc.scalar.activation(sh1[0:64, j * TILE:(j + 1) * TILE], y1[0:64, j, :], ACT.Copy).then_inc(sh1_done, 1)
                        nc.scalar.activation(sh1[64:P, j * TILE + 1:(j + 1) * TILE + 1], y1[64:P, j, :],
                                             ACT.Copy).then_inc(sh1_done, 1)
                    for j in range(2):
                        act.wait_ge(cen_mm, 2 * b + j + 1)
                        nc.scalar.activation(fsq[:, j, :], bank[4 + j][:, :], ACT.Square).then_inc(fsq_done, 1)
                    for j in range(2):
                        act.wait_ge(var_mm, 2 * b + j + 1)
                        nc.scalar.activation(fln[:, j, :], bank[7 - j][:, :], ACT.Ln, bias=eps_col).then_inc(fln_done, 1)
                    for j in range(2):
                        act.wait_ge(fln_done, 2 * b + j + 1)
                        nc.scalar.activation(frs[:, j, :], fln[:, j, :], ACT.Exp, scale=-0.5).then_inc(frs_done, 1)
                    for n in range(6):
                        j, r = divmod(n, 3)
                        act.wait_ge(up_mm, 6 * b + n + 1)
                        if n >= 2:
                            act.wait_ge(hm_done, 6 * b + n)
                        nc.scalar.activation(gg[0:HW[r], n % 2, :], bank[2 * (n % 2) + 1][0:HW[r], :], ACT.Gelu,
                                             bias=W["b1"][0:HW[r], 3 + r:4 + r]).then_inc(gg_done, 1)
                    for j in range(2):
                        n = TILE if j == 0 else TILE - 1
                        act.wait_ge(y_done, 2 * b + j + 1)
                        nc.scalar.sem_inc(tick, 1)
                        nc.scalar.activation(sh[0:64, cols(2 * b + j)], y[0:64, cols(2 * b + j)], ACT.Copy)
                        nc.scalar.activation(sh[64:P, bass.ds(b * L + j * TILE + 1, n)], y[64:P, bass.ds(b * L + j * TILE, n)],
                                             ACT.Copy).then_inc(sh_done, 1)

            @block.vector
            def _(dve):
                nc.vector.memset(k[:, :, 0:QT], 0.0).then_inc(init, 1)
                nc.vector.memset(v[:, :, :], 1.0).then_inc(init, 1)
                nc.vector.memset(pr[:, :, 0:QT - WIN], 0.0).then_inc(init, 1)
                nc.vector.memset(rs[:, :, :], 0.0).then_inc(init, 1)
                dve.wait_ge(init, 4)
                nc.vector.sem_inc(turned_done, 2)
                nc.vector.sem_inc(ss_done, 2)
                nc.vector.sem_inc(max_done, 2)
                nc.vector.sem_inc(ev_done[1], 1)
                nc.vector.sem_inc(on_done, 1)
                nc.vector.sem_inc(hm_done, 1)

                def rotate(b, n):
                    j, r, z = units[n]
                    dve.wait_ge(pq_done, NU * b + n + 1)
                    dve.wait_ge(sum_done, NU * b + n + 1)
                    for a in (1, 0):
                        if a == 0:
                            dve.wait_ge(sq_done, NU * b + n + 3)
                        last = nc.vector.scalar_tensor_tensor(
                            out=turned[:, n % 2, a, :], in0=bank[2 * a + n % 2][:, :],
                            scalar=W["scales"][:, 2 * z + a:2 * z + a + 1],
                            in1=tables[:, 2 * z + a, j * TILE:(j + 1) * TILE], op0=ALU.mult, op1=ALU.mult)
                    last.then_inc(turned_done, 1)

                def bound(b, n):
                    dve.wait_ge(ss_mm, NU * b + n + 3)
                    dve.wait_ge(ln_done, NU * b + n + 1)
                    nc.vector.tensor_scalar(ss[:, n % 2, :], bank[4 + n % 2][:, :], TINY, None, ALU.max).then_inc(ss_done, 1)

                def evacuate(g, mm):
                    dve.wait_ge(t_done, HF * g + 2 * mm + 2 + HF)
                    dve.wait_ge(av_done, HF * g + 2 * mm + 2)
                    nc.vector.tensor_copy(prT[:, 1, :, :].rearrange("q a n -> q (a n)"), bank[3][:, :]).then_inc(ev_done[1], 1)

                def body(b, g, i, where):
                    for s in range(HF):
                        dve.wait_ge(s_done, HF * g + s + HF + 1)
                        dve.wait_ge(exp_done, HF * g + s + 1)
                        nc.vector.sem_inc(tick, 1)
                        nc.vector.tensor_tensor_reduce(ms[:, s % 4, :], bank[s % 2][:, 0:KW], masks[:, min(where, 1), :],
                                                       -1.0, 3e38, ALU.add, ALU.min, nmx[:, s:s + 1]).then_inc(max_done, 1)
                        if s == 5:
                            evacuate(g, 1)
                    evacuate(g, 3)
                    dve.wait_ge(av_done, HF * g + HF + 4)
                    for a in range(2):
                        o = bank[4 + a][:, 0:4 * (DF + 1)].rearrange("q (h d) -> q h d", d=DF + 1)
                        nc.vector.reciprocal(rs[:, a, :], o[:, :, DF]).then_inc(rs_done, 1)
                    if where > 0:
                        dve.wait_ge(ot_done, g)
                    for a in range(2):
                        o = bank[4 + a][:, 0:4 * (DF + 1)].rearrange("q (h d) -> q h d", d=DF + 1)
                        dve.wait_ge(rs_done, 2 * g + a + 1)
                        last = nc.vector.tensor_tensor(on[:, 4 * a:4 * a + 4, :], o[:, :, 0:DF],
                                                       rs[:, a, :].unsqueeze(2).to_broadcast([P, 4, DF]), ALU.mult)
                    last.then_inc(on_done, 1)

                with nc.vector.Fori(0, NB) as b:
                    rotate(b, 0)
                    for n in range(NU):
                        if n + 1 < NU:
                            rotate(b, n + 1)
                        bound(b, n)
                    tiles(nc.vector, b, body)
                    nc.vector.memset(sh1[64:P, 0:1], 0.0).then_inc(zero_done, 1)
                    for j in range(2):
                        dve.wait_ge(wo_mm, 2 * b + j + 1)
                        dve.wait_ge(sh_done, 2 * b + 2)
                        nc.vector.tensor_tensor(y1[:, j, :], bank[7 - j][:, :], y[:, cols(2 * b + j)], ALU.add
                                                ).then_inc(y1_done, 1)
                    for j in range(2):
                        dve.wait_ge(frs_done, 2 * b + j + 1)
                        nc.vector.tensor_tensor(frs[:, j, :], bank[4 + j][:, :], frs[:, j, :], ALU.mult).then_inc(xn_done, 1)
                        dve.wait_ge(xn_done, 2 * b + j + 1)
                        nc.vector.tensor_scalar(fh[:, j, :], frs[:, j, :], W["ln"][:, 0:1], W["ln"][:, 1:2],
                                                ALU.mult, ALU.add).then_inc(fh_done, 1)
                    for n in range(6):
                        j, r = divmod(n, 3)
                        dve.wait_ge(gg_done, 6 * b + n + 1)
                        dve.wait_ge(dn_mm, 6 * b + n + 4)
                        nc.vector.scalar_tensor_tensor(out=hm[r][0:HW[r], :], in0=bank[2 * (n % 2)][0:HW[r], :],
                                                       scalar=W["b1"][0:HW[r], r:r + 1], in1=gg[0:HW[r], n % 2, :],
                                                       op0=ALU.add, op1=ALU.mult).then_inc(hm_done, 1)
                        if r == 2:
                            dve.wait_ge(dn_mm, 6 * b + 3 * j + 9)
                            nc.vector.scalar_tensor_tensor(out=y[:, cols(2 * b + j)], in0=bank[4 + j][:, :],
                                                           scalar=W["ln"][:, 2:3], in1=y1[:, j, :], op0=ALU.add,
                                                           op1=ALU.add).then_inc(y_done, 1)

            @block.gpsimd
            def _(pool):
                nc.gpsimd.sem_inc(sum_done, 2)
                nc.gpsimd.sem_inc(qk_done, 2)
                pool.wait_ge(init, 4)

                def mask_queries(g, i, a):
                    pool.wait_ge(s_done, HF * g + 4 * a + 4)
                    nc.gpsimd.sem_inc(tick, 1)
                    nc.gpsimd.tensor_tensor(
                        qm[:, 4 * a:4 * a + 4, :].rearrange("q (r e) n -> q r e n", e=2),
                        q[:, 2 * a:2 * a + 2, bass.ds(i * QT, QT)].unsqueeze(2).to_broadcast([P, 2, 2, QT]),
                        head_mask.unsqueeze(1).unsqueeze(3).to_broadcast([P, 2, 2, QT]), ALU.mult).then_inc(qm_done, 1)

                def body(b, g, i, where):
                    if where < 2:
                        for a in range(2):
                            mask_queries(g + 1, i + 1, a)

                with nc.gpsimd.Fori(0, NB) as b:
                    for n in range(NU):
                        j, r, z = units[n]
                        dst = q[:, r, j * TILE:(j + 1) * TILE] if z == 0 else k[:, r, QT + j * TILE:QT + (j + 1) * TILE]
                        pool.wait_ge(turned_done, NU * b + n + 3)
                        pool.wait_ge(qk_done, NU * b + n + 1)
                        nc.gpsimd.tensor_tensor(tsum[:, n % 2, :], turned[:, n % 2, 0, :], turned[:, n % 2, 1, :],
                                                ALU.add).then_inc(sum_done, 1)
                        pool.wait_ge(sum_done, NU * b + n + 3)
                        pool.wait_ge(rn_done, NU * b + n + 3)
                        if n == 0:
                            pool.wait_ge(s_done, HF * NI * b + HF)
                        nc.gpsimd.tensor_tensor(dst, tsum[:, n % 2, :], rn[:, n % 2, :], ALU.mult).then_inc(qk_done, 1)
                    pool.wait_ge(qk_done, NU * b + NU + 2)
                    for a in range(2):
                        mask_queries(8 * b, 0, a)
                    tiles(nc.gpsimd, b, body)


def add_gated(nc, tag, x, y, mod_gate):
    with Pool_(nc, tag) as m:
        done = m.sem("done")
        with nc.Block() as block:
            @block.vector
            def _(dve):
                with nc.vector.Fori(0, NB) as b:
                    xt = x[:, cols(b, L)]
                    nc.vector.scalar_tensor_tensor(out=xt, in0=y[:, cols(b, L)], scalar=mod_gate(b), in1=xt, op0=ALU.mult,
                                                   op1=ALU.add).then_inc(done, 1)


def load_weights(nc, mem, tag, vecs0, d):
    in_w = mem.sb("in_w", [P, 4 * P])
    xp_w = mem.sb("xp_w", [P, 2, 2 * NS + 2 * P])
    dt_w = mem.sb("dt_w", [NS, 2 * P])
    out_w = mem.sb("out_w", [P, 2, P])
    loaded = mem.sem("w_loaded")
    with nc.Block() as block:
        @block.sync
        def _(sp):
            sp.dma_start(in_w[:, :], d["in_w"]).then_inc(loaded, 16)
            sp.dma_start(xp_w[:, :, :], d["xp_w"]).then_inc(loaded, 16)
            sp.dma_start(dt_w[:, :], d["dt_w"]).then_inc(loaded, 16)
            sp.dma_start(out_w[:, :, :], d["out_w"]).then_inc(loaded, 16)
            sp.wait_ge(loaded, 64)
    return {
        "in_w": in_w, "xp_w": xp_w, "dt_w": dt_w, "out_w": out_w,
        "in_b": vecs0[:, 0:4], "conv_w": vecs0[:, 4:12].rearrange("q (c k) -> q c k", c=2), "conv_b": vecs0[:, 12:14],
        "dsB_b": vecs0[0:32, 14:15], "u_b": vecs0[:, 15:17], "dt_b": vecs0[:, 17:19], "D": vecs0[:, 19:21],
        "out_b": vecs0[:, 21:22],
    }


def build(nc, d, out, dbg=None, stop=99):
    with Pool_(nc, "k_") as g:
        consts = g.sb("consts", [P, 3 * P])
        vecs0 = g.sb("vecs0", [P, 40])
        eps_col = g.sb("eps_col", [P, 1])
        one_col = g.sb("one_col", [P, 1])
        mod0 = g.sb("mod0", [P, 6, NB])
        mod1 = g.sb("mod1", [P, 6, NB])
        x = g.sb("x", [P, T])
        setup = g.sem("setup")
        setc = g.sem("setc")
        with nc.Block() as block:
            @block.sync
            def _(sp):
                sp.dma_start(consts[:, :], d["consts"]).then_inc(setup, 16)
                sp.dma_start(vecs0[:, 0:28], d["vecs0"]).then_inc(setup, 16)
                sp.dma_start(x[:, :], d["xT"]).then_inc(setup, 16)
                sp.wait_ge(setup, 48)

            @block.vector
            def _(dve):
                nc.vector.memset(eps_col[:, :], EPS).then_inc(setc, 1)
                nc.vector.memset(one_col[:, :], 1.0).then_inc(setc, 1)
        center, mean, ident = (consts[:, k * P:(k + 1) * P] for k in range(3))
        modulation(nc, g, d["c0T"], d["wmod0"], "m0_", mod0)
        modulation(nc, g, d["c1T"], d["wmod1"], "m1_", mod1)

        def dump(ap):
            s = g.sem("dump")
            with nc.Block() as block:
                @block.sync
                def _(sp):
                    sp.dma_start(dbg, ap).then_inc(s, 16)
                    sp.wait_ge(s, 16)

        with Pool_(nc, "a_") as a:
            W = load_weights(nc, a, "wa_", vecs0, d)
            u = a.sb("u", [P, 2, T])
            delta = a.sb("delta", [P, 2, T])
            zs = a.sb("zs", [P, 2, T])
            B_dram = nc.dram_tensor("B_scratch", [NS, T], F32, kind="Internal").ap()
            with Pool_(nc, "ah_") as ah:
                h = ah.sb("h", [P, T])
                layernorm(nc, g, "ln1_", x, h, center, mean, eps_col[:, :],
                          lambda b: mod0[:, 1, bass.ds(b, 1)], lambda b: mod0[:, 0, bass.ds(b, 1)])
                if stop == 1:
                    return dump(h[:, :])
                mamba_inputs(nc, "mi_", W, h, u, delta, zs, B_dram)
            if stop == 2:
                return dump(u[:, :, :])
            softplus(nc, "sp_", delta, one_col[:, :])
            if stop == 3:
                return dump(delta[:, :, :])
            if stop == 4:
                return dump(B_dram)
            mamba_scan(nc, "ms_", W, x, u, delta, zs, B_dram, ident, mod0)
        if stop == 5:
            return dump(x[:, :])

        with Pool_(nc, "b_") as b:
            w1 = b.sb("w1", [P, 8, 4 * P])
            w2 = b.sb("w2", [P, 8, 4, P])
            gw = b.sb("gw", [P, 9 + 9 + 32])
            b2 = b.sb("b2", [8, P])
            h = b.sb("h", [P, T])
            w_dram = nc.dram_tensor("w_scratch", [PAIRS, 64, P], F32, kind="Internal").ap()
            moe_loaded = b.sem("moe_loaded")
            gate_loaded = b.sem("gate_loaded")
            with nc.Block() as block:
                @block.sync
                def _(sp):
                    sp.dma_start(gw[:, :], d["gate"]).then_inc(gate_loaded, 16)
                    sp.dma_start(w1[:, :, :], d["W1"]).then_inc(moe_loaded, 16)
                    sp.dma_start(w2[:, :, :, :], d["W2"]).then_inc(moe_loaded, 16)
                    sp.dma_start(b2[:, :], d["b2"]).then_inc(moe_loaded, 16)
                    sp.wait_ge(gate_loaded, 16)
            layernorm(nc, g, "ln2_", x, h, center, mean, eps_col[:, :],
                      lambda p: mod0[:, 4, bass.ds(p, 1)], lambda p: mod0[:, 3, bass.ds(p, 1)])
            if stop == 6:
                return dump(h[:, :])
            moe_gate(nc, "mg_", h, gw[:, 0:9], gw[:, 9:18], ident, w_dram)
            if stop == 7:
                return dump(w_dram)
            moe(nc, "mo_", x, h, w1, gw[:, 18:50], w2, b2[:, :], moe_loaded, 48, w_dram, mod0)
        if stop == 8:
            return dump(x[:, :])

        with Pool_(nc, "c_") as c:
            q = c.sb("q", [P, T + QT])
            k = c.sb("k", [P, T + 2 * QT])
            v = c.sb("v", [P, NQ + 1, VW])
            vg = c.sb("vg", [32, 2, NB, VW // 2])
            out_w = c.sb("out_w", [P, P])
            cc = c.sb("cc", [P, HB + 8])
            masks = c.sb("masks", [P, 3, 2 * QT + NG4])
            c_loaded = c.sem("c_loaded")
            with Pool_(nc, "ch_") as ch:
                h = ch.sb("h", [P, T])
                qkv_w = ch.sb("qkv_w", [P, 5 * P])
                rope = ch.sb("rope", [P, 4, L])
                with nc.Block() as block:
                    @block.sync
                    def _(sp):
                        for dst, name in ((qkv_w[:, :], "qkv_w"), (rope[:, :, :], "rope"), (vg[:, :, :, :], "vg"),
                                          (out_w[:, :], "out_w1"), (cc[:, :], "cc"), (masks[:, :, :], "masks")):
                            sp.dma_start(dst, d[name]).then_inc(c_loaded, 16)
                        sp.wait_ge(c_loaded, 96)
                layernorm(nc, g, "ln3_", x, h, center, mean, eps_col[:, :],
                          lambda p: mod1[:, 1, bass.ds(p, 1)], lambda p: mod1[:, 0, bass.ds(p, 1)])
                rope_qkv(nc, "rq_", h, qkv_w, rope, q, k, v, vg, cc[0:32, HB:HB + 8])
            if stop == 9:
                return dump(q[:, 0:T])
            if stop == 10:
                return dump(k[:, QT:QT + T])
            oT = c.sb("oT", [P, T + QT])
            band_attention(nc, "ba_", q, k, v, vg, cc[:, 0:HB], masks, ident, oT)
            if stop == 11:
                return dump(oT[:, QT:QT + T])
            out_project(nc, "op_", x, oT, QT, out_w[:, :], lambda p: mod1[:, 2, bass.ds(p, 1)])
        if stop == 12:
            return dump(x[:, :])

        with Pool_(nc, "d_") as dd:
            y = dd.sb("y", [P, T])
            sh = dd.sb("sh", [P, T])
            tables = dd.sb("tables", [P, 4, L])
            dc = dd.sb("dc", [P, P + 2])
            norm_bias = dd.sb("norm_bias", [P, 1])
            masks = dd.sb("masks", [P, 2, WIN + QT])
            qk_w = dd.sb("qk_w", [P, 4, 4 * P])
            v_w = dd.sb("v_w", [P, 4 * P])
            wo_w = dd.sb("wo_w", [P, 4, P])
            w1_w = dd.sb("w1_w", [P, 2 * HID])
            w2_w = dd.sb("w2_w", [P, 3, P])
            dv = dd.sb("dv", [P, 13])
            W = {"qk": qk_w, "v": v_w, "wo": wo_w, "w1": w1_w, "w2": w2_w, "scales": dv[:, 0:4], "b1": dv[:, 4:10],
                 "ln": dv[:, 10:13]}

            def load_layer(n):
                s_ = dd.sem(f"layer{n}")
                with nc.Block() as block:
                    @block.sync
                    def _(sp):
                        for dst, name in ((qk_w[:, :, :], "f_qk"), (v_w[:, :], "f_v"), (wo_w[:, :, :], "f_wo"),
                                          (w1_w[:, :], "f_w1"), (w2_w[:, :, :], "f_w2"), (dv[:, :], "f_dv")):
                            sp.dma_start(dst, d[f"{name}{n}"]).then_inc(s_, 16)
                        if n == 0:
                            for dst, name in ((tables[:, :, :], "f_tables"), (dc[:, :], "f_dc"), (masks[:, :, :], "f_masks")):
                                sp.dma_start(dst, d[name]).then_inc(s_, 16)
                        sp.wait_ge(s_, 96 if n else 144)

                    @block.vector
                    def _(dve):
                        nc.vector.memset(norm_bias[:, :], 0.5 * float(np.log(LN_SCALE))).then_inc(setc, 1)

            load_layer(0)
            layernorm(nc, g, "ln4_", x, y, center, mean, eps_col[:, :],
                      lambda p: mod1[:, 4, bass.ds(p, 1)], lambda p: mod1[:, 3, bass.ds(p, 1)])
            if stop == 13:
                return dump(y[:, :])
            shifted_copy(nc, "sc_", y, sh)
            for n in range(2):
                if n:
                    load_layer(n)
                local_layer(nc, f"l{n}_", W, y, sh, tables, dc[:, 0:P], center, mean, ident, dc[:, P:P + 2], masks,
                            (eps_col[:, :], norm_bias[:, :]))
                if stop == 14 + n:
                    return dump(y[:, :])
            add_gated(nc, "ag_", x, y, lambda b: mod1[:, 5, bass.ds(b, 1)])
        written = g.sem("written")
        with nc.Block() as block:
            @block.sync
            def _(sp):
                sp.dma_start(out, x[:, :]).then_inc(written, 16)
                sp.wait_ge(written, 16)


_V0 = 28


def layout(i):
    f = np.float32
    c = np.ascontiguousarray
    eye = np.eye(P, dtype=f)
    mean = np.full((P, P), 1.0 / P, f)

    def col(v):
        return c(v.reshape(-1, P).T)

    dsB_b = np.zeros((P, 1), f)
    dsB_b[0:32, 0] = i["L0_attn_x_proj_b"][0:32]
    vecs0 = np.concatenate([
        col(i["L0_attn_in_proj_b"]),
        i["L0_attn_conv_w"].reshape(2, P, 4).transpose(1, 0, 2).reshape(P, 8),
        col(i["L0_attn_conv_b"]),
        dsB_b,
        col(i["L0_attn_x_proj_b"][32:]),
        col(i["L0_attn_dt_proj_b"]),
        col(i["L0_attn_D"]),
        col(i["L0_attn_out_proj_b"]),
        np.zeros((P, 6), f),
    ], 1)
    w = i["L1_attn_qkv_w"].reshape(3, P, P)
    swap = np.arange(P) ^ 1
    qkv_w = np.concatenate([w[0], w[0][swap], w[1], w[1][swap], w[2]], 0).T
    inv_freq = (1.0 / f(10000.0) ** (np.arange(0, DH, 2, dtype=f) / f(DH))).astype(f)
    ang = np.outer(np.arange(L, dtype=f), inv_freq).astype(f)
    ang = np.concatenate([ang, ang], -1).T
    sign = np.where(np.arange(DH) % 2 == 0, -1.0, 1.0).astype(f)[:, None]
    cos, sin = np.tile(np.cos(ang), (HB, 1)).astype(f), np.tile(np.sin(ang) * sign, (HB, 1)).astype(f)
    r = f(DH ** -0.5)
    rope = np.stack([cos * r, sin * r, cos, sin], 1)
    vg = np.zeros((32, 2, NB, HB // 2, DH + 1), f)
    cc = np.zeros((P, HB + 8), f)
    for hd in range(HB):
        cc[hd * DH:(hd + 1) * DH, hd] = 1
        for j in range(NG4):
            vg[(hd % 8) * NG4 + j, hd // 8, :, hd % 8, DH] = 1
            cc[(hd % 8) * NG4 + j, HB + hd % 8] = 1
    ii, jj = np.arange(QT)[:, None], np.arange(QT)[None, :]
    masks = np.full((P, 3, 2 * QT + NG4), MASKED, f)
    masks[:, :, QT:2 * QT][np.broadcast_to((jj <= ii)[:, None], (P, 3, QT))] = 0
    masks[:, 1, 0:QT][(jj >= ii) | (jj < NG4)] = 0
    masks[:, 2, 0:QT][jj >= ii] = 0
    masks[:, 2, 2 * QT:] = 0
    half = np.arange(0, DF, 2, dtype=f)
    inv_freq = (1.0 / f(10000.0) ** (half / f(DF))).astype(f)
    tok = np.arange(L, dtype=f)
    fr = (tok[:, None] * inv_freq[None, :]).astype(f)
    fr = np.concatenate([fr, fr], -1)
    base = ((half + f(0.4 * DF)) / f(1.4 * DF)).astype(f)
    scale = (base[None, :] ** ((tok - L // 2) / f(WIN // 2))[:, None]).astype(f)
    scale = np.concatenate([scale, scale], -1)
    sg = np.where(np.arange(DF) < DF // 2, f(-1), f(1))
    cs, sn = np.cos(fr), np.sin(fr) * sg
    tables = np.stack([np.tile(a.T, (2, 1)) for a in (cs * scale * f(8), sn * scale * f(8), cs / scale, sn / scale)], 1)
    f_dc = np.zeros((P, P + 2), f)
    f_dc[0:DF, 0:DF] = f_dc[DF:, DF:P] = 1
    f_dc[0:DF, P] = f_dc[DF:, P + 1] = 1
    jj = np.arange(WIN + QT)[None, :] - WIN
    f_masks = np.full((P, 2, WIN + QT), MASKED, f)
    f_masks[:, 1][(jj <= ii) & (ii - jj <= WIN)] = 0
    f_masks[:, 0][(jj <= ii) & (ii - jj <= WIN) & (jj >= 0)] = 0
    layers = {}
    turn = (np.arange(4 * P) ^ (DF // 2))
    for n in range(2):
        wqkv = i["L1_ffn_wqkv"][n]
        wq, wk, wv = wqkv[:, 0:512], wqkv[:, 512:1024], wqkv[:, 1024:]
        qs, ks = np.tile(i["L1_ffn_q_scale"][n], 2)[:, None], np.tile(i["L1_ffn_k_scale"][n], 2)[:, None]
        tn = np.arange(P) ^ (DF // 2)
        b1 = np.zeros((P, 6), f)
        for r in range(3):
            m = min(P, HID - r * P)
            b1[0:m, r] = i["L1_ffn_b1"][n][r * P:r * P + m]
            b1[0:m, 3 + r] = i["L1_ffn_b1"][n][HID + r * P:HID + r * P + m]
        w2 = np.zeros((3 * P, P), f)
        w2[0:HID] = i["L1_ffn_w2"][n]
        layers |= {
            f"f_qk{n}": c(np.stack([wq, wq[:, turn], wk, wk[:, turn]], 1)),
            f"f_v{n}": c(wv),
            f"f_wo{n}": c(i["L1_ffn_wo"][n].reshape(4, P, P).transpose(1, 0, 2)),
            f"f_w1{n}": c(i["L1_ffn_w1"][n]),
            f"f_w2{n}": c(w2.reshape(3, P, P).transpose(1, 0, 2)),
            f"f_dv{n}": c(np.concatenate([qs, qs[tn], ks, ks[tn], b1, i["L1_ffn_ln_g"][n][:, None],
                                          i["L1_ffn_ln_b"][n][:, None], i["L1_ffn_b2"][n][:, None]], 1)),
        }
    return layers | {
        "f_tables": c(tables.astype(f)),
        "f_dc": f_dc,
        "f_masks": f_masks,
        "qkv_w": c(qkv_w),
        "rope": c(rope),
        "vg": c(vg.reshape(32, 2, NB, VW // 2)),
        "cc": cc,
        "masks": masks,
        "out_w1": c(i["L1_attn_out_w"].T),
        "xT": c(i["L0_attn_x"].reshape(T, P).T),
        "consts": c(np.concatenate([eye - mean, mean, eye], 1)),
        "vecs0": c(vecs0),
        "c0T": c(i["L0_c"].T),
        "c1T": c(i["L1_c"].T),
        "in_w": c(i["L0_attn_in_proj_w"]),
        "xp_w": c(i["L0_attn_x_proj_w"].reshape(2, P, -1).transpose(1, 0, 2)),
        "dt_w": c(i["L0_attn_dt_proj_w"]),
        "out_w": c(i["L0_attn_out_proj_w"].reshape(2, P, P).transpose(1, 0, 2)),
        "gate": c(np.concatenate([
            i["L0_ffn_Wg"], i["L0_ffn_Wt"], np.broadcast_to(i["L0_ffn_bg"], (P, 8)), np.broadcast_to(i["L0_ffn_bt"], (P, 1)),
            i["L0_ffn_b1"].reshape(8, 4, P).transpose(2, 0, 1).reshape(P, 32)], 1)),
        "W1": c(i["L0_ffn_W1"].transpose(1, 0, 2)),
        "W2": c(i["L0_ffn_W2"].reshape(8, 4, P, P).transpose(2, 0, 1, 3)),
        "b2": c(i["L0_ffn_b2"]),
        "wmod0": c(i["L0_wmod"]),
        "wmod1": c(i["L1_wmod"]),
    }


STOP = 99
DBG = None


def kernel(**inputs):
    import concourse.bacc as bacc
    from concourse.bass_utils import run_bass_kernel_spmd as run

    arrays = layout({k: np.asarray(v) for k, v in inputs.items()})
    nc = bacc.Bacc("TRN2", target_bir_lowering=False, num_devices=1)
    d = {k: nc.dram_tensor(f"in_{k}", list(v.shape), F32, kind="ExternalInput").ap() for k, v in arrays.items()}
    out = nc.dram_tensor("out", [P, T], F32, kind="ExternalOutput").ap()
    dbg = nc.dram_tensor("dbg", DBG, F32, kind="ExternalOutput").ap() if DBG else None
    build(nc, d, out, dbg, STOP)
    r = run(nc, [{f"in_{k}": v for k, v in arrays.items()}], core_ids=[0])
    got = r.results[0]["out"]
    return np.ascontiguousarray(got.T).reshape(NB, L, P)
```

```python
from contextlib import ExitStack

import numpy as np

import concourse.bass as bass
from concourse import mybir

ALU = mybir.AluOpType
ACT = mybir.ActivationFunctionType
F32 = mybir.dt.float32
F32R = mybir.dt.float32r
AX_X = mybir.AxisListType.X

P = 128
NB = 4
L = 1024
T = NB * L
TILE = 512
PAIRS = T // (2 * TILE)
XCW = L + 4
NS = 16
EPS = 1e-5
LN_EXP = "natural_log_exp_and_others"


class PhaseMemory:

    def __init__(self, nc, prefix):
        self.nc, self.prefix, self.stack, self.sems = nc, prefix, ExitStack(), []

    def __enter__(self):
        return self

    def __exit__(self, *a):
        if self.sems:
            self.nc.clear_and_free_semaphores(self.sems)
            self.nc.all_engine_barrier()
        return self.stack.__exit__(*a)

    def sb(self, name, shape, dt=F32):
        return self.stack.enter_context(self.nc.sbuf_tensor(self.prefix + name, shape, dt))

    def ps(self, name, shape, dt=F32):
        return self.stack.enter_context(self.nc.psum_tensor(self.prefix + name, shape, dt))

    def sem(self, name):
        self.sems.append(self.nc.alloc_semaphore(name=self.prefix + name))
        return self.sems[-1]


def cols(t, n=TILE):
    return bass.ds(t * n, n)


def upper(engine, hi, full):
    return engine.tensor_copy(hi.bitcast(F32R), full)


def lower(engine, lo, full, hi):
    return engine.tensor_tensor(lo.bitcast(F32R), full, hi, ALU.subtract)


def product(nc, out, w, x, start, stop):
    for n, (i, j) in enumerate(((0, 0), (0, 1), (1, 0))):
        last = nc.tensor.matmul(out, w[i].bitcast(F32R), x[j].bitcast(F32R), start=start and n == 0, stop=stop and n == 2)
    return last


def split_parts(nc, tag, arrays, loaded=None, n_loads=0):
    with PhaseMemory(nc, tag) as m:
        hi_done = m.sem("hi_done")
        lo_done = m.sem("lo_done")

        def pieces():
            for arrays3 in arrays:
                n = arrays3[0].shape[-1]
                cut = n * 11 // 16
                yield [a[:, 0:cut] for a in arrays3], [a[:, cut:n] for a in arrays3]

        with nc.Block() as block:
            @block.vector
            def _(dve):
                if loaded is not None:
                    dve.wait_ge(loaded, n_loads)
                n = 0
                for (full, hi, lo), (full2, hi2, _lo2) in pieces():
                    upper(nc.vector, hi2, full2).then_inc(hi_done, 1)
                    upper(nc.vector, hi, full).then_inc(hi_done, 1)
                    n += 2
                    dve.wait_ge(hi_done, n)
                    lower(nc.vector, lo, full, hi).then_inc(lo_done, 1)

            @block.gpsimd
            def _(pool):
                n = 0
                for _first, (full2, hi2, lo2) in pieces():
                    pool.wait_ge(hi_done, n + 1)
                    n += 2
                    lower(nc.gpsimd, lo2, full2, hi2).then_inc(lo_done, 1)


def modulation(nc, mem, cT_d, wmod_d, tag, mod):
    with PhaseMemory(nc, tag) as m:
        cT = m.sb("cT", [P, NB])
        silu_c = m.sb("silu_c", [P, NB])
        wmod = m.sb("wmod", [P, 6 * P])
        raw = m.sb("raw", [P, 6, NB])
        sign = m.sb("sign", [P, 2, NB])
        size = m.sb("size", [P, 2, NB])
        size2 = m.sb("size2", [P, 2, NB])
        acc = m.ps("acc", [P, 6, NB])
        loaded = m.sem("loaded")
        silu_done = m.sem("silu_done")
        mm_done = m.sem("mm_done")
        step = m.sem("step")
        with nc.Block() as block:
            @block.sync
            def _(sp):
                sp.dma_start(cT[:, :], cT_d).then_inc(loaded, 16)
                sp.dma_start(wmod[:, :], wmod_d).then_inc(loaded, 16)

            @block.scalar
            def _(act):
                act.wait_ge(loaded, 32)
                nc.scalar.activation(silu_c[:, :], cT[:, :], ACT.Silu).then_inc(silu_done, 1)

            @block.tensor
            def _(pe):
                pe.wait_ge(silu_done, 1)
                for j in range(6):
                    last = nc.tensor.matmul(acc[:, j, :], wmod[:, j * P:(j + 1) * P], silu_c[:, :], start=True, stop=True)
                last.then_inc(mm_done, 1)

            @block.vector
            def _(dve):
                dve.wait_ge(mm_done, 1)
                nc.vector.tensor_copy(raw[:, :, :], acc[:, :, :]).then_inc(step, 1)
                dve.wait_ge(step, 1)
                nc.vector.tensor_copy(mod[:, 0::3, :], raw[:, 0::3, :]).then_inc(step, 1)
                nc.vector.tensor_scalar(mod[:, 1::3, :], raw[:, 1::3, :], 1.0, None, ALU.add).then_inc(step, 1)
                nc.vector.tensor_scalar(sign[:, :, :], raw[:, 2::3, :], 0.0, 2.0, ALU.is_ge, ALU.mult).then_inc(step, 1)
                nc.vector.scalar_tensor_tensor(out=size[:, :, :], in0=raw[:, 2::3, :], scalar=-1.0, in1=raw[:, 2::3, :],
                                               op0=ALU.mult, op1=ALU.max).then_inc(step, 1)
                dve.wait_ge(step, 5)
                nc.vector.tensor_scalar(size2[:, :, :], size[:, :, :], 0.25, None, ALU.max).then_inc(step, 1)
                dve.wait_ge(step, 6)
                nc.vector.scalar_tensor_tensor(out=mod[:, 2::3, :], in0=sign[:, :, :], scalar=-1.0, in1=size2[:, :, :],
                                               op0=ALU.add, op1=ALU.mult).then_inc(step, 1)


def layernorm(nc, tag, x, h, center, mean, eps_col, scale, shift):
    NT = T // TILE
    with PhaseMemory(nc, tag) as m:
        sq = m.sb("sq", [P, 2, TILE])
        lnv = m.sb("lnv", [P, 2, TILE])
        rstd = m.sb("rstd", [P, 2, TILE])
        xn = m.sb("xn", [P, 2, TILE])
        cen = m.ps("cen", [P, 4, 512])
        var = m.ps("var", [P, 2, 512])
        cen_done = m.sem("cen_done")
        sq_done = m.sem("sq_done")
        var_done = m.sem("var_done")
        ln_done = m.sem("ln_done")
        rstd_done = m.sem("rstd_done")
        xn_done = m.sem("xn_done")
        h_done = m.sem("h_done")

        def tile(t):
            return slice(t * TILE, (t + 1) * TILE)

        with nc.Block() as block:
            @block.tensor
            def _(pe):
                def centre(t):
                    if t >= 4:
                        pe.wait_ge(xn_done, t - 3)
                    nc.tensor.matmul(cen[:, t % 4, :], center, x[:, tile(t)], start=True, stop=True).then_inc(cen_done, 1)

                for t in range(3):
                    centre(t)
                for t in range(NT):
                    pe.wait_ge(sq_done, t + 1)
                    if t >= 2:
                        pe.wait_ge(ln_done, t - 1)
                    nc.tensor.matmul(var[:, t % 2, :], mean, sq[:, t % 2, :], start=True, stop=True).then_inc(var_done, 1)
                    if t + 3 < NT:
                        centre(t + 3)

            @block.scalar
            def _(act):
                nc.scalar.preload_act_table_set(LN_EXP)

                def square(t):
                    act.wait_ge(cen_done, t + 1)
                    if t >= 2:
                        act.wait_ge(var_done, t - 1)
                    nc.scalar.activation(sq[:, t % 2, :], cen[:, t % 4, :], ACT.Square).then_inc(sq_done, 1)

                square(0)
                square(1)
                for t in range(NT):
                    act.wait_ge(var_done, t + 1)
                    if t >= 2:
                        act.wait_ge(rstd_done, t - 1)
                    nc.scalar.activation(lnv[:, t % 2, :], var[:, t % 2, :], ACT.Ln, bias=eps_col).then_inc(ln_done, 1)
                    if t + 2 < NT:
                        square(t + 2)
                    act.wait_ge(ln_done, t + 1)
                    if t >= 2:
                        act.wait_ge(xn_done, t - 1)
                    nc.scalar.activation(rstd[:, t % 2, :], lnv[:, t % 2, :], ACT.Exp, scale=-0.5).then_inc(rstd_done, 1)

            @block.vector
            def _(dve):
                for t in range(NT):
                    b = t * TILE // L
                    dve.wait_ge(rstd_done, t + 1)
                    if t >= 2:
                        dve.wait_ge(h_done, t - 1)
                    nc.vector.tensor_tensor(xn[:, t % 2, :], cen[:, t % 4, :], rstd[:, t % 2, :], ALU.mult).then_inc(xn_done, 1)
                    dve.wait_ge(xn_done, t + 1)
                    nc.vector.tensor_scalar(h[:, tile(t)], xn[:, t % 2, :], scale[:, b:b + 1], shift[:, b:b + 1],
                                            ALU.mult, ALU.add).then_inc(h_done, 1)


def mamba_inputs(nc, tag, W, h, u, delta, zs, B_dram):
    NT = T // TILE
    with PhaseMemory(nc, tag) as m:
        xc = m.sb("xc", [P, 2, NB * XCW])
        cv = m.sb("cv", [P, 2, TILE])
        cv2 = m.sb("cv2", [P, 2, TILE])
        xcs = m.sb("xcs", [P, 2, 2, TILE])
        dsB = m.sb("dsB", [32, 2, TILE])
        p_in = m.ps("p_in", [P, 4, 512])
        p_xp = m.ps("p_xp", [P, 3, 512])
        p_dt = m.ps("p_dt", [P, 512])
        pads = m.sem("pads")
        in_done = m.sem("in_done")
        xc_done = m.sem("xc_done")
        conv_step = m.sem("conv_step")
        silu_done = m.sem("silu_done")
        xp_done = m.sem("xp_done")
        xp_out = m.sem("xp_out")
        dt_done = m.sem("dt_done")
        dt_out = m.sem("dt_out")
        B_out = [m.sem(f"B_out{j}") for j in range(2)]

        def steps(eng, step):
            with eng.Fori(0, PAIRS - 1) as p:
                step(2 * p, (p + 1, 0), (p, 1), 0)
                step(2 * p + 1, (p + 1, 1), (p + 1, 0), 1)
            step(NT - 2, None, (NB - 1, 1), 0)
            step(NT - 1, None, None, 1)

        with nc.Block() as block:
            @block.tensor
            def _(pe):
                def in_proj(t):
                    for k in range(4):
                        pe.wait_ge(xc_done, 4 * t + k + 1)
                        nc.tensor.matmul(p_in[:, k, :], W["in_w"][:, k * P:(k + 1) * P], h[:, cols(t)],
                                         start=True, stop=True).then_inc(in_done, 1)

                def x_proj(t, j):
                    for k in range(3):
                        out = p_xp[0:32, 0, :] if k == 0 else p_xp[:, k, :]
                        lo, hi = (0, 32) if k == 0 else (32 + (k - 1) * P, 32 + k * P)
                        pe.wait_ge(silu_done, 2 * t + 4)
                        pe.wait_ge(xp_out, 3 * t + k + 1)
                        for c in range(2):
                            last = nc.tensor.matmul(out, W["xp_w"][:, c, lo:hi], xcs[:, j, c, :],
                                                    start=c == 0, stop=c == 1)
                        last.then_inc(xp_done, 1)
                    for c in range(2):
                        pe.wait_ge(xp_out, 3 * t + 4)
                        pe.wait_ge(dt_out, 2 * t + c + 1)
                        nc.tensor.matmul(p_dt[:, :], W["dt_w"][:, c * P:(c + 1) * P], dsB[0:16, j, :],
                                         start=True, stop=True).then_inc(dt_done, 1)

                nc.tensor.sem_inc(xp_done, 6)
                nc.tensor.sem_inc(dt_done, 4)
                def step(t, two_on, one_on, j):
                    if two_on is not None:
                        in_proj(t + 2)
                    x_proj(t, j)

                in_proj(0)
                in_proj(1)
                steps(nc.tensor, step)

            @block.scalar
            def _(act):
                def leave_in(t, b, half):
                    for k in range(4):
                        act.wait_ge(in_done, 4 * t + k + 1)
                        if k < 2:
                            nc.scalar.activation(xc[:, k, bass.ds(b * XCW + 3 + half * TILE, TILE)], p_in[:, k, :],
                                                 ACT.Identity, bias=W["in_b"][:, k:k + 1]).then_inc(xc_done, 1)
                        else:
                            nc.scalar.activation(zs[:, k - 2, cols(t)], p_in[:, k, :], ACT.Silu,
                                                 bias=W["in_b"][:, k:k + 1]).then_inc(xc_done, 1)

                def silu_conv(t, j):
                    for c in range(2):
                        act.wait_ge(conv_step, 8 * t + 8 + c)
                        act.wait_ge(xp_done, 3 * t + 3)
                        nc.scalar.activation(xcs[:, j, c, :], cv[:, c, :], ACT.Silu,
                                             bias=W["conv_b"][:, c:c + 1]).then_inc(silu_done, 1)

                nc.scalar.sem_inc(xc_done, 4)
                nc.scalar.sem_inc(silu_done, 2)
                nc.scalar.preload_act_table(ACT.Silu)

                def step(t, two_on, one_on, j):
                    if two_on is not None:
                        leave_in(t + 2, *two_on)
                    if one_on is not None:
                        silu_conv(t + 1, 1 - j)

                leave_in(0, 0, 0)
                leave_in(1, 0, 1)
                silu_conv(0, 0)
                steps(nc.scalar, step)

            @block.vector
            def _(dve):
                def conv(t, p, half):
                    dve.wait_ge(xc_done, 4 * t + 4 + 2)
                    for k in range(4):
                        for c in range(2):
                            n = 8 * t + 1 + 2 * k + c
                            src = xc[:, c, bass.ds(p * XCW + half * TILE + k, TILE)]
                            w = W["conv_w"][:, c, k:k + 1]
                            dst = (cv2 if k % 2 == 0 else cv)[:, c, :]
                            if k == 0:
                                if c == 0:
                                    dve.wait_ge(conv_step, n)
                                nc.vector.tensor_scalar(dst, src, w, None, ALU.mult).then_inc(conv_step, 1)
                            else:
                                dve.wait_ge(conv_step, n - 1)
                                if k == 1:
                                    dve.wait_ge(silu_done, 2 * t + c + 1)
                                prev = (cv if k % 2 == 0 else cv2)[:, c, :]
                                nc.vector.scalar_tensor_tensor(out=dst, in0=src, scalar=w, in1=prev, op0=ALU.mult,
                                                               op1=ALU.add).then_inc(conv_step, 1)

                def leave_xp(t, j):
                    dve.wait_ge(xp_done, 3 * t + 7)
                    dve.wait_ge(dt_done, 2 * t + 2)
                    dve.wait_ge(B_out[j], 8 * t - 8 * j + 16)
                    nc.vector.tensor_scalar(dsB[:, j, :], p_xp[0:32, 0, :], W["dsB_b"], None, ALU.add).then_inc(xp_out, 1)
                    for c in range(2):
                        dve.wait_ge(xp_done, 3 * t + 8 + c)
                        nc.vector.tensor_scalar(u[:, c, cols(t)], p_xp[:, 1 + c, :], W["u_b"][:, c:c + 1], None,
                                                ALU.add).then_inc(xp_out, 1)
                    for c in range(2):
                        dve.wait_ge(dt_done, 2 * t + c + 5)
                        nc.vector.tensor_scalar(delta[:, c, cols(t)], p_dt[:, :], W["dt_b"][:, c:c + 1], None,
                                                ALU.add).then_inc(dt_out, 1)

                nc.vector.sem_inc(xp_out, 3)
                nc.vector.sem_inc(dt_out, 1)
                nc.vector.memset(xc[:, :, :].rearrange("q c (b w) -> q c b w", b=NB)[:, :, :, 0:3], 0.0).then_inc(conv_step, 1)

                def step(t, two_on, one_on, j):
                    if one_on is not None:
                        conv(t + 1, *one_on)
                    leave_xp(t, j)

                conv(0, 0, 0)
                steps(nc.vector, step)

            @block.sync
            def _(sp):
                for j in range(2):
                    nc.sync.sem_inc(B_out[j], 16)
                with nc.sync.Fori(0, PAIRS) as p:
                    for j in range(2):
                        sp.wait_ge(xp_out, 3 * (2 * p + j) + 4)
                        sp.dma_start(B_dram[:, cols(2 * p + j)], dsB[16:32, j, :]).then_inc(B_out[j], 16)
                for j in range(2):
                    sp.wait_ge(B_out[j], 16 * (PAIRS + 1))


def mamba_scan(nc, tag, W, x, u, delta, zs, B_dram, ident, one_col, mod):
    NG = 4
    CH = NS // NG
    ND = 2
    NI = 4
    NT = 2
    U = 2 * NS
    with PhaseMemory(nc, tag) as m:
        w = m.sb("w", [P, 2, L])
        soft = m.sb("soft", [P, L])
        relu = m.sb("relu", [P, L])
        Bb = m.sb("Bb", [P, 2, NG, L])
        dec = m.sb("dec", [P, ND, L])
        inp = m.sb("inp", [P, NI, L])
        st = m.sb("st", [P, NT, L])
        yu = m.sb("yu", [P, L])
        upd = m.sb("upd", [P, TILE])
        p_y = m.ps("p_y", [P, 2, 2, 512])
        p_o = m.ps("p_o", [P, 2, 512])
        B_in = [m.sem(f"B_in{k}") for k in range(2)]
        w_done = m.sem("w_done")
        soft_step = m.sem("soft_step")
        delta_done = m.sem("delta_done")
        tick = m.sem("tick")
        dec_done = m.sem("dec_done")
        inp_v = m.sem("inp_v")
        inp_g = m.sem("inp_g")
        st_done = m.sem("st_done")
        sum_done = m.sem("sum_done")
        yu_done = m.sem("yu_done")
        y_done = m.sem("y_done")
        o_done = m.sem("o_done")
        upd_done = m.sem("upd_done")
        add_done = m.sem("add_done")
        units = [(q, c, q * NG + i, i) for q in range(CH) for c in range(2) for i in range(NG)]
        on_pool = [k % 2 == 1 for k in range(U)]
        before_v = [sum(not o for o in on_pool[:k]) for k in range(U + 1)]
        before_g = [sum(on_pool[:k]) for k in range(U + 1)]

        def batches(eng, body):
            body(0, True, False)
            with eng.Fori(1, NB - 1) as b:
                body(b, False, False)
            body(NB - 1, False, True)

        with nc.Block() as block:
            @block.sync
            def _(sp):
                with nc.sync.Fori(0, NB) as b:
                    for q in range(CH):
                        sp.wait_ge(inp_v, before_v[U] * b + before_v[8 * q] + 4)
                        sp.wait_ge(inp_g, before_g[U] * b + before_g[8 * q] + 4)
                        sp.dma_start(Bb[:, q % 2, :, :], B_dram[q * NG:(q + 1) * NG, cols(b, L)].partition_broadcast(P)
                                     ).then_inc(B_in[q % 2], 16)

            @block.scalar
            def _(act):
                def positive(b, c, step):
                    n = 4 * (2 * b + c)
                    v = delta[:, c, cols(b, L)]
                    if step == 0:
                        act.wait_ge(delta_done, 2 * b + c + 1)
                        nc.scalar.sem_inc(tick, 1)
                        nc.scalar.activation(soft[:, :], v, ACT.Abs).then_inc(soft_step, 1)
                    if step == 1:
                        nc.scalar.activation(relu[:, :], v, ACT.Relu).then_inc(soft_step, 1)
                    if step == 2:
                        act.wait_ge(soft_step, n + 1)
                        nc.scalar.activation(soft[:, :], soft[:, :], ACT.Exp, scale=-1.0).then_inc(soft_step, 1)
                    if step == 3:
                        act.wait_ge(soft_step, n + 3)
                        nc.scalar.activation(soft[:, :], soft[:, :], ACT.Ln, bias=one_col).then_inc(soft_step, 1)

                def body(b, first, last):
                    for k, (q, c, n, i) in enumerate(units):
                        if q == 0 and i == 0:
                            act.wait_ge(delta_done, 2 * b + c + 2)
                        act.wait_ge(st_done, U * b + k + NI - ND + 1)
                        nc.scalar.sem_inc(tick, 1)
                        nc.scalar.activation(dec[:, k % ND, :], delta[:, c, cols(b, L)], ACT.Exp,
                                             scale=-float(n + 1)).then_inc(dec_done, 1)
                        if 6 <= k < 22 and k % 2 == 0 and not last:
                            positive(b + 1, (k - 6) // 8, (k - 6) // 2 % 4)

                nc.scalar.preload_act_table_set(LN_EXP)
                for c in range(2):
                    for step in range(4):
                        positive(0, c, step)
                batches(nc.scalar, body)

            def make_input(eng, ns, k, b, done):
                q, c, n, i = units[k]
                eng.wait_ge(B_in[q % 2], 32 * b + 16 * (q // 2) + 16)
                eng.wait_ge(w_done, 2 * b + c + 1)
                eng.wait_ge(st_done, U * b + k + 1)
                ns.tensor_tensor(inp[:, k % NI, :], w[:, c, :], Bb[:, q % 2, i, :], ALU.mult).then_inc(done, 1)

            @block.gpsimd
            def _(pool):
                def add_positive(b, c):
                    pool.wait_ge(soft_step, 4 * (2 * b + c) + 4)
                    nc.gpsimd.sem_inc(tick, 1)
                    nc.gpsimd.tensor_tensor(delta[:, c, cols(b, L)], soft[:, :], relu[:, :], ALU.add).then_inc(delta_done, 1)

                def factor(b, c, first):
                    pool.wait_ge(delta_done, 2 * b + c + 2)
                    if not first:
                        pool.wait_ge(inp_v, before_v[U] * (b - 1) + before_v[28 + 4 * c] + 8)
                        pool.wait_ge(inp_g, before_g[U] * (b - 1) + before_g[28 + 4 * c] + 8)
                    nc.gpsimd.tensor_tensor(w[:, c, :], u[:, c, cols(b, L)], delta[:, c, cols(b, L)],
                                            ALU.mult).then_inc(w_done, 1)

                def body(b, first, last):
                    for k in range(U):
                        if on_pool[k]:
                            make_input(pool, nc.gpsimd, k, b, inp_g)
                        if not last:
                            if k in (13, 21):
                                add_positive(b + 1, k // 8 - 1)
                            if k in (27, 31):
                                factor(b + 1, k // 4 - 6, False)

                nc.gpsimd.sem_inc(inp_g, 8)
                nc.gpsimd.sem_inc(delta_done, 1)
                for c in range(2):
                    add_positive(0, c)
                    factor(0, c, True)
                batches(nc.gpsimd, body)

            @block.vector
            def _(dve):
                nc.vector.sem_inc(inp_v, 8)
                nc.vector.sem_inc(st_done, NI)
                nc.vector.sem_inc(yu_done, 2)
                nc.vector.sem_inc(upd_done, 2)
                nc.vector.sem_inc(add_done, 1)
                nc.vector.sem_inc(y_done, 1)

                def scan(k, b):
                    dve.wait_ge(dec_done, U * b + k + 1)
                    if on_pool[k]:
                        dve.wait_ge(inp_g, before_g[U] * b + before_g[k] + 9)
                    else:
                        dve.wait_ge(inp_v, before_v[U] * b + before_v[k] + 9)
                    dve.wait_ge(sum_done, U * b + k + 1)
                    nc.vector.tensor_tensor_scan(st[:, k % NT, :], dec[:, k % ND, :], inp[:, k % NI, :], 0.0,
                                                 ALU.mult, ALU.add).then_inc(st_done, 1)

                def gated(b, c):
                    dve.wait_ge(sum_done, U * b + 28 + 4 * c + NT)
                    dve.wait_ge(y_done, 2 * b + c + 1)
                    nc.vector.scalar_tensor_tensor(
                        out=yu[:, :], in0=u[:, c, cols(b, L)], scalar=W["D"][:, c:c + 1],
                        in1=p_y[:, c, :, :].rearrange("q a n -> q (a n)"), op0=ALU.mult, op1=ALU.add).then_inc(yu_done, 1)
                    dve.wait_ge(yu_done, 2 * b + c + 3)
                    nc.vector.tensor_tensor(zs[:, c, cols(b, L)], yu[:, :], zs[:, c, cols(b, L)], ALU.mult).then_inc(y_done, 1)

                def add_output(b):
                    for k in range(2):
                        dve.wait_ge(o_done, 2 * b + k + 3)
                        dve.wait_ge(add_done, 2 * b + k + 1)
                        nc.vector.tensor_scalar(upd[:, :], p_o[:, k, :], W["out_b"], mod[:, 2, bass.ds(b, 1)], ALU.add,
                                                ALU.mult).then_inc(upd_done, 1)
                        dve.wait_ge(upd_done, 2 * b + k + 3)
                        nc.vector.tensor_tensor(x[:, cols(2 * b + k)], x[:, cols(2 * b + k)], upd[:, :],
                                                ALU.add).then_inc(add_done, 1)

                def body(b, first, last):
                    for k in range(U):
                        if not on_pool[k]:
                            make_input(dve, nc.vector, k, b, inp_v)
                        if k >= 1:
                            scan(k - 1, b)
                        if k == 3 and not first:
                            gated(b - 1, 1)
                        if k == 8 and not first:
                            add_output(b - 1)
                        if k == U - 1:
                            gated(b, 0)
                    scan(U - 1, b)

                batches(nc.vector, body)
                gated(NB - 1, 1)
                add_output(NB - 1)

            @block.tensor
            def _(pe):
                nc.tensor.sem_inc(sum_done, NT)
                nc.tensor.sem_inc(o_done, 2)

                def project(b):
                    for a in range(2):
                        pe.wait_ge(y_done, 2 * b + 3)
                        pe.wait_ge(upd_done, 2 * b + a + 1)
                        for c in range(2):
                            last = nc.tensor.matmul(p_o[:, a, :], W["out_w"][:, c, :], zs[:, c, cols(2 * b + a)],
                                                    start=c == 0, stop=c == 1)
                        last.then_inc(o_done, 1)

                def body(b, first, last):
                    for k, (q, c, n, i) in enumerate(units):
                        pe.wait_ge(st_done, U * b + k + NI + 1)
                        if n == 0:
                            pe.wait_ge(yu_done, 2 * b + c + 1)
                        for a in range(2):
                            last = nc.tensor.matmul(p_y[:, c, a, :], ident, st[:, k % NT, a * TILE:(a + 1) * TILE],
                                                    start=n == 0, stop=n == NS - 1)
                        last.then_inc(sum_done, 1)
                        if k == 4 and not first:
                            project(b - 1)

                batches(nc.tensor, body)
                project(NB - 1)


def moe_gate(nc, tag, h, gate_w, gate_b, ident, w_dram, to_split, weights_loaded, n_loads):
    E, NT = 8, T // P
    with PhaseMemory(nc, tag) as m:
        hs = m.sb("hs", [P, 2, TILE])
        lg = m.sb("lg", [P, NT, E + 1])
        top = m.sb("top", [P, NT])
        ex = m.sb("ex", [P, NT, E])
        ez = m.sb("ez", [P, NT])
        den = m.sb("den", [P, NT])
        rden = m.sb("rden", [P, NT])
        thr = m.sb("thr", [P, NT])
        gate = m.sb("gate", [P, NT, E])
        w = m.sb("w", [P, PAIRS, E, NT // PAIRS])
        wT = m.sb("wT", [64, PAIRS, P])
        p_lg = m.ps("p_lg", [P, 2, 512])
        p_wT = m.ps("p_wT", [64, PAIRS, P])
        hs_done = m.sem("hs_done")
        lg_mm = m.sem("lg_mm")
        lg_done = m.sem("lg_done")
        step = m.sem("step")
        exp_done = m.sem("exp_done")
        wT_mm = m.sem("wT_mm")
        wT_done = m.sem("wT_done")
        stored = m.sem("stored")
        hi_done = m.sem("hi_done")
        lo_done = m.sem("lo_done")
        with nc.Block() as block:
            @block.scalar
            def _(act):
                with nc.scalar.Fori(0, PAIRS) as p:
                    for j in range(2):
                        act.wait_ge(lg_mm, 2 * p + j + 1)
                        nc.scalar.activation(hs[:, j, :], h[:, cols(2 * p + j)], ACT.Copy).then_inc(hs_done, 1)
                act.wait_ge(step, 2)
                nc.scalar.activation(ex[:, :, :], gate[:, :, :], ACT.Exp).then_inc(exp_done, 1)
                nc.scalar.activation(ez[:, :], lg[:, :, E], ACT.Exp, scale=-1.0).then_inc(exp_done, 1)

            @block.tensor
            def _(pe):
                nc.tensor.sem_inc(lg_mm, 2)
                with nc.tensor.Fori(0, PAIRS) as p:
                    for j in range(2):
                        pe.wait_ge(hs_done, 2 * p + j + 1)
                        pe.wait_ge(lg_done, 2 * p + j + 1)
                        for q in range(4):
                            last = nc.tensor.matmul(p_lg[:, j, q * 16:q * 16 + E + 1], hs[:, j, q * P:(q + 1) * P],
                                                    gate_w, start=True, stop=True)
                        last.then_inc(lg_mm, 1)
                pe.wait_ge(step, 12)
                for p in range(PAIRS):
                    last = nc.tensor.transpose(p_wT[:, p, :], w[:, p, :, :].rearrange("q e t -> q (e t)"), ident)
                last.then_inc(wT_mm, 1)

            @block.vector
            def _(dve):
                nc.vector.sem_inc(lg_done, 2)
                dve.wait_ge(weights_loaded, n_loads)
                for full, hi, _lo in to_split:
                    upper(nc.vector, hi, full).then_inc(hi_done, 1)
                with nc.vector.Fori(0, PAIRS) as p:
                    for j in range(2):
                        dve.wait_ge(lg_mm, 2 * p + j + 3)
                        nc.vector.tensor_tensor(
                            lg[:, bass.ds(8 * p + 4 * j, 4), :],
                            p_lg[:, j, 0:64].rearrange("q (a e) -> q a e", e=16)[:, :, 0:E + 1],
                            gate_b.unsqueeze(1).to_broadcast([P, 4, E + 1]), ALU.add).then_inc(lg_done, 1)
                n = [0]

                def then(ins):
                    n[0] += 1
                    ins.then_inc(step, 1)
                    dve.wait_ge(step, n[0])

                def over_e(v):
                    return v.unsqueeze(2).to_broadcast([P, NT, E])

                dve.wait_ge(lg_done, 2 * PAIRS + 2)
                then(nc.vector.tensor_reduce(top[:, :], lg[:, :, 0:E], AX_X, ALU.max))
                then(nc.vector.tensor_tensor(gate[:, :, :], lg[:, :, 0:E], over_e(top[:, :]), ALU.subtract))
                dve.wait_ge(exp_done, 2)
                then(nc.vector.tensor_reduce(den[:, :], ex[:, :, :], AX_X, ALU.add))
                then(nc.vector.reciprocal(rden[:, :], den[:, :]))
                then(nc.vector.tensor_tensor(gate[:, :, :], ex[:, :, :], over_e(rden[:, :]), ALU.mult))
                then(nc.vector.tensor_scalar(ez[:, :], ez[:, :], 1.0, None, ALU.add))
                then(nc.vector.reciprocal(thr[:, :], ez[:, :]))
                then(nc.vector.tensor_scalar(thr[:, :], thr[:, :], 0.125, None, ALU.mult))
                then(nc.vector.tensor_tensor(gate[:, :, :], gate[:, :, :], over_e(thr[:, :]), ALU.subtract))
                then(nc.vector.tensor_scalar(gate[:, :, :], gate[:, :, :], 0.0, None, ALU.max))
                then(nc.vector.tensor_reduce(den[:, :], gate[:, :, :], AX_X, ALU.add))
                then2 = nc.vector.scalar_tensor_tensor(out=top[:, :], in0=den[:, :], scalar=0.0, in1=den[:, :],
                                                       op0=ALU.is_equal, op1=ALU.add)
                then2.then_inc(wT_done, 1)
                dve.wait_ge(wT_done, 1)
                nc.vector.reciprocal(rden[:, :], top[:, :]).then_inc(wT_done, 1)
                dve.wait_ge(wT_done, 2)
                then(nc.vector.tensor_tensor(
                    w[:, :, :, :].rearrange("q p e t -> q p t e"),
                    gate[:, :, :].rearrange("q (p t) e -> q p t e", p=PAIRS),
                    rden[:, :].rearrange("q (p t) -> q p t", p=PAIRS).unsqueeze(3).to_broadcast([P, PAIRS, NT // PAIRS, E]),
                    ALU.mult))
                dve.wait_ge(wT_mm, 1)
                nc.vector.tensor_copy(wT[:, :, :], p_wT[:, :, :]).then_inc(wT_done, 1)

            @block.gpsimd
            def _(pool):
                for n, (full, hi, lo) in enumerate(to_split):
                    pool.wait_ge(hi_done, n + 1)
                    lower(nc.gpsimd, lo, full, hi).then_inc(lo_done, 1)

            @block.sync
            def _(sp):
                sp.wait_ge(wT_done, 3)
                sp.dma_start(w_dram.rearrange("p (e t) k -> (e t) p k", e=E), wT[:, :, :]).then_inc(stored, 16)
                sp.wait_ge(stored, 16)


def moe(nc, tag, x, h, w1, b1, w2, b2, w_dram, mod):
    E, K = 8, 4
    U = 2 * E
    with PhaseMemory(nc, tag) as m:
        wb = m.sb("wb", [P, 2, E, TILE])
        wT = m.sb("wT", [E, 2, TILE])
        h_hi = m.sb("h_hi", [P, 2, TILE])
        h_lo = m.sb("h_lo", [P, 2, TILE])
        hid = m.sb("hid", [P, K, TILE])
        hid_hi = m.sb("hid_hi", [P, 2, K, TILE])
        hid_lo = m.sb("hid_lo", [P, 2, K, TILE])
        part = m.sb("part", [P, 2, TILE])
        b2w = m.sb("b2w", [P, 2, TILE])
        acc = m.sb("acc", [P, 2, TILE])
        p_up = m.ps("p_up", [P, K, 512])
        p_dn = m.ps("p_dn", [P, 2, 512])
        p_b = m.ps("p_b", [P, 512])
        w_in = [m.sem(f"w_in{j}") for j in range(2)]
        up_done = m.sem("up_done")
        tick = m.sem("tick")
        hi_done = m.sem("hi_done")
        lo_done = m.sem("lo_done")
        h_hi_done = m.sem("h_hi_done")
        h_done = m.sem("h_done")
        gelu_done = m.sem("gelu_done")
        dn_done = m.sem("dn_done")
        mul_done = m.sem("mul_done")
        add_done = m.sem("add_done")
        b_done = m.sem("b_done")
        b2w_done = m.sem("b2w_done")
        x_done = m.sem("x_done")
        with nc.Block() as block:
            @block.sync
            def _(sp):
                with nc.sync.Fori(0, PAIRS) as p:
                    for j in range(2):
                        sp.wait_ge(x_done, 2 * p + j + 1)
                        src = w_dram[bass.ds(p, 1), :, :].rearrange("p (e t) k -> (p e) (t k)", e=E)[:, j * TILE:(j + 1) * TILE]
                        sp.dma_start(wb[:, j, :, :], src.partition_broadcast(P)).then_inc(w_in[j], 16)
                        sp.dma_start(wT[:, j, :], src).then_inc(w_in[j], 16)

            @block.tensor
            def _(pe):
                nc.tensor.sem_inc(dn_done, 2)

                def up(p, k):
                    j, e = divmod(k, E)
                    if e == 0:
                        pe.wait_ge(h_done, 2 * p + j + 1)
                    for i in range(K):
                        pe.wait_ge(gelu_done, 4 * U * p + 4 * k + i + 1)
                        product(nc, p_up[:, i, :], [z[:, e, i * P:(i + 1) * P] for z in w1], (h_hi[:, j, :], h_lo[:, j, :]),
                                True, True).then_inc(up_done, 1)

                def down(p, k):
                    j, e = divmod(k, E)
                    if e == 0:
                        pe.wait_ge(w_in[j], 32 * p + 32)
                        pe.wait_ge(b2w_done, 2 * p + j + 1)
                        nc.tensor.matmul(p_b[:, :], b2, wT[:, j, :], start=True, stop=True).then_inc(b_done, 1)
                    pe.wait_ge(mul_done, U * p + k + 1)
                    for i in range(K):
                        pe.wait_ge(lo_done, 4 * U * p + 4 * k + i + 5)
                        last = product(nc, p_dn[:, k % 2, :], [z[:, e, i, :] for z in w2],
                                       (hid_hi[:, k % 2, i, :], hid_lo[:, k % 2, i, :]), i == 0, i == K - 1)
                    last.then_inc(dn_done, 1)

                with nc.tensor.Fori(0, PAIRS) as p:
                    up(p, 0)
                    for k in range(U):
                        if k + 1 < U:
                            up(p, k + 1)
                        down(p, k)

            @block.scalar
            def _(act):
                nc.scalar.preload_act_table(ACT.Gelu_apprx_tanh)
                nc.scalar.sem_inc(gelu_done, 4)
                nc.scalar.sem_inc(b2w_done, 1)
                with nc.scalar.Fori(0, PAIRS) as p:
                    for k in range(U):
                        j, e = divmod(k, E)
                        for i in range(K):
                            act.wait_ge(lo_done, 4 * U * p + 4 * k + i + 1)
                            act.wait_ge(up_done, 4 * U * p + 4 * k + i + 1)
                            nc.scalar.activation(hid[:, i, :], p_up[:, i, :], ACT.Gelu_apprx_tanh,
                                                 bias=b1[:, e * K + i:e * K + i + 1]).then_inc(gelu_done, 1)
                        if e == 0:
                            act.wait_ge(b_done, 2 * p + j + 1)
                            act.wait_ge(x_done, 2 * p + j + 1)
                            nc.scalar.activation(b2w[:, j, :], p_b[:, :], ACT.Copy).then_inc(b2w_done, 1)

            @block.vector
            def _(dve):
                nc.vector.sem_inc(mul_done, 2)
                nc.vector.sem_inc(x_done, 2)

                nc.vector.sem_inc(lo_done, 4)

                def split(p, k):
                    if k % E == 0:
                        j = k // E
                        dve.wait_ge(dn_done, U * p + k + 2 - E if j else U * p + 1)
                        nc.vector.sem_inc(tick, 1)
                        upper(nc.vector, h_hi[:, j, :], h[:, cols(2 * p + j)]).then_inc(h_hi_done, 1)
                        dve.wait_ge(h_hi_done, 2 * p + j + 1)
                        lower(nc.vector, h_lo[:, j, :], h[:, cols(2 * p + j)], h_hi[:, j, :]).then_inc(h_done, 1)
                    for i in range(K):
                        n = 4 * U * p + 4 * k + i
                        dve.wait_ge(gelu_done, n + 5)
                        if i == 0:
                            dve.wait_ge(dn_done, U * p + k + 1)
                        upper(nc.vector, hid_hi[:, k % 2, i, :], hid[:, i, :]).then_inc(hi_done, 1)
                        dve.wait_ge(hi_done, n + 1)
                        lower(nc.vector, hid_lo[:, k % 2, i, :], hid[:, i, :], hid_hi[:, k % 2, i, :]).then_inc(lo_done, 1)
                with nc.vector.Fori(0, PAIRS) as p:
                    split(p, 0)
                    for k in range(U):
                        if k + 1 < U:
                            split(p, k + 1)
                        j, e = divmod(k, E)
                        dve.wait_ge(w_in[j], 32 * p + 32)
                        dve.wait_ge(dn_done, U * p + k + 3)
                        dve.wait_ge(add_done, U * p + k + 1)
                        nc.vector.tensor_tensor(part[:, k % 2, :], p_dn[:, k % 2, :], wb[:, j, e, :],
                                                ALU.mult).then_inc(mul_done, 1)
                        if e == E - 1:
                            dve.wait_ge(add_done, U * p + k + 3)
                            nc.vector.scalar_tensor_tensor(
                                out=x[:, cols(2 * p + j)], in0=acc[:, j, :], scalar=mod[:, 5, bass.ds(p, 1)],
                                in1=x[:, cols(2 * p + j)], op0=ALU.mult, op1=ALU.add).then_inc(x_done, 1)

            @block.gpsimd
            def _(pool):
                nc.gpsimd.sem_inc(add_done, 2)
                with nc.gpsimd.Fori(0, PAIRS) as p:
                    for k in range(U):
                        j, e = divmod(k, E)
                        pool.wait_ge(mul_done, U * p + k + 3)
                        pool.wait_ge(add_done, U * p + k + 2)
                        if e == 0:
                            pool.wait_ge(b2w_done, 2 * p + j + 2)
                            pool.wait_ge(x_done, 2 * p + j + 1)
                        nc.gpsimd.tensor_tensor(acc[:, j, :], b2w[:, j, :] if e == 0 else acc[:, j, :], part[:, k % 2, :],
                                                ALU.add).then_inc(add_done, 1)


HB = 16
DH = P // HB
VW = HB * (DH + 1)
QT = P
NG4 = 4
NQ = T // QT
MASKED = -1e30


def rope_qkv(nc, tag, h, qkv_w, rope, q, k, v, vg, hm):
    with PhaseMemory(nc, tag) as m:
        hs = m.sb("hs", [P, 2, TILE])
        hg = m.sb("hg", [P, HB // 2, NG4])
        turned = m.sb("turned", [P, 4, TILE])
        p_qk = m.ps("p_qk", [P, 4, 512])
        p_v = m.ps("p_v", [P, 4, P])
        p_g = m.ps("p_g", [32, P])
        pads = m.sem("pads")
        hs_done = m.sem("hs_done")
        hg_done = m.sem("hg_done")
        qk_mm = m.sem("qk_mm")
        v_mm = m.sem("v_mm")
        g_mm = m.sem("g_mm")
        turned_done = m.sem("turned_done")
        sum_done = m.sem("sum_done")
        v_done = m.sem("v_done")
        g_done = m.sem("g_done")
        with nc.Block() as block:
            @block.tensor
            def _(pe):
                nc.tensor.sem_inc(v_mm, 2)
                nc.tensor.sem_inc(g_mm, 1)
                with nc.tensor.Fori(0, PAIRS) as p:
                    for j in range(2):
                        t = 2 * p + j
                        for r in range(4):
                            pe.wait_ge(turned_done, 4 * t + r + 1)
                            nc.tensor.matmul(p_qk[:, r, :], qkv_w[:, r * P:(r + 1) * P], h[:, cols(t)],
                                             start=True, stop=True).then_inc(qk_mm, 1)
                        pe.wait_ge(hs_done, t + 1)
                        pe.wait_ge(v_done, t + 1)
                        for a in range(4):
                            last = nc.tensor.matmul(p_v[:, a, :], hs[:, j, a * P:(a + 1) * P], qkv_w[:, 4 * P:5 * P],
                                                    start=True, stop=True)
                        last.then_inc(v_mm, 1)
                        if j == 0:
                            pe.wait_ge(hg_done, p + 1)
                            pe.wait_ge(g_done, p + 1)
                            nc.tensor.matmul(p_g[:, :], hg[:, :, :].rearrange("q h j -> q (h j)"), qkv_w[:, 4 * P:5 * P],
                                             start=True, stop=True).then_inc(g_mm, 1)

            @block.scalar
            def _(act):
                nc.scalar.sem_inc(v_done, 1)
                act.wait_ge(pads, 5)
                with nc.scalar.Fori(0, PAIRS) as p:
                    for j in range(2):
                        t = 2 * p + j
                        act.wait_ge(v_mm, t + 1)
                        nc.scalar.activation(hs[:, j, :], h[:, cols(t)], ACT.Copy).then_inc(hs_done, 1)
                        if j == 0:
                            act.wait_ge(hs_done, t + 1)
                            act.wait_ge(g_mm, p + 1)
                            nc.scalar.activation(hg[:, :, :], hs[:, 0, 0:NG4].unsqueeze(1).to_broadcast([P, HB // 2, NG4]),
                                                 ACT.Copy).then_inc(hg_done, 1)
                        act.wait_ge(v_mm, t + 3)
                        nc.scalar.activation(
                            v[:, bass.ds(4 * t + 1, 4), :].rearrange("q t (h d) -> q (t h) d", d=DH + 1)[:, :, 0:DH],
                            p_v[:, :, :].rearrange("q t (h d) -> q (t h) d", d=DH), ACT.Copy).then_inc(v_done, 1)

            @block.vector
            def _(dve):
                nc.vector.memset(k[:, 0:QT], 0.0).then_inc(pads, 1)
                nc.vector.memset(k[:, QT + T:2 * QT + T], 0.0).then_inc(pads, 1)
                nc.vector.memset(q[:, T:T + QT], 0.0).then_inc(pads, 1)
                nc.vector.memset(v[:, :, :], 1.0).then_inc(pads, 1)
                nc.vector.memset(turned[:, 0, 0:1], 0.0).then_inc(pads, 1)
                dve.wait_ge(pads, 5)
                nc.vector.sem_inc(turned_done, 4)
                nc.vector.sem_inc(g_done, 1)
                with nc.vector.Fori(0, PAIRS) as p:
                    for j in range(2):
                        t = 2 * p + j
                        for r in range(4):
                            dve.wait_ge(qk_mm, 4 * t + r + 1)
                            dve.wait_ge(sum_done, 2 * t + r // 2 + 1)
                            nc.vector.tensor_tensor(turned[:, r, :], p_qk[:, r, :], rope[:, r, j * TILE:(j + 1) * TILE],
                                                    ALU.mult).then_inc(turned_done, 1)
                        if j == 0:
                            dve.wait_ge(g_mm, p + 2)
                            for a in range(2):
                                last = nc.vector.tensor_tensor(
                                    vg[:, a, bass.ds(p, 1), :].rearrange("q b (h d) -> q (b h) d", d=DH + 1)[:, :, 0:DH],
                                    p_g[:, 8 * a * DH:8 * (a + 1) * DH].rearrange("q (h d) -> q h d", d=DH),
                                    hm.unsqueeze(2).to_broadcast([32, 8, DH]), ALU.mult)
                            last.then_inc(g_done, 1)

            @block.gpsimd
            def _(pool):
                nc.gpsimd.sem_inc(sum_done, 2)
                pool.wait_ge(pads, 5)
                with nc.gpsimd.Fori(0, PAIRS) as p:
                    for j in range(2):
                        t = 2 * p + j
                        for r, dst in ((0, q[:, cols(t)]), (1, k[:, bass.ds(QT + t * TILE, TILE)])):
                            pool.wait_ge(turned_done, 4 * t + 2 * r + 6)
                            nc.gpsimd.tensor_tensor(dst, turned[:, 2 * r, :], turned[:, 2 * r + 1, :],
                                                    ALU.add).then_inc(sum_done, 1)


def band_attention(nc, tag, q, k, v, vg, cc, masks, ident, oT):
    KW = 2 * QT
    H2 = HB // 2
    GW = H2 * (DH + 1)
    head_mask, table_mask = cc[:, 0:HB], cc[:, HB + 8:HB + 8 + NQ]
    with PhaseMemory(nc, tag) as m:
        qm = m.sb("qm", [P, HB, QT])
        qs = m.sb("qs", [P, QT])
        kg = m.sb("kg", [P, NQ, HB, NG4])
        vgt = m.sb("vgt", [32, 2, NQ, GW])
        mask = m.sb("mask", [P, 2, KW])
        gs = m.sb("gs", [P, 2, HB, NG4])
        gmin = m.sb("gmin", [P, 2, HB])
        gd = m.sb("gd", [P, 2, H2, NG4])
        pg = m.sb("pg", [P, 2, H2, NG4])
        ms = m.sb("ms", [P, 4, KW])
        nmx = m.sb("nmx", [P, HB])
        pr = m.sb("pr", [P, HB, KW])
        prT = m.sb("prT", [P, 2, 2, KW])
        pgT = m.sb("pgT", [32, 2, QT])
        rs = m.sb("rs", [P, 2, H2])
        on = m.sb("on", [P, HB, DH])
        p_s = m.ps("p_s", [P, 2, 512])
        p_t = m.ps("p_t", [P, 2, 512])
        p_g = m.ps("p_g", [32, 512])
        p_o = m.ps("p_o", [P, 2, 512])
        p_x = m.ps("p_x", [P, 512])
        tick = m.sem("tick")
        setup_done = m.sem("setup_done")
        qm_done = m.sem("qm_done")
        qs_done = m.sem("qs_done")
        sg_done = m.sem("sg_done")
        gs_done = m.sem("gs_done")
        gmin_done = m.sem("gmin_done")
        mask_done = m.sem("mask_done")
        gd_done = m.sem("gd_done")
        pg_done = m.sem("pg_done")
        s_done = m.sem("s_done")
        max_done = m.sem("max_done")
        exp_done = m.sem("exp_done")
        t_done = m.sem("t_done")
        ev_done = [m.sem("ev_act"), m.sem("ev_dve")]
        av_done = m.sem("av_done")
        gT_done = m.sem("gT_done")
        gc_done = m.sem("gc_done")
        ag_done = m.sem("ag_done")
        rs_done = m.sem("rs_done")
        on_done = m.sem("on_done")
        ot_done = m.sem("ot_done")
        oc_done = m.sem("oc_done")

        def tiles(eng, body):
            body(0, 0, True, False)
            with eng.Fori(0, NQ // 2 - 1) as gg:
                body(2 * gg + 1, 1, False, False)
                body(2 * gg + 2, 0, False, False)
            body(NQ - 1, 1, False, True)

        with nc.Block() as block:
            @block.gpsimd
            def _(pool):
                def mask_queries(g, a):
                    pool.wait_ge(s_done, HB * g + H2 * a + H2)
                    nc.gpsimd.sem_inc(tick, 1)
                    nc.gpsimd.tensor_tensor(
                        qm[:, H2 * a:H2 * (a + 1), :], q[:, bass.ds(g * QT, QT)].unsqueeze(1).to_broadcast([P, H2, QT]),
                        head_mask[:, H2 * a:H2 * (a + 1)].unsqueeze(2).to_broadcast([P, H2, QT]),
                        ALU.mult).then_inc(qm_done, 1)

                def copy_queries(g):
                    pool.wait_ge(sg_done, g)
                    nc.gpsimd.sem_inc(tick, 1)
                    nc.gpsimd.tensor_copy(qs[:, :], q[:, bass.ds(g * QT, QT)]).then_inc(qs_done, 1)

                def body(g, par, first, last):
                    if not last:
                        mask_queries(g + 1, 0)
                        copy_queries(g + 2)
                        mask_queries(g + 1, 1)

                nc.gpsimd.tensor_copy(qs[:, :], q[:, 0:QT]).then_inc(qs_done, 1)
                for b in range(NB):
                    nc.gpsimd.tensor_tensor(
                        kg[:, 8 * b:8 * b + 8, :, :],
                        k[:, QT + b * L:QT + b * L + NG4].unsqueeze(1).unsqueeze(2).to_broadcast([P, 8, HB, NG4]),
                        head_mask.unsqueeze(1).unsqueeze(3).to_broadcast([P, 8, HB, NG4]), ALU.mult
                    ).then_inc(setup_done, 1)
                    if b == 0:
                        mask_queries(0, 0)
                        mask_queries(0, 1)
                copy_queries(1)
                tiles(nc.gpsimd, body)

            @block.tensor
            def _(pe):
                nc.tensor.sem_inc(s_done, HB)
                nc.tensor.sem_inc(t_done, HB)
                nc.tensor.sem_inc(av_done, 4)
                nc.tensor.sem_inc(gT_done, 2)
                nc.tensor.sem_inc(ag_done, 2)
                nc.tensor.sem_inc(ot_done, 1)

                def scores(g, hd):
                    if hd % H2 == 0:
                        pe.wait_ge(qm_done, 2 * g + hd // H2 + 1)
                    if hd % 2 == 0:
                        pe.wait_ge(max_done, HB * g + hd + 2)
                    nc.tensor.matmul(p_s[:, hd // 2 % 2, hd % 2 * KW:(hd % 2 + 1) * KW], qm[:, hd, :], k[:, bass.ds(g * QT, KW)],
                                     start=True, stop=True).then_inc(s_done, 1)

                def scores_global(g):
                    pe.wait_ge(qs_done, g + 1)
                    pe.wait_ge(oc_done, g)
                    nc.tensor.matmul(p_x[:, 0:HB * NG4], qs[:, :],
                                     kg[:, bass.ds(g, 1), :, :].rearrange("q t h j -> q (t h j)"),
                                     start=True, stop=True).then_inc(sg_done, 1)

                def turn(g, hd):
                    pe.wait_ge(exp_done, HB * g + hd + 5)
                    if hd % 2 == 0:
                        pe.wait_ge(ev_done[hd // 2 % 2], 4 * g + hd // 4 + 1)
                    for a in range(2):
                        last = nc.tensor.transpose(p_t[:, hd // 2 % 2, (2 * (hd % 2) + a) * QT:(2 * (hd % 2) + a + 1) * QT],
                                                   pr[:, hd, a * QT:(a + 1) * QT], ident)
                    last.then_inc(t_done, 1)

                def values(g, hd):
                    if hd % 2 == 0:
                        pe.wait_ge(ev_done[hd // 2 % 2], 4 * g + hd // 4 + 2)
                    if hd % H2 == 0:
                        pe.wait_ge(on_done, 2 * g + hd // H2 + 1)
                    for a in range(2):
                        last = nc.tensor.matmul(p_o[:, hd // H2, hd % H2 * (DH + 1):(hd % H2 + 1) * (DH + 1)],
                                                prT[:, hd // 2 % 2, hd % 2, a * QT:(a + 1) * QT],
                                                v[:, bass.ds(g + a, 1), hd * (DH + 1):(hd + 1) * (DH + 1)].rearrange(
                                                    "q t d -> q (t d)"),
                                                start=hd % H2 == 0 and a == 0, stop=False, skip_group_check=True)
                    last.then_inc(av_done, 1)

                def turn_global(g, a):
                    pe.wait_ge(pg_done, 2 * g + a + 3)
                    pe.wait_ge(gc_done, 2 * g + a + 1)
                    nc.tensor.transpose(p_g[:, 0:QT], pg[:, a, :, :].rearrange("q h j -> q (h j)"), ident
                                        ).then_inc(gT_done, 1)

                def values_global(g, a):
                    pe.wait_ge(gc_done, 2 * g + a + 2)
                    nc.tensor.sem_inc(tick, 1)
                    nc.tensor.matmul(p_o[:, a, 0:GW], pgT[:, a, :],
                                     vgt[:, a, bass.ds(g, 1), :].rearrange("q t d -> q (t d)"),
                                     start=False, stop=True, skip_group_check=True).then_inc(ag_done, 1)

                def turn_out(g, ahead):
                    pe.wait_ge(on_done, 2 * g + 4)
                    pe.wait_ge(gs_done, g + 1 + ahead)
                    nc.tensor.transpose(p_x[:, 0:QT], on[:, :, :].rearrange("q h d -> q (h d)"), ident).then_inc(ot_done, 1)

                def before(g, m, ahead):
                    if m == 0:
                        values(g, HB - 2)
                        values(g, HB - 1)
                    if m == 1:
                        turn_global(g, 1)
                    if m == 3:
                        values_global(g, 1)
                    if m == 5:
                        turn_out(g, ahead)

                def body(g, par, first, last):
                    for m in range(HB // 2):
                        for e in range(2):
                            if m + 2 < HB // 2:
                                scores(g, 2 * m + 4 + e)
                            elif not last:
                                scores(g + 1, 2 * m + 4 + e - HB)
                        turn(g, 2 * m)
                        turn(g, 2 * m + 1)
                        if m > 0:
                            values(g, 2 * m - 2)
                            values(g, 2 * m - 1)
                        if not first:
                            before(g - 1, m, 1 if last else 2)
                        if m == 1 and not last:
                            scores_global(g + 1)
                        if m == 4:
                            turn_global(g, 0)
                        if m == 6:
                            values_global(g, 0)

                pe.wait_ge(setup_done, 2 * NB)
                scores_global(0)
                scores(0, 0)
                scores(0, 1)
                scores(0, 2)
                scores(0, 3)
                tiles(nc.tensor, body)
                for m in range(6):
                    before(NQ - 1, m, 0)

            @block.scalar
            def _(act):
                nc.scalar.preload_act_table_set(LN_EXP)
                nc.scalar.sem_inc(exp_done, 4)
                nc.scalar.sem_inc(pg_done, 2)
                nc.scalar.sem_inc(ev_done[0], 1)
                for b in range(NB):
                    nc.scalar.activation(vgt[:, :, 8 * b:8 * b + 8, :], vg[:, :, b, :].unsqueeze(2).to_broadcast([32, 2, 8, GW]),
                                         ACT.Copy).then_inc(setup_done, 1)

                def exp_global(g, a):
                    act.wait_ge(gd_done, 2 * g + a + 1)
                    act.wait_ge(gT_done, 2 * g + a + 1)
                    nc.scalar.activation(pg[:, a, :, :], gd[:, a, :, :], ACT.Exp, scale=-1.0).then_inc(pg_done, 1)

                def leave_out(g):
                    act.wait_ge(ot_done, g + 2)
                    nc.scalar.sem_inc(tick, 1)
                    nc.scalar.activation(oT[:, bass.ds(g * QT, QT)], p_x[:, 0:QT], ACT.Copy).then_inc(oc_done, 1)

                def evacuate(g, mm):
                    act.wait_ge(t_done, HB * g + 2 * mm + 2 + HB)
                    act.wait_ge(av_done, HB * g + 2 * mm + 2)
                    nc.scalar.activation(prT[:, 0, :, :].rearrange("q a n -> q (a n)"), p_t[:, 0, :], ACT.Copy
                                         ).then_inc(ev_done[0], 1)

                def body(g, par, first, last):
                    for s in range(HB):
                        act.wait_ge(max_done, HB * g + s + 5)
                        act.wait_ge(t_done, HB * g + s + 1)
                        nc.scalar.activation(pr[:, s, :], ms[:, s % 4, :], ACT.Exp, bias=nmx[:, s:s + 1],
                                             scale=-1.0).then_inc(exp_done, 1)
                        if s % 4 == 2:
                            evacuate(g, s // 2 - 1)
                        if s == 0 and not first:
                            exp_global(g - 1, 1)
                        if s == 8:
                            exp_global(g, 0)
                        if s == 12 and not first:
                            leave_out(g - 1)

                nc.scalar.sem_inc(oc_done, 2)
                tiles(nc.scalar, body)
                exp_global(NQ - 1, 1)
                leave_out(NQ - 1)

            @block.vector
            def _(dve):
                nc.vector.sem_inc(max_done, 4)
                nc.vector.sem_inc(ev_done[1], 1)
                nc.vector.sem_inc(gc_done, 1)
                nc.vector.sem_inc(on_done, 2)

                def prepare(g, par, early):
                    if not early:
                        dve.wait_ge(gd_done, 2 * g - 2)
                        dve.wait_ge(max_done, HB * g + 4 - HB)
                    dve.wait_ge(sg_done, g + 1)
                    nc.vector.tensor_scalar(gs[:, par, :, :].rearrange("q h j -> q (h j)"), p_x[:, 0:HB * NG4],
                                            table_mask[:, bass.ds(g, 1)], -1.0, ALU.add, ALU.mult).then_inc(gs_done, 1)
                    nc.vector.tensor_copy(mask[:, par, :], masks[:, bass.ds(g, 1), :].rearrange("q t n -> q (t n)")
                                          ).then_inc(mask_done, 1)
                    dve.wait_ge(gs_done, g + 1)
                    nc.vector.tensor_reduce(out=gmin[:, par, :], in_=gs[:, par, :, :], axis=AX_X, op=ALU.min
                                            ).then_inc(gmin_done, 1)

                def subtract(g, par, a):
                    dve.wait_ge(max_done, HB * g + H2 * a + H2 + 4)
                    dve.wait_ge(pg_done, 2 * g + a + 1)
                    h = slice(H2 * a, H2 * (a + 1))
                    nc.vector.tensor_tensor(gd[:, a, :, :], gs[:, par, h, :], nmx[:, h].unsqueeze(2).to_broadcast([P, H2, NG4]),
                                            ALU.subtract).then_inc(gd_done, 1)

                def evacuate(g, mm):
                    dve.wait_ge(t_done, HB * g + 2 * mm + 2 + HB)
                    dve.wait_ge(av_done, HB * g + 2 * mm + 2)
                    nc.vector.tensor_copy(prT[:, 1, :, :].rearrange("q a n -> q (a n)"), p_t[:, 1, :]).then_inc(ev_done[1], 1)

                def leave_global(g, a):
                    dve.wait_ge(gT_done, 2 * g + a + 3)
                    dve.wait_ge(ag_done, 2 * g + a + 1)
                    nc.vector.tensor_copy(pgT[:, a, :], p_g[:, 0:QT]).then_inc(gc_done, 1)

                def normalise(g, a):
                    dve.wait_ge(av_done, HB * g + H2 * a + H2 + 4)
                    dve.wait_ge(ag_done, 2 * g + a + 3)
                    dve.wait_ge(on_done, 2 * g + a + 1)
                    o = p_o[:, a, 0:GW].rearrange("q (h d) -> q h d", d=DH + 1)
                    nc.vector.reciprocal(rs[:, a, :], o[:, :, DH]).then_inc(rs_done, 1)
                    dve.wait_ge(rs_done, 2 * g + a + 1)
                    dve.wait_ge(ot_done, g + 1)
                    nc.vector.tensor_tensor(on[:, H2 * a:H2 * (a + 1), :], o[:, :, 0:DH],
                                            rs[:, a, :].unsqueeze(2).to_broadcast([P, H2, DH]), ALU.mult).then_inc(on_done, 1)

                def before(g, s):
                    if s == 1:
                        evacuate(g, HB // 2 - 1)
                    if s == 5:
                        leave_global(g, 1)
                    if s == 9:
                        normalise(g, 1)

                def body(g, par, first, last):
                    dve.wait_ge(gmin_done, g + 1)
                    dve.wait_ge(mask_done, g + 1)
                    for s in range(HB):
                        if s % 2 == 0:
                            dve.wait_ge(s_done, HB * g + s + HB + 2)
                        dve.wait_ge(exp_done, HB * g + s + 1)
                        nc.vector.sem_inc(tick, 1)
                        nc.vector.tensor_tensor_reduce(ms[:, s % 4, :], p_s[:, s // 2 % 2, s % 2 * KW:(s % 2 + 1) * KW], mask[:, par, :], -1.0,
                                                       gmin[:, par, s:s + 1], ALU.add, ALU.min, nmx[:, s:s + 1]
                                                       ).then_inc(max_done, 1)
                        if s % 4 == 1 and s > 1:
                            evacuate(g, (s - 3) // 2)
                        if not first:
                            before(g - 1, s)
                        if s == H2 - 1:
                            subtract(g, par, 0)
                            if not last:
                                prepare(g + 1, 1 - par, first)
                        if s == 11:
                            leave_global(g, 0)
                    subtract(g, par, 1)
                    normalise(g, 0)

                prepare(0, 0, True)
                tiles(nc.vector, body)
                for s in range(10):
                    before(NQ - 1, s)


def out_project(nc, tag, x, oT, off, w, mod_gate):
    with PhaseMemory(nc, tag) as m:
        p_o = m.ps("p_o", [P, 2, 512])
        mm_done = m.sem("mm_done")
        x_done = m.sem("x_done")
        with nc.Block() as block:
            @block.tensor
            def _(pe):
                with nc.tensor.Fori(0, PAIRS) as p:
                    for j in range(2):
                        pe.wait_ge(x_done, 2 * p + j + 1)
                        nc.tensor.matmul(p_o[:, j, :], w, oT[:, bass.ds(off + (2 * p + j) * TILE, TILE)],
                                         start=True, stop=True).then_inc(mm_done, 1)

            @block.vector
            def _(dve):
                nc.vector.sem_inc(x_done, 2)
                with nc.vector.Fori(0, PAIRS) as p:
                    for j in range(2):
                        dve.wait_ge(mm_done, 2 * p + j + 1)
                        xt = x[:, cols(2 * p + j)]
                        nc.vector.scalar_tensor_tensor(out=xt, in0=p_o[:, j, :], scalar=mod_gate(p), in1=xt, op0=ALU.mult,
                                                       op1=ALU.add).then_inc(x_done, 1)


HF = 8
DF = 64
WIN = 64
VF = HF * (DF + 1)
HID = 341
HR = HID - 2 * P
LN_SCALE = 65536.0
TINY = 1e-24


def shifted_copy(nc, tag, y, sh):
    with PhaseMemory(nc, tag) as m:
        done = m.sem("done")
        zero = m.sem("zero")
        with nc.Block() as block:
            @block.scalar
            def _(act):
                for b in range(NB):
                    lo = b * L
                    nc.scalar.activation(sh[0:64, lo:lo + L], y[0:64, lo:lo + L], ACT.Copy).then_inc(done, 1)

            @block.vector
            def _(dve):
                for b in range(NB):
                    lo = b * L
                    nc.vector.memset(sh[64:P, lo:lo + 1], 0.0).then_inc(zero, 1)
                    nc.vector.tensor_copy(sh[64:P, lo + 1:lo + L], y[64:P, lo:lo + L - 1]).then_inc(done, 1)


def local_attention(nc, tag, W, y, sh, tables, blocks, ident, head_mask, masks, norm_bias):
    NU = 16
    NI = L // QT
    KW = 2 * WIN
    VP = 2 * (DF + 1)
    with PhaseMemory(nc, tag) as m:
        q = m.sb("q", [P, 4, L])
        k = m.sb("k", [P, 4, QT + L])
        v = m.sb("v", [P, NI, VF])
        v_mid = m.sb("v_mid", [P, NI, VF])
        oT = m.sb("oT", [P, 4, L])
        sh_hi = m.sb("sh_hi", [P, 2, TILE])
        sh_lo = m.sb("sh_lo", [P, 2, TILE])
        sq = m.sb("sq", [P, 2, TILE])
        turned = oT[:, 0:2, :].rearrange("q e (a n) -> q e a n", a=2)
        ss = m.sb("ss", [P, 2, TILE])
        lns = m.sb("lns", [P, 2, TILE])
        rn = m.sb("rn", [P, 2, TILE])
        tsum = oT[:, 2:4, :].rearrange("q e (a n) -> q (e a) n", a=2)
        qm = lns[:, :, :].rearrange("q j (h n) -> q (j h) n", n=QT)
        ms = m.sb("ms", [P, 4, KW])
        nmx = m.sb("nmx", [P, HF])
        pr = ss[:, :, :].rearrange("q j (h n) -> q (j h) n", n=KW)
        prT = sq
        on = rn[:, 0, :].rearrange("q (h d) -> q h d", d=DF)
        rs = m.sb("rs", [P, 4])
        bank = [m.ps(f"bank{n}", [P, 512]) for n in range(8)]

        init = m.sem("init")
        tick = m.sem("tick")
        pq_done = m.sem("pq_done")
        sq_done = m.sem("sq_done")
        ss_mm = m.sem("ss_mm")
        ss_done = m.sem("ss_done")
        ln_done = m.sem("ln_done")
        rn_done = m.sem("rn_done")
        turned_done = m.sem("turned_done")
        sum_done = m.sem("sum_done")
        qk_done = [m.sem("qk_dve"), m.sem("qk_pool")]
        hi_done = m.sem("hi_done")
        parts_done = m.sem("parts_done")
        v_mm = m.sem("v_mm")
        v_done = m.sem("v_done")
        mid_done = m.sem("mid_done")
        qm_done = m.sem("qm_done")
        s_done = m.sem("s_done")
        max_done = m.sem("max_done")
        exp_done = m.sem("exp_done")
        t_done = m.sem("t_done")
        ev_done = [m.sem("ev_act"), m.sem("ev_dve")]
        av_done = m.sem("av_done")
        rs_done = m.sem("rs_done")
        on_done = m.sem("on_done")
        ot_done = m.sem("ot_done")
        oc_done = m.sem("oc_done")
        wo_mm = m.sem("wo_mm")
        y_done = m.sem("y_done")
        units = [(j, r, z) for j in range(2) for z in range(2) for r in range(4)]

        def rotated(n):
            j, r, z = units[n]
            return q[:, r, j * TILE:(j + 1) * TILE] if z == 0 else k[:, r, QT + j * TILE:QT + (j + 1) * TILE]

        def tiles(eng, b, body):
            body(b, NI * b, 0, 0)
            body(b, NI * b + 1, 1, 1)
            with eng.Fori(2, NI - 1) as i:
                body(b, NI * b + i, i, 2)
            body(b, NI * b + NI - 1, NI - 1, 3)

        with nc.Block() as block:
            @block.tensor
            def _(pe):
                nc.tensor.sem_inc(ss_mm, 2)
                nc.tensor.sem_inc(v_mm, 8)
                nc.tensor.sem_inc(s_done, HF)
                nc.tensor.sem_inc(t_done, 2)
                nc.tensor.sem_inc(av_done, 4)
                nc.tensor.sem_inc(wo_mm, 2)

                def project(b, n):
                    j, r, z = units[n]
                    pe.wait_ge(sq_done, NU * b + n + 1)
                    pe.wait_ge(turned_done, NU * b + n + 1)
                    if n == 0:
                        pe.wait_ge(y_done, 2 * b + 2)
                        pe.wait_ge(parts_done, 2 * b + 1)
                    if n == NU // 2:
                        pe.wait_ge(parts_done, 2 * b + 2)
                    for a in range(2):
                        last = product(nc, bank[2 * a + n % 2][:, :], [w[:, 2 * z + a, r * P:(r + 1) * P] for w in W["qk"]],
                                       (sh_hi[:, j, :], sh_lo[:, j, :]), True, True)
                    last.then_inc(pq_done, 1)

                def squares(b, n):
                    pe.wait_ge(sq_done, NU * b + n + 3)
                    pe.wait_ge(ss_done, NU * b + n + 1)
                    nc.tensor.matmul(bank[4 + n % 2][:, :], blocks, sq[:, n % 2, :], start=True, stop=True).then_inc(ss_mm, 1)

                def scores(g, i, e):
                    pe.wait_ge(qm_done, 2 * g + e + 1)
                    pe.wait_ge(max_done, HF * g + 4 * e + 4)
                    for r in range(4):
                        nc.tensor.matmul(bank[e][:, r * KW:(r + 1) * KW], qm[:, 4 * e + r, :],
                                         k[:, r, bass.ds(i * QT + QT - WIN + e * WIN, KW)],
                                         start=True, stop=True).then_inc(s_done, 1)

                def turn(g, e):
                    pe.wait_ge(exp_done, HF * g + 4 * e + 8)
                    pe.wait_ge(ev_done[e], g + 1)
                    for r in range(4):
                        last = nc.tensor.transpose(bank[2 + e][:, r * QT:(r + 1) * QT], pr[:, 4 * e + r, :], ident)
                    last.then_inc(t_done, 1)

                def values(g, i, e):
                    pe.wait_ge(ev_done[e], g + 2)
                    for a in range(2):
                        pe.wait_ge(on_done, 4 * g + 2 * e + a + 1)
                        for r in range(2 * a, 2 * a + 2):
                            last = nc.tensor.matmul(bank[4 + a][:, r % 2 * VP:(r % 2 + 1) * VP], prT[:, e, r * QT:(r + 1) * QT],
                                                    (v if e else v_mid)[:, bass.ds(i, 1), r * VP:(r + 1) * VP].rearrange(
                                                        "q t d -> q (t d)"), start=True, stop=True)
                        last.then_inc(av_done, 1)

                def turn_out(g):
                    pe.wait_ge(on_done, 4 * g + 6)
                    pe.wait_ge(oc_done, g + 1)
                    for r in range(4):
                        last = nc.tensor.transpose(bank[6][:, r * QT:(r + 1) * QT],
                                                   on[:, 2 * r:2 * r + 2, :].rearrange("q h d -> q (h d)"), ident)
                    last.then_inc(ot_done, 1)

                def body(b, g, i, where):
                    for e in range(2):
                        if where < 3:
                            scores(g + 1, i + 1, e)
                        turn(g, e)
                        if e == 1:
                            values(g, i, 0)
                        elif where > 0:
                            values(g - 1, i - 1, 1)
                    if where > 0:
                        turn_out(g - 1)
                    if where == 3:
                        values(g, i, 1)
                        turn_out(g)

                with nc.tensor.Fori(0, NB) as b:
                    project(b, 0)
                    for n in range(NU):
                        if n + 1 < NU:
                            project(b, n + 1)
                        squares(b, n)
                    for t in range(NI):
                        pe.wait_ge(v_done, NI * b + t + 1)
                        product(nc, bank[6 + t % 2][:, :], [x[:, t // 4, t % 4 * P:(t % 4 + 1) * P] for x in (sh_hi, sh_lo)],
                                W["v"], True, True).then_inc(v_mm, 1)
                    for s in qk_done:
                        pe.wait_ge(s, NU // 2 * (b + 1) + 2)
                    pe.wait_ge(v_done, NI * b + NI + 2)
                    pe.wait_ge(mid_done, (2 * NI - 1) * (b + 1))
                    for e in range(2):
                        scores(NI * b, 0, e)
                    tiles(nc.tensor, b, body)
                    for j in range(2):
                        pe.wait_ge(oc_done, NI * b + (NI // 2) * (j + 1) + 1)
                        for r in range(4):
                            last = nc.tensor.matmul(bank[7 - j][:, :], W["wo"][:, r, :], oT[:, r, j * TILE:(j + 1) * TILE],
                                                    start=r == 0, stop=r == 3)
                        last.then_inc(wo_mm, 1)

            @block.scalar
            def _(act):
                nc.scalar.sem_inc(sq_done, 2)
                nc.scalar.sem_inc(ln_done, 2)
                nc.scalar.sem_inc(rn_done, 2)
                nc.scalar.sem_inc(v_done, 2)
                nc.scalar.sem_inc(exp_done, 4)
                nc.scalar.sem_inc(ev_done[0], 1)
                nc.scalar.sem_inc(oc_done, 1)
                act.wait_ge(init, 3)

                def square(b, n):
                    act.wait_ge(pq_done, NU * b + n + 1)
                    act.wait_ge(ss_mm, NU * b + n + 1)
                    nc.scalar.activation(sq[:, n % 2, :], bank[n % 2][:, :], ACT.Square).then_inc(sq_done, 1)

                def inverse_norm(b, n):
                    act.wait_ge(ss_done, NU * b + n + 3)
                    act.wait_ge(rn_done, NU * b + n + 1)
                    nc.scalar.activation(lns[:, n % 2, :], ss[:, n % 2, :], ACT.Ln, scale=LN_SCALE).then_inc(ln_done, 1)
                    act.wait_ge(ln_done, NU * b + n + 3)
                    act.wait_ge(qk_done[n % 2], NU // 2 * b + n // 2 + 2)
                    nc.scalar.activation(rn[:, n % 2, :], lns[:, n % 2, :], ACT.Exp, scale=-0.5,
                                         bias=norm_bias).then_inc(rn_done, 1)

                def evacuate(g):
                    act.wait_ge(t_done, 2 * g + 3)
                    act.wait_ge(av_done, 4 * g + 2)
                    nc.scalar.activation(prT[:, 0, :], bank[2][:, :], ACT.Copy).then_inc(ev_done[0], 1)

                def leave_out(g, i):
                    act.wait_ge(ot_done, g + 1)
                    nc.scalar.sem_inc(tick, 1)
                    nc.scalar.activation(oT[:, :, bass.ds(i * QT, QT)],
                                         bank[6][:, :].rearrange("q (r n) -> q r n", r=4), ACT.Copy).then_inc(oc_done, 1)

                def body(b, g, i, where):
                    for s in range(HF):
                        act.wait_ge(max_done, HF * g + s + 9)
                        act.wait_ge(t_done, 2 * g + s // 4 + 1)
                        nc.scalar.activation(pr[:, s, :], ms[:, s % 4, :], ACT.Exp, bias=nmx[:, s:s + 1],
                                             scale=-1.0).then_inc(exp_done, 1)
                        if s == 3 and where > 1:
                            leave_out(g - 2, i - 2)
                        if s == 5:
                            evacuate(g)
                    if where == 3:
                        leave_out(g - 1, i - 1)
                        leave_out(g, i)

                with nc.scalar.Fori(0, NB) as b:
                    nc.scalar.preload_act_table_set(LN_EXP)
                    square(b, 0)
                    square(b, 1)
                    for n in range(NU):
                        if n + 2 < NU:
                            square(b, n + 2)
                        inverse_norm(b, n)
                    for t in range(NI):
                        act.wait_ge(v_mm, NI * b + t + NI + 1)
                        nc.scalar.activation(v[:, t, :].rearrange("q (h d) -> q h d", d=DF + 1)[:, :, 0:DF],
                                             bank[6 + t % 2][:, :].rearrange("q (h d) -> q h d", d=DF),
                                             ACT.Copy).then_inc(v_done, 1)
                    tiles(nc.scalar, b, body)

            @block.vector
            def _(dve):
                nc.vector.memset(k[:, :, 0:QT], 0.0).then_inc(init, 1)
                nc.vector.memset(v[:, :, :], 1.0).then_inc(init, 1)
                nc.vector.memset(v_mid[:, :, :], 1.0).then_inc(init, 1)
                dve.wait_ge(init, 3)
                nc.vector.sem_inc(turned_done, 2)
                nc.vector.sem_inc(qk_done[0], 2)
                nc.vector.sem_inc(ss_done, 2)
                nc.vector.sem_inc(max_done, 8)
                nc.vector.sem_inc(ev_done[1], 1)
                nc.vector.sem_inc(on_done, 2)
                nc.vector.sem_inc(y_done, 2)

                def rotate(b, n):
                    j, r, z = units[n]
                    dve.wait_ge(pq_done, NU * b + n + 1)
                    dve.wait_ge(sum_done, NU * b + n + 1)
                    for a in (1, 0):
                        if a == 0:
                            dve.wait_ge(sq_done, NU * b + n + 3)
                        last = nc.vector.scalar_tensor_tensor(
                            out=turned[:, n % 2, a, :], in0=bank[2 * a + n % 2][:, :],
                            scalar=W["scales"][:, 2 * z + a:2 * z + a + 1],
                            in1=tables[:, 2 * z + a, j * TILE:(j + 1) * TILE], op0=ALU.mult, op1=ALU.mult)
                    last.then_inc(turned_done, 1)

                def bound(b, n):
                    dve.wait_ge(ss_mm, NU * b + n + 3)
                    dve.wait_ge(ln_done, NU * b + n + 1)
                    nc.vector.tensor_scalar(ss[:, n % 2, :], bank[4 + n % 2][:, :], TINY, None, ALU.max).then_inc(ss_done, 1)

                def scale(b, n):
                    dst = rotated(n)
                    dve.wait_ge(sum_done, NU * b + n + 3)
                    dve.wait_ge(rn_done, NU * b + n + 3)
                    if n == 0:
                        dve.wait_ge(s_done, HF * NI * b + HF)
                    nc.vector.tensor_tensor(dst, tsum[:, n % 4, :], rn[:, n % 2, :], ALU.mult).then_inc(qk_done[0], 1)

                def middle_values(b):
                    for t in range(NI):
                        dve.wait_ge(v_done, NI * b + t + 3)
                        nc.vector.tensor_copy(v_mid[WIN:P, t, :], v[0:WIN, t, :]).then_inc(mid_done, 1)
                        if t + 1 < NI:
                            nc.vector.tensor_copy(v_mid[0:WIN, t + 1, :], v[WIN:P, t, :]).then_inc(mid_done, 1)

                def evacuate(g):
                    dve.wait_ge(t_done, 2 * g + 4)
                    dve.wait_ge(av_done, 4 * g + 4)
                    nc.vector.tensor_copy(prT[:, 1, :], bank[3][:, :]).then_inc(ev_done[1], 1)

                def normalise(g, e, first):
                    for a in range(2):
                        n = 4 * g + 2 * e + a
                        dve.wait_ge(av_done, n + 5)
                        dve.wait_ge(on_done, n + 1)
                        o = bank[4 + a][:, 0:2 * VP].rearrange("q (r d) -> q r d", d=VP)
                        for z in range(2):
                            rows, d0 = slice(z * WIN, (z + 1) * WIN), z * (DF + 1)
                            nc.vector.reciprocal(rs[rows, 2 * a:2 * a + 2], o[rows, :, d0 + DF]).then_inc(rs_done, 1)
                        if not first:
                            dve.wait_ge(ot_done, g)
                        for z in range(2):
                            rows, d0 = slice(z * WIN, (z + 1) * WIN), z * (DF + 1)
                            dve.wait_ge(rs_done, 2 * n + z + 1)
                            last = nc.vector.tensor_tensor(
                                on[e * WIN:(e + 1) * WIN, 4 * a:4 * a + 4, :].rearrange("q (r z) d -> q r z d", z=2)[:, :, z, :],
                                o[rows, :, d0:d0 + DF], rs[rows, 2 * a:2 * a + 2].unsqueeze(2).to_broadcast([WIN, 2, DF]),
                                ALU.mult)
                        last.then_inc(on_done, 1)

                def body(b, g, i, where):
                    for e in range(2):
                        for s in range(4 * e, 4 * e + 4):
                            if s % 4 == 0:
                                dve.wait_ge(s_done, HF * g + 4 * e + 12)
                            dve.wait_ge(exp_done, HF * g + s + 1)
                            nc.vector.sem_inc(tick, 1)
                            nc.vector.tensor_tensor_reduce(ms[:, s % 4, :], bank[e][:, s % 4 * KW:(s % 4 + 1) * KW],
                                                           masks[:, 0 if where == 0 and e == 0 else 1, :], -1.0, 3e38,
                                                           ALU.add, ALU.min, nmx[:, s:s + 1]).then_inc(max_done, 1)
                        if where > 0:
                            if e == 0:
                                evacuate(g - 1)
                            normalise(g - 1, e, where == 1)
                    if where == 3:
                        evacuate(g)
                        normalise(g, 0, False)
                        normalise(g, 1, False)

                def split(b, j):
                    dve.wait_ge(v_mm, NI * b + 4 * j + 4)
                    nc.vector.sem_inc(tick, 1)
                    upper(nc.vector, sh_hi[:, j, :], sh[:, cols(2 * b + j)]).then_inc(hi_done, 1)
                    dve.wait_ge(hi_done, 2 * b + j + 1)
                    lower(nc.vector, sh_lo[:, j, :], sh[:, cols(2 * b + j)], sh_hi[:, j, :]).then_inc(parts_done, 1)

                with nc.vector.Fori(0, NB) as b:
                    split(b, 0)
                    split(b, 1)
                    rotate(b, 0)
                    for n in range(NU):
                        if n + 1 < NU:
                            rotate(b, n + 1)
                        bound(b, n)
                        if n % 2 == 0 and n > 0:
                            scale(b, n - 2)
                    scale(b, NU - 2)
                    middle_values(b)
                    tiles(nc.vector, b, body)
                    for j in range(2):
                        dve.wait_ge(wo_mm, 2 * b + j + 3)
                        nc.vector.tensor_tensor(y[:, cols(2 * b + j)], bank[7 - j][:, :], y[:, cols(2 * b + j)], ALU.add
                                                ).then_inc(y_done, 1)

            @block.gpsimd
            def _(pool):
                nc.gpsimd.sem_inc(sum_done, 2)
                nc.gpsimd.sem_inc(qk_done[1], 2)
                pool.wait_ge(init, 3)

                def scale(b, n):
                    dst = rotated(n)
                    pool.wait_ge(sum_done, NU * b + n + 3)
                    pool.wait_ge(rn_done, NU * b + n + 3)
                    if n == 1:
                        pool.wait_ge(s_done, HF * NI * b + HF)
                    nc.gpsimd.tensor_tensor(dst, tsum[:, n % 4, :], rn[:, n % 2, :], ALU.mult).then_inc(qk_done[1], 1)

                def mask_queries(g, i, a):
                    pool.wait_ge(s_done, HF * g + 4 * a + 4)
                    nc.gpsimd.sem_inc(tick, 1)
                    nc.gpsimd.tensor_tensor(
                        qm[:, 4 * a:4 * a + 4, :].rearrange("q r (z n) -> q r z n", z=2),
                        q[:, :, bass.ds(i * QT + a * WIN, WIN)].unsqueeze(2).to_broadcast([P, 4, 2, WIN]),
                        head_mask.unsqueeze(1).unsqueeze(3).to_broadcast([P, 4, 2, WIN]), ALU.mult).then_inc(qm_done, 1)

                def body(b, g, i, where):
                    if where < 3:
                        for a in range(2):
                            mask_queries(g + 1, i + 1, a)

                with nc.gpsimd.Fori(0, NB) as b:
                    for n in range(NU):
                        pool.wait_ge(turned_done, NU * b + n + 3)
                        pool.wait_ge(qk_done[n % 2], NU // 2 * b + n // 2 + 1)
                        nc.gpsimd.tensor_tensor(tsum[:, n % 4, :], turned[:, n % 2, 0, :], turned[:, n % 2, 1, :],
                                                ALU.add).then_inc(sum_done, 1)
                        if n % 2 == 1 and n > 2:
                            scale(b, n - 2)
                    scale(b, NU - 1)
                    for s in qk_done:
                        pool.wait_ge(s, NU // 2 * (b + 1) + 2)
                    for a in range(2):
                        mask_queries(8 * b, 0, a)
                    tiles(nc.gpsimd, b, body)


def feed_forward(nc, tag, W, y, sh, center, mean, eps_col):
    NT = T // TILE
    HW = (P, P, HR)
    with PhaseMemory(nc, tag) as m:
        sq = m.sb("sq", [P, 2, TILE])
        lnv = m.sb("lnv", [P, TILE])
        rstd = m.sb("rstd", [P, 2, TILE])
        xn = m.sb("xn", [P, TILE])
        fh = m.sb("fh", [P, 2, TILE])
        gg = m.sb("gg", [P, 2, TILE])
        hm = m.sb("hm", [P, 3, TILE])
        p_c = m.ps("p_c", [P, 2, 512])
        p_v = m.ps("p_v", [P, 512])
        p_u = m.ps("p_u", [P, 4, 512])
        p_d = m.ps("p_d", [P, 512])
        cen_mm = m.sem("cen_mm")
        sq_done = m.sem("sq_done")
        var_mm = m.sem("var_mm")
        ln_done = m.sem("ln_done")
        rstd_done = m.sem("rstd_done")
        xn_done = m.sem("xn_done")
        fh_done = m.sem("fh_done")
        up_mm = m.sem("up_mm")
        gelu_done = m.sem("gelu_done")
        hm_done = m.sem("hm_done")
        down_mm = m.sem("down_mm")
        y_done = m.sem("y_done")

        def steps(eng, step):
            with eng.Fori(0, NT // 2 - 2) as p:
                step(2 * p, 0, 3)
                step(2 * p + 1, 1, 3)
            for t in range(NT - 4, NT):
                step(t, t % 2, NT - 1 - t)

        with nc.Block() as block:
            @block.tensor
            def _(pe):
                def centre(t, j):
                    pe.wait_ge(xn_done, t + 1)
                    nc.tensor.matmul(p_c[:, j, :], center, sh[:, cols(t)], start=True, stop=True).then_inc(cen_mm, 1)

                def variance(t, j):
                    pe.wait_ge(sq_done, t + 3)
                    pe.wait_ge(ln_done, t + 1)
                    nc.tensor.matmul(p_v[:, :], mean, sq[:, j, :], start=True, stop=True).then_inc(var_mm, 1)

                def up(t, j, r):
                    n = (3 * j + r) % 2
                    pe.wait_ge(hm_done, 3 * t + r + 1)
                    for a in range(2):
                        last = nc.tensor.matmul(p_u[0:HW[r], 2 * n + a, :],
                                                W["w1"][:, a * HID + r * P:a * HID + r * P + HW[r]], fh[:, j, :],
                                                start=True, stop=True)
                    last.then_inc(up_mm, 1)

                def down(t, r):
                    pe.wait_ge(hm_done, 3 * t + r + 3)
                    if r == 0:
                        pe.wait_ge(y_done, t + 1)
                    nc.tensor.matmul(p_d[:, :], W["w2"][0:HW[r], r, :], hm[0:HW[r], r, :], start=r == 0,
                                     stop=r == 2).then_inc(down_mm, 1)

                def step(t, j, ahead):
                    pe.wait_ge(fh_done, t + 2)
                    up(t, j, 0)
                    up(t, j, 1)
                    down(t, 0)
                    up(t, j, 2)
                    down(t, 1)
                    if ahead >= 2:
                        variance(t + 2, j)
                    if ahead >= 3:
                        centre(t + 3, 1 - j)
                    down(t, 2)

                nc.tensor.sem_inc(var_mm, 2)
                nc.tensor.sem_inc(up_mm, 4)
                nc.tensor.sem_inc(down_mm, 3)
                centre(0, 0)
                centre(1, 1)
                variance(0, 0)
                variance(1, 1)
                centre(2, 0)
                steps(nc.tensor, step)

            @block.scalar
            def _(act):
                def square(t, j):
                    act.wait_ge(cen_mm, t + 1)
                    act.wait_ge(var_mm, t + 1)
                    nc.scalar.activation(sq[:, j, :], p_c[:, j, :], ACT.Square).then_inc(sq_done, 1)

                def inverse_deviation(t, j):
                    nc.scalar.preload_act_table_set(LN_EXP)
                    act.wait_ge(var_mm, t + 3)
                    act.wait_ge(rstd_done, t + 2)
                    nc.scalar.activation(lnv[:, :], p_v[:, :], ACT.Ln, bias=eps_col).then_inc(ln_done, 1)
                    act.wait_ge(ln_done, t + 2)
                    act.wait_ge(xn_done, t + 1)
                    nc.scalar.activation(rstd[:, j, :], lnv[:, :], ACT.Exp, scale=-0.5).then_inc(rstd_done, 1)

                def step(t, j, ahead):
                    for r in range(3):
                        n = (3 * j + r) % 2
                        act.wait_ge(up_mm, 3 * t + r + 5)
                        act.wait_ge(hm_done, 3 * t + r + 1)
                        nc.scalar.activation(gg[0:HW[r], n, :], p_u[0:HW[r], 2 * n + 1, :], ACT.Gelu,
                                             bias=W["b1"][0:HW[r], 3 + r:4 + r]).then_inc(gelu_done, 1)
                    if ahead >= 2:
                        inverse_deviation(t + 2, j)
                    if ahead >= 3:
                        square(t + 3, 1 - j)

                nc.scalar.sem_inc(sq_done, 2)
                nc.scalar.sem_inc(ln_done, 1)
                nc.scalar.sem_inc(rstd_done, 2)
                square(0, 0)
                square(1, 1)
                inverse_deviation(0, 0)
                inverse_deviation(1, 1)
                square(2, 0)
                steps(nc.scalar, step)

            @block.vector
            def _(dve):
                def normalise(t, j):
                    dve.wait_ge(rstd_done, t + 3)
                    dve.wait_ge(fh_done, t + 1)
                    nc.vector.tensor_tensor(xn[:, :], p_c[:, j, :], rstd[:, j, :], ALU.mult).then_inc(xn_done, 1)
                    dve.wait_ge(xn_done, t + 3)
                    dve.wait_ge(up_mm, 3 * t + 1)
                    nc.vector.tensor_scalar(fh[:, j, :], xn[:, :], W["ln"][:, 0:1], W["ln"][:, 1:2],
                                            ALU.mult, ALU.add).then_inc(fh_done, 1)

                def step(t, j, ahead):
                    for r in range(3):
                        n = (3 * j + r) % 2
                        dve.wait_ge(gelu_done, 3 * t + r + 1)
                        dve.wait_ge(down_mm, 3 * t + r + 1)
                        nc.vector.scalar_tensor_tensor(out=hm[0:HW[r], r, :], in0=p_u[0:HW[r], 2 * n, :],
                                                       scalar=W["b1"][0:HW[r], r:r + 1], in1=gg[0:HW[r], n, :],
                                                       op0=ALU.add, op1=ALU.mult).then_inc(hm_done, 1)
                    dve.wait_ge(down_mm, 3 * t + 6)
                    nc.vector.scalar_tensor_tensor(out=y[:, cols(t)], in0=p_d[:, :], scalar=W["ln"][:, 2:3],
                                                   in1=y[:, cols(t)], op0=ALU.add, op1=ALU.add).then_inc(y_done, 1)
                    if ahead >= 2:
                        normalise(t + 2, j)

                nc.vector.sem_inc(xn_done, 2)
                nc.vector.sem_inc(fh_done, 1)
                nc.vector.sem_inc(hm_done, 2)
                nc.vector.sem_inc(y_done, 1)
                normalise(0, 0)
                normalise(1, 1)
                steps(nc.vector, step)


def add_gated(nc, tag, x, y, mod_gate):
    with PhaseMemory(nc, tag) as m:
        done = m.sem("done")
        with nc.Block() as block:
            @block.vector
            def _(dve):
                with nc.vector.Fori(0, NB) as b:
                    xt = x[:, cols(b, L)]
                    nc.vector.scalar_tensor_tensor(out=xt, in0=y[:, cols(b, L)], scalar=mod_gate(b), in1=xt, op0=ALU.mult,
                                                   op1=ALU.add).then_inc(done, 1)


def wait_for(nc, loaded, n):
    with nc.Block() as block:
        @block.sync
        def _(sp):
            sp.wait_ge(loaded, n)


def load_weights(nc, mem, tag, vecs0, d):
    in_w = mem.sb("in_w", [P, 4 * P])
    xp_w = mem.sb("xp_w", [P, 2, 2 * NS + 2 * P])
    dt_w = mem.sb("dt_w", [NS, 2 * P])
    out_w = mem.sb("out_w", [P, 2, P])
    loaded = mem.sem("w_loaded")
    with nc.Block() as block:
        @block.sync
        def _(sp):
            sp.dma_start(in_w[:, :], d["in_w"]).then_inc(loaded, 16)
            sp.dma_start(xp_w[:, :, :], d["xp_w"]).then_inc(loaded, 16)
            sp.dma_start(dt_w[:, :], d["dt_w"]).then_inc(loaded, 16)
            sp.dma_start(out_w[:, :, :], d["out_w"]).then_inc(loaded, 16)
            sp.wait_ge(loaded, 64)
    return {
        "in_w": in_w, "xp_w": xp_w, "dt_w": dt_w, "out_w": out_w,
        "in_b": vecs0[:, 0:4], "conv_w": vecs0[:, 4:12].rearrange("q (c k) -> q c k", c=2), "conv_b": vecs0[:, 12:14],
        "dsB_b": vecs0[0:32, 14:15], "u_b": vecs0[:, 15:17], "dt_b": vecs0[:, 17:19], "D": vecs0[:, 19:21],
        "out_b": vecs0[:, 21:22],
    }


def build(nc, d, out, dbg=None, stop=99):
    with PhaseMemory(nc, "k_") as g:
        consts = g.sb("consts", [P, 3 * P])
        vecs0 = g.sb("vecs0", [P, 40])
        eps_col = g.sb("eps_col", [P, 1])
        one_col = g.sb("one_col", [P, 1])
        mod0 = g.sb("mod0", [P, 6, NB])
        mod1 = g.sb("mod1", [P, 6, NB])
        x = g.sb("x", [P, T])
        setup = g.sem("setup")
        setc = g.sem("setc")
        with nc.Block() as block:
            @block.sync
            def _(sp):
                sp.dma_start(consts[:, :], d["consts"]).then_inc(setup, 16)
                sp.dma_start(vecs0[:, 0:28], d["vecs0"]).then_inc(setup, 16)
                sp.dma_start(x[:, :], d["xT"]).then_inc(setup, 16)
                sp.wait_ge(setup, 48)

            @block.vector
            def _(dve):
                nc.vector.memset(eps_col[:, :], EPS).then_inc(setc, 1)
                nc.vector.memset(one_col[:, :], 1.0).then_inc(setc, 1)
        center, mean, ident = (consts[:, k * P:(k + 1) * P] for k in range(3))
        modulation(nc, g, d["c0T"], d["wmod0"], "m0_", mod0)
        modulation(nc, g, d["c1T"], d["wmod1"], "m1_", mod1)

        def dump(ap):
            s = g.sem("dump")
            with nc.Block() as block:
                @block.sync
                def _(sp):
                    sp.dma_start(dbg, ap).then_inc(s, 16)
                    sp.wait_ge(s, 16)

        with PhaseMemory(nc, "a_") as a:
            W = load_weights(nc, a, "wa_", vecs0, d)
            u = a.sb("u", [P, 2, T])
            delta = a.sb("delta", [P, 2, T])
            zs = a.sb("zs", [P, 2, T])
            B_dram = nc.dram_tensor("B_scratch", [NS, T], F32, kind="Internal").ap()
            with PhaseMemory(nc, "ah_") as ah:
                h = ah.sb("h", [P, T])
                layernorm(nc, "ln1_", x, h, center, mean, eps_col[:, :], mod0[:, 1, :], mod0[:, 0, :])
                if stop == 1:
                    return dump(h[:, :])
                mamba_inputs(nc, "mi_", W, h, u, delta, zs, B_dram)
            if stop == 2:
                return dump(u[:, :, :])
            mamba_scan(nc, "ms_", W, x, u, delta, zs, B_dram, ident, one_col[:, :], mod0)
        if stop == 5:
            return dump(x[:, :])

        with PhaseMemory(nc, "b_") as b:
            w1 = [b.sb(f"w1_{z}", [P, 8, 4 * P]) for z in ("hi", "lo")]
            w2 = [b.sb(f"w2_{z}", [P, 8, 4, P]) for z in ("hi", "lo")]
            gw = b.sb("gw", [P, 9 + 9 + 32])
            b2 = b.sb("b2", [8, P])
            h = b.sb("h", [P, T])
            w_dram = nc.dram_tensor("w_scratch", [PAIRS, 64, P], F32, kind="Internal").ap()
            moe_loaded = b.sem("moe_loaded")
            gate_loaded = b.sem("gate_loaded")
            with PhaseMemory(nc, "bw_") as bw:
                w1_full = bw.sb("w1_full", [P, 8, 4 * P])
                w2_full = bw.sb("w2_full", [P, 8, 4, P])
                with nc.Block() as block:
                    @block.sync
                    def _(sp):
                        sp.dma_start(gw[:, :], d["gate"]).then_inc(gate_loaded, 16)
                        sp.dma_start(w1_full[:, :, :], d["W1"]).then_inc(moe_loaded, 16)
                        sp.dma_start(w2_full[:, :, :, :], d["W2"]).then_inc(moe_loaded, 16)
                        sp.dma_start(b2[:, :], d["b2"]).then_inc(moe_loaded, 16)
                        sp.wait_ge(gate_loaded, 16)
                layernorm(nc, "ln2_", x, h, center, mean, eps_col[:, :], mod0[:, 4, :], mod0[:, 3, :])
                if stop == 6:
                    return dump(h[:, :])
                moe_gate(nc, "mg_", h, gw[:, 0:9], gw[:, 9:18], ident, w_dram,
                         [tuple(a[:, :, :].rearrange("q a b -> q (a b)") for a in (w1_full, *w1)),
                          tuple(a[:, :, :, :].rearrange("q a b c -> q (a b c)") for a in (w2_full, *w2))], moe_loaded, 48)
            if stop == 7:
                return dump(w_dram)
            moe(nc, "mo_", x, h, w1, gw[:, 18:50], w2, b2[:, :], w_dram, mod0)
        if stop == 8:
            return dump(x[:, :])

        with PhaseMemory(nc, "c_") as c:
            q = c.sb("q", [P, T + QT])
            k = c.sb("k", [P, T + 2 * QT])
            v = c.sb("v", [P, NQ + 1, VW])
            vg = c.sb("vg", [32, 2, NB, VW // 2])
            out_w = c.sb("out_w", [P, P])
            cc = c.sb("cc", [P, HB + 8 + NQ])
            masks = c.sb("masks", [P, NQ, 2 * QT])
            c_loaded = c.sem("c_loaded")
            masks_loaded = c.sem("masks_loaded")
            with PhaseMemory(nc, "ch_") as ch:
                h = ch.sb("h", [P, T])
                qkv_w = ch.sb("qkv_w", [P, 5 * P])
                rope = ch.sb("rope", [P, 4, L])
                with nc.Block() as block:
                    @block.sync
                    def _(sp):
                        for dst, name in ((qkv_w[:, :], "qkv_w"), (rope[:, :, :], "rope"), (vg[:, :, :, :], "vg"),
                                          (out_w[:, :], "out_w1"), (cc[:, :], "cc")):
                            sp.dma_start(dst, d[name]).then_inc(c_loaded, 16)
                        for b in range(NB):
                            sp.dma_start(masks[:, 8 * b:8 * b + 2, :], d["masks"][:, 0:2, :]).then_inc(masks_loaded, 16)
                            sp.dma_start(masks[:, 8 * b + 2:8 * b + 8, :],
                                         d["masks"][:, 2:3, :].to_broadcast([P, 6, 2 * QT])).then_inc(masks_loaded, 16)
                layernorm(nc, "ln3_", x, h, center, mean, eps_col[:, :], mod1[:, 1, :], mod1[:, 0, :])
                wait_for(nc, c_loaded, 80)
                rope_qkv(nc, "rq_", h, qkv_w, rope, q, k, v, vg, cc[0:32, HB:HB + 8])
            if stop == 9:
                return dump(q[:, 0:T])
            if stop == 10:
                return dump(k[:, QT:QT + T])
            oT = c.sb("oT", [P, T])
            wait_for(nc, masks_loaded, 2 * NB * 16)
            band_attention(nc, "ba_", q, k, v, vg, cc, masks, ident, oT)
            if stop == 11:
                return dump(oT[:, :])
            out_project(nc, "op_", x, oT, 0, out_w[:, :], lambda p: mod1[:, 2, bass.ds(p, 1)])
        if stop == 12:
            return dump(x[:, :])

        with PhaseMemory(nc, "d_") as dd:
            y = dd.sb("y", [P, T])
            sh = dd.sb("sh", [P, T])
            tables = dd.sb("tables", [P, 4, L])
            dc = dd.sb("dc", [P, P + 2])
            norm_bias = dd.sb("norm_bias", [P, 1])
            masks = dd.sb("masks", [P, 2, 2 * WIN])
            qk_w = [dd.sb(f"qk_w_{z}", [P, 4, 4 * P]) for z in ("hi", "lo")]
            v_w = [dd.sb(f"v_w_{z}", [P, 4 * P]) for z in ("hi", "lo")]
            wo_w = dd.sb("wo_w", [P, 4, P])
            w1_w = dd.sb("w1_w", [P, 2 * HID])
            w2_w = dd.sb("w2_w", [P, 3, P])
            dv = dd.sb("dv", [P, 13])
            W = {"qk": qk_w, "v": [w[:, :] for w in v_w], "wo": wo_w, "w1": w1_w, "w2": w2_w, "scales": dv[:, 0:4], "b1": dv[:, 4:10],
                 "ln": dv[:, 10:13]}

            flat = "q a b -> q (a b)"
            loaded = [dd.sem(f"layer{n}") for n in range(2)]

            def load_layer(n, qk_full, v_full):
                with nc.Block() as block:
                    @block.sync
                    def _(sp):
                        for dst, name in ((qk_full[:, :, :], "f_qk"), (v_full[:, :], "f_v"), (wo_w[:, :, :], "f_wo"),
                                          (w1_w[:, :], "f_w1"), (w2_w[:, :, :], "f_w2"), (dv[:, :], "f_dv")):
                            sp.dma_start(dst, d[f"{name}{n}"]).then_inc(loaded[n], 16)
                        if n == 0:
                            for dst, name in ((tables[:, :, :], "f_tables"), (dc[:, :], "f_dc"), (masks[:, :, :], "f_masks")):
                                sp.dma_start(dst, d[name]).then_inc(loaded[n], 16)

                    if n == 0:
                        @block.vector
                        def _(dve):
                            nc.vector.memset(norm_bias[:, :], 0.5 * float(np.log(LN_SCALE))).then_inc(setc, 1)

            def split_layer(n, qk_full, v_full):
                split_parts(nc, f"wp{n}_", [[a[:, :, :].rearrange(flat) for a in (qk_full, *qk_w)],
                                            [a[:, :] for a in (v_full, *v_w)]], loaded[n], 96 if n else 144)

            def full_weights(n):
                dw = PhaseMemory(nc, f"dw{n}_")
                return dw, dw.sb("qk_full", [P, 4, 4 * P]), dw.sb("v_full", [P, 4 * P])

            scope, *full = full_weights(0)
            with scope:
                load_layer(0, *full)
                layernorm(nc, "ln4_", x, y, center, mean, eps_col[:, :], mod1[:, 4, :], mod1[:, 3, :])
                split_layer(0, *full)
            if stop == 13:
                return dump(y[:, :])
            for n in range(2):
                if n:
                    scope, *full = full_weights(n)
                    with scope:
                        load_layer(n, *full)
                        split_layer(n, *full)
                shifted_copy(nc, f"sa{n}_", y, sh)
                local_attention(nc, f"at{n}_", W, y, sh, tables, dc[:, 0:P], ident, dc[:, P:P + 2], masks, norm_bias[:, :])
                shifted_copy(nc, f"sf{n}_", y, sh)
                feed_forward(nc, f"ff{n}_", W, y, sh, center, mean, eps_col[:, :])
                if stop == 14 + n:
                    return dump(y[:, :])
            add_gated(nc, "ag_", x, y, lambda b: mod1[:, 5, bass.ds(b, 1)])
        written = g.sem("written")
        with nc.Block() as block:
            @block.sync
            def _(sp):
                sp.dma_start(out, x[:, :]).then_inc(written, 16)
                sp.wait_ge(written, 16)


_V0 = 28


def layout(i):
    f = np.float32
    c = np.ascontiguousarray
    eye = np.eye(P, dtype=f)
    mean = np.full((P, P), 1.0 / P, f)

    def col(v):
        return c(v.reshape(-1, P).T)

    dsB_b = np.zeros((P, 1), f)
    dsB_b[0:32, 0] = i["L0_attn_x_proj_b"][0:32]
    vecs0 = np.concatenate([
        col(i["L0_attn_in_proj_b"]),
        i["L0_attn_conv_w"].reshape(2, P, 4).transpose(1, 0, 2).reshape(P, 8),
        col(i["L0_attn_conv_b"]),
        dsB_b,
        col(i["L0_attn_x_proj_b"][32:]),
        col(i["L0_attn_dt_proj_b"]),
        col(i["L0_attn_D"]),
        col(i["L0_attn_out_proj_b"]),
        np.zeros((P, 6), f),
    ], 1)
    w = i["L1_attn_qkv_w"].reshape(3, P, P)
    swap = np.arange(P) ^ 1
    qkv_w = np.concatenate([w[0], w[0][swap], w[1], w[1][swap], w[2]], 0).T
    inv_freq = f(1) / (10000.0 ** (np.arange(0, DH, 2) / DH)).astype(f)
    ang = np.outer(np.arange(L, dtype=f), inv_freq).astype(f)
    ang = np.concatenate([ang, ang], -1).T
    sign = np.where(np.arange(DH) % 2 == 0, -1.0, 1.0).astype(f)[:, None]
    cos, sin = np.tile(np.cos(ang), (HB, 1)).astype(f), np.tile(np.sin(ang) * sign, (HB, 1)).astype(f)
    r = f(DH ** -0.5)
    rope = np.stack([cos * r, sin * r, cos, sin], 1)
    vg = np.zeros((32, 2, NB, HB // 2, DH + 1), f)
    cc = np.zeros((P, HB + 8 + NQ), f)
    for hd in range(HB):
        cc[hd * DH:(hd + 1) * DH, hd] = 1
        for j in range(NG4):
            vg[(hd % 8) * NG4 + j, hd // 8, :, hd % 8, DH] = 1
            cc[(hd % 8) * NG4 + j, HB + hd % 8] = 1
    ii, jj = np.arange(QT)[:, None], np.arange(QT)[None, :]
    masks = np.full((P, 3, 2 * QT), MASKED, f)
    masks[:, :, QT:2 * QT][np.broadcast_to((jj <= ii)[:, None], (P, 3, QT))] = 0
    masks[:, 1, 0:QT][(jj >= ii) | (jj < NG4)] = 0
    masks[:, 2, 0:QT][jj >= ii] = 0
    cc[:, HB + 8:].reshape(P, NB, 8)[:, :, 0:2] = MASKED
    half = np.arange(0, DF, 2, dtype=f)
    inv_freq = f(1) / (10000.0 ** (np.arange(0, DF, 2) / DF)).astype(f)
    tok = np.arange(L, dtype=f)
    fr = (tok[:, None] * inv_freq[None, :]).astype(f)
    fr = np.concatenate([fr, fr], -1)
    base = ((half + f(0.4 * DF)) / f(1.4 * DF)).astype(f)
    scale = (base[None, :] ** ((tok - L // 2) / f(WIN // 2))[:, None]).astype(f)
    scale = np.concatenate([scale, scale], -1)
    sg = np.where(np.arange(DF) < DF // 2, f(-1), f(1))
    cs, sn = np.cos(fr), np.sin(fr) * sg
    tables = np.stack([np.tile(a.T, (2, 1)) for a in (cs * scale * f(8), sn * scale * f(8), cs / scale, sn / scale)], 1)
    f_dc = np.zeros((P, P + 2), f)
    f_dc[0:DF, 0:DF] = f_dc[DF:, DF:P] = 1
    f_dc[0:DF, P] = f_dc[DF:, P + 1] = 1
    ii, jj = np.arange(P)[:, None] % WIN, np.arange(2 * WIN)[None, :] - WIN
    f_masks = np.full((P, 2, 2 * WIN), MASKED, f)
    f_masks[:, 1][(jj <= ii) & (ii - jj <= WIN)] = 0
    f_masks[:, 0][(jj <= ii) & (ii - jj <= WIN) & (jj >= 0)] = 0
    layers = {}
    turn = (np.arange(4 * P) ^ (DF // 2))
    for n in range(2):
        wqkv = i["L1_ffn_wqkv"][n]
        wq, wk, wv = wqkv[:, 0:512], wqkv[:, 512:1024], wqkv[:, 1024:]
        qs, ks = np.tile(i["L1_ffn_q_scale"][n], 2)[:, None], np.tile(i["L1_ffn_k_scale"][n], 2)[:, None]
        tn = np.arange(P) ^ (DF // 2)
        b1 = np.zeros((P, 6), f)
        for r in range(3):
            m = min(P, HID - r * P)
            b1[0:m, r] = i["L1_ffn_b1"][n][r * P:r * P + m]
            b1[0:m, 3 + r] = i["L1_ffn_b1"][n][HID + r * P:HID + r * P + m]
        w2 = np.zeros((3 * P, P), f)
        w2[0:HID] = i["L1_ffn_w2"][n]
        layers |= {
            f"f_qk{n}": c(np.stack([wq, wq[:, turn], wk, wk[:, turn]], 1)),
            f"f_v{n}": c(wv),
            f"f_wo{n}": c(i["L1_ffn_wo"][n].reshape(4, P, P).transpose(1, 0, 2)),
            f"f_w1{n}": c(i["L1_ffn_w1"][n]),
            f"f_w2{n}": c(w2.reshape(3, P, P).transpose(1, 0, 2)),
            f"f_dv{n}": c(np.concatenate([qs, qs[tn], ks, ks[tn], b1, i["L1_ffn_ln_g"][n][:, None],
                                          i["L1_ffn_ln_b"][n][:, None], i["L1_ffn_b2"][n][:, None]], 1)),
        }
    return layers | {
        "f_tables": c(tables.astype(f)),
        "f_dc": f_dc,
        "f_masks": f_masks,
        "qkv_w": c(qkv_w),
        "rope": c(rope),
        "vg": c(vg.reshape(32, 2, NB, VW // 2)),
        "cc": cc,
        "masks": masks,
        "out_w1": c(i["L1_attn_out_w"].T),
        "xT": c(i["L0_attn_x"].reshape(T, P).T),
        "consts": c(np.concatenate([eye - mean, mean, eye], 1)),
        "vecs0": c(vecs0),
        "c0T": c(i["L0_c"].T),
        "c1T": c(i["L1_c"].T),
        "in_w": c(i["L0_attn_in_proj_w"]),
        "xp_w": c(i["L0_attn_x_proj_w"].reshape(2, P, -1).transpose(1, 0, 2)),
        "dt_w": c(i["L0_attn_dt_proj_w"]),
        "out_w": c(i["L0_attn_out_proj_w"].reshape(2, P, P).transpose(1, 0, 2)),
        "gate": c(np.concatenate([
            i["L0_ffn_Wg"], i["L0_ffn_Wt"], np.broadcast_to(i["L0_ffn_bg"], (P, 8)), np.broadcast_to(i["L0_ffn_bt"], (P, 1)),
            i["L0_ffn_b1"].reshape(8, 4, P).transpose(2, 0, 1).reshape(P, 32)], 1)),
        "W1": c(i["L0_ffn_W1"].transpose(1, 0, 2)),
        "W2": c(i["L0_ffn_W2"].reshape(8, 4, P, P).transpose(2, 0, 1, 3)),
        "b2": c(i["L0_ffn_b2"]),
        "wmod0": c(i["L0_wmod"]),
        "wmod1": c(i["L1_wmod"]),
    }


STOP = 99
DBG = None


def kernel(**inputs):
    import concourse.bacc as bacc
    from concourse.bass_utils import run_bass_kernel_spmd as run

    arrays = layout({k: np.asarray(v) for k, v in inputs.items()})
    nc = bacc.Bacc("TRN2", target_bir_lowering=False, num_devices=1)
    d = {k: nc.dram_tensor(f"in_{k}", list(v.shape), F32, kind="ExternalInput").ap() for k, v in arrays.items()}
    out = nc.dram_tensor("out", [P, T], F32, kind="ExternalOutput").ap()
    dbg = nc.dram_tensor("dbg", DBG, F32, kind="ExternalOutput").ap() if DBG else None
    build(nc, d, out, dbg, STOP)
    r = run(nc, [{f"in_{k}": v for k, v in arrays.items()}], core_ids=[0])
    got = r.results[0]["out"]
    return np.ascontiguousarray(got.T).reshape(NB, L, P)
```
